# Optimizing a Trainium2 kernel written in Bass

```python
import numpy as np
import jax
import jax.numpy as jnp

def _softmax(x, axis=-1):
    return jax.nn.softmax(x, axis=axis)

def _gelu(x):
    return jax.nn.gelu(x, approximate=True)

def _silu(x):
    return jax.nn.silu(x)

def _sigmoid(x):
    return jax.nn.sigmoid(x)

def _layernorm(x, axis=-1, eps=1e-05):
    m = jnp.mean(x, axis=axis, keepdims=True)
    v = jnp.var(x, axis=axis, keepdims=True)
    return (x - m) / jnp.sqrt(v + eps)

def _scatter_add(tgt, idx, src, axis=0):
    return tgt.at[idx].add(src)

def _segment_sum(src, seg, n):
    return jax.ops.segment_sum(src, seg, n)
kernel_name = 'mk_decoder_postln_d1_seqx_r4_5c9d6a'

def setup_inputs(seed: int=0):
    np.random.seed(seed)
    _w = jnp.asarray

    def _rec_inputs():
        import jax
        import jax.numpy as jnp
        _rk = jax.random.key(seed)
        x = -0.0002928 + 1 * jax.random.normal(jax.random.fold_in(_rk, 1), (16, 256, 256), jnp.float32)
        _lenS = 256 - jax.random.randint(jax.random.fold_in(_rk, 7), (16,), 0, max(1, 256 // 4) + 1, jnp.int32)
        _lenS2 = 77 - jax.random.randint(jax.random.fold_in(_rk, 8), (16,), 0, max(1, 77 // 4) + 1, jnp.int32)
        _ctx_1024P = jax.random.normal(jax.random.fold_in(_rk, 11), (16, 16, 256), jnp.float32)
        _ctx_1024c = jax.random.dirichlet(jax.random.fold_in(_rk, 511), 0.3 * jnp.ones((16,), jnp.float32), (16, 77))
        _ctx_1024t = jnp.einsum('bsk,bkd->bsd', _ctx_1024c, _ctx_1024P)
        _ctx_1024t = _ctx_1024t * jax.lax.rsqrt(jnp.mean(jnp.square(_ctx_1024t)) + 1e-12) * 0.953939
        ctx_1024 = -1.39393e-06 + 0.999914 * (_ctx_1024t + 0.3 * jax.random.normal(jax.random.fold_in(_rk, 611), (16, 77, 256), jnp.float32))
        return (x, ctx_1024)
    x, ctx_1024 = _rec_inputs()

    def _L0_attn_setup():
        import jax, jax.numpy as jnp
        import numpy as np
        import math
        NUM_HEADS = 16
        SEGMENT_SIZE = 128
        DILATION = 2

        def hilbert_map(seq_len: int) -> np.ndarray:
            if seq_len <= 64:
                return np.arange(seq_len, dtype=np.int64)
            g = int(math.ceil(math.sqrt(seq_len)))
            fm = np.zeros(seq_len, dtype=np.int64)
            idx = 0
            for row in range(g):
                cols = range(g) if row % 2 == 0 else range(g - 1, -1, -1)
                for col in cols:
                    lp = row * g + col
                    if lp < seq_len and idx < seq_len:
                        fm[lp] = idx
                        idx += 1
            return fm
        key = jax.random.key(seed)
        k1, k2, k3 = jax.random.split(key, 3)
        B, S, D = (2, 2048, 256)
        x = jax.random.normal(k1, (B, S, D), dtype=jnp.float32)
        W_qkv = jax.random.normal(k2, (D, 3 * D), dtype=jnp.float32) * 0.02
        W_out = jax.random.normal(k3, (D, D), dtype=jnp.float32) * 0.02
        return {'x': x, 'W_qkv': W_qkv, 'W_out': W_out}
    _L0_attn_all = _L0_attn_setup()
    _L0_attn_in = {k: v for k, v in _L0_attn_all.items() if k in ('W_qkv', 'W_out')}
    del _L0_attn_all

    def _L0_xattn_setup():
        import jax, jax.numpy as jnp
        import numpy as np
        H = 16
        D_MODEL = 256
        D_K = D_MODEL // H
        key = jax.random.key(seed)
        ks = jax.random.split(key, 11)
        B, S = (2, 512)
        scale = 1.0 / np.sqrt(D_MODEL)
        inp = {'query': jax.random.normal(ks[0], (B, S, D_MODEL), dtype=jnp.float32), 'key': jax.random.normal(ks[1], (B, S, D_MODEL), dtype=jnp.float32), 'value': jax.random.normal(ks[2], (B, S, D_MODEL), dtype=jnp.float32), 'Wq': jax.random.normal(ks[3], (D_MODEL, D_MODEL), dtype=jnp.float32) * scale, 'bq': jnp.zeros((D_MODEL,), dtype=jnp.float32), 'Wk': jax.random.normal(ks[4], (D_MODEL, D_MODEL), dtype=jnp.float32) * scale, 'bk': jnp.zeros((D_MODEL,), dtype=jnp.float32), 'Wv': jax.random.normal(ks[5], (D_MODEL, D_MODEL), dtype=jnp.float32) * scale, 'bv': jnp.zeros((D_MODEL,), dtype=jnp.float32), 'Wo': jax.random.normal(ks[6], (D_MODEL, D_MODEL), dtype=jnp.float32) * scale, 'bo': jnp.zeros((D_MODEL,), dtype=jnp.float32)}
        return inp
    _L0_xattn_all = _L0_xattn_setup()
    _L0_xattn_in = {k: v for k, v in _L0_xattn_all.items() if k in ('Wq', 'bq', 'Wk', 'bk', 'Wv', 'bv', 'Wo', 'bo')}
    del _L0_xattn_all

    def _L0_ffn_setup():
        import jax, jax.numpy as jnp
        import numpy as np
        B, S, D, E, F = (2, 512, 256, 14, 512)
        key = jax.random.key(seed)
        k = jax.random.split(key, 4)
        h = jax.random.normal(k[0], (B, S, D), dtype=jnp.float32)
        router_w = jax.random.normal(k[1], (D, E), dtype=jnp.float32) * 0.02
        w1 = jax.random.uniform(k[2], (E, D, F), dtype=jnp.float32, minval=-1.0, maxval=1.0) * float(np.sqrt(6.0 / D))
        w2 = jax.random.uniform(k[3], (E, F, D), dtype=jnp.float32, minval=-1.0, maxval=1.0) * float(np.sqrt(6.0 / F))
        b1 = jnp.zeros((E, F), dtype=jnp.float32)
        b2 = jnp.zeros((E, D), dtype=jnp.float32)
        return {'h': h, 'router_w': router_w, 'w1': w1, 'b1': b1, 'w2': w2, 'b2': b2}
    _L0_ffn_all = _L0_ffn_setup()
    _L0_ffn_in = {k: v for k, v in _L0_ffn_all.items() if k in ('router_w', 'w1', 'b1', 'w2', 'b2')}
    del _L0_ffn_all
    return {'x': x, 'ctx_1024': ctx_1024, 'L0_attn_W_qkv': _L0_attn_in['W_qkv'], 'L0_attn_W_out': _L0_attn_in['W_out'], 'L0_xattn_Wq': _L0_xattn_in['Wq'], 'L0_xattn_bq': _L0_xattn_in['bq'], 'L0_xattn_Wk': _L0_xattn_in['Wk'], 'L0_xattn_bk': _L0_xattn_in['bk'], 'L0_xattn_Wv': _L0_xattn_in['Wv'], 'L0_xattn_bv': _L0_xattn_in['bv'], 'L0_xattn_Wo': _L0_xattn_in['Wo'], 'L0_xattn_bo': _L0_xattn_in['bo'], 'L0_ffn_router_w': _L0_ffn_in['router_w'], 'L0_ffn_w1': _L0_ffn_in['w1'], 'L0_ffn_b1': _L0_ffn_in['b1'], 'L0_ffn_w2': _L0_ffn_in['w2'], 'L0_ffn_b2': _L0_ffn_in['b2']}

def reference(x, ctx_1024, L0_attn_W_qkv, L0_attn_W_out, L0_xattn_Wq, L0_xattn_bq, L0_xattn_Wk, L0_xattn_bk, L0_xattn_Wv, L0_xattn_bv, L0_xattn_Wo, L0_xattn_bo, L0_ffn_router_w, L0_ffn_w1, L0_ffn_b1, L0_ffn_w2, L0_ffn_b2):
    import jax
    import jax.numpy as jnp

    def _L0_attn_ref(x, W_qkv, W_out):
        import jax, jax.numpy as jnp
        import numpy as np
        import math
        NUM_HEADS = 16
        SEGMENT_SIZE = 128
        DILATION = 2

        def hilbert_map(seq_len: int) -> np.ndarray:
            if seq_len <= 64:
                return np.arange(seq_len, dtype=np.int64)
            g = int(math.ceil(math.sqrt(seq_len)))
            fm = np.zeros(seq_len, dtype=np.int64)
            idx = 0
            for row in range(g):
                cols = range(g) if row % 2 == 0 else range(g - 1, -1, -1)
                for col in cols:
                    lp = row * g + col
                    if lp < seq_len and idx < seq_len:
                        fm[lp] = idx
                        idx += 1
            return fm
        B, S, Dm = x.shape
        H, Dh = (NUM_HEADS, Dm // NUM_HEADS)
        seg, dil = (SEGMENT_SIZE, DILATION)
        scale = Dh ** (-0.5)
        qkv = (x @ W_qkv).reshape(B, S, 3, H, Dh)
        q = jnp.transpose(qkv[:, :, 0], (0, 2, 1, 3))
        k = jnp.transpose(qkv[:, :, 1], (0, 2, 1, 3))
        v = jnp.transpose(qkv[:, :, 2], (0, 2, 1, 3))
        m = jnp.asarray(hilbert_map(S))
        q, k, v = (q[:, :, m], k[:, :, m], v[:, :, m])
        nseg = S // seg
        qs = q.reshape(B, H, nseg, seg, Dh)
        ks = k.reshape(B, H, nseg, seg, Dh)[:, :, :, ::dil]
        vs = v.reshape(B, H, nseg, seg, Dh)[:, :, :, ::dil]
        scores = jnp.einsum('bhnqd,bhnkd->bhnqk', qs, ks) * scale
        attn = jax.nn.softmax(scores, axis=-1)
        out = jnp.einsum('bhnqk,bhnkd->bhnqd', attn, vs).reshape(B, H, S, Dh)
        inv = jnp.argsort(m)
        out = out[:, :, inv]
        out = jnp.transpose(out, (0, 2, 1, 3)).reshape(B, S, Dm)
        return out @ W_out

    def _L0_xattn_ref(query, key, value, Wq, bq, Wk, bk, Wv, bv, Wo, bo):
        import jax, jax.numpy as jnp
        import numpy as np
        H = 16
        D_MODEL = 256
        D_K = D_MODEL // H
        B, S, _ = query.shape

        def proj(x, W, b):
            y = jnp.einsum('bsd,ed->bse', x, W) + b
            return y.reshape(B, -1, H, D_K).transpose(0, 2, 1, 3)
        q = proj(query, Wq, bq)
        k = proj(key, Wk, bk)
        v = proj(value, Wv, bv)
        scores = jnp.einsum('bhqd,bhkd->bhqk', q, k) / jnp.sqrt(jnp.float32(D_K))
        p = jax.nn.softmax(scores, axis=-1)
        ctx = jnp.einsum('bhqk,bhkd->bhqd', p, v)
        ctx = ctx.transpose(0, 2, 1, 3).reshape(B, S, H * D_K)
        out = jnp.einsum('bsd,ed->bse', ctx, Wo) + bo
        return out

    def _L0_ffn_ref(h, router_w, w1, b1, w2, b2):
        import jax, jax.numpy as jnp
        import numpy as np
        B, S, D, E, F = (2, 512, 256, 14, 512)
        Bb, Ss, Dd = h.shape
        x = h.reshape(-1, Dd)
        logits = x @ router_w
        assignments = jnp.argmax(logits, axis=-1)
        probs = jax.nn.softmax(logits, axis=-1)
        weights = jnp.take_along_axis(probs, assignments[:, None], axis=1)[:, 0]
        hid = jnp.einsum('nd,edf->nef', x, w1) + b1
        hid = jax.nn.gelu(hid, approximate=False)
        all_out = jnp.einsum('nef,efd->ned', hid, w2) + b2
        sel = jnp.take_along_axis(all_out, assignments[:, None, None], axis=1)[:, 0, :]
        moe_out = (sel * weights[:, None]).reshape(Bb, Ss, Dd)
        return moe_out
    x = _layernorm(x + _L0_attn_ref(x, L0_attn_W_qkv, L0_attn_W_out), axis=-1)
    x = _layernorm(x + _L0_xattn_ref(x, ctx_1024, ctx_1024, L0_xattn_Wq, L0_xattn_bq, L0_xattn_Wk, L0_xattn_bk, L0_xattn_Wv, L0_xattn_bv, L0_xattn_Wo, L0_xattn_bo), axis=-1)
    x = _layernorm(x + _L0_ffn_ref(x, L0_ffn_router_w, L0_ffn_w1, L0_ffn_b1, L0_ffn_w2, L0_ffn_b2), axis=-1)
    return x

_drawn_inputs = setup_inputs


def setup_inputs(seed=0):
    import zlib

    import numpy as np

    out = dict(_drawn_inputs(seed))
    spreads = {'L0_xattn_bq': (0.0, 0.1),
     'L0_xattn_bk': (0.0, 0.8),
     'L0_xattn_bv': (0.0, 0.1),
     'L0_xattn_bo': (0.0, 0.1),
     'L0_ffn_b1': (0.0, 0.668),
     'L0_ffn_b2': (0.0, 0.665)}
    factors = {'L0_attn_W_qkv': 2.84, 'L0_attn_W_out': 2.678}
    for name, (base, spread) in spreads.items():
        noise = np.random.default_rng([zlib.crc32(name.encode()), seed]).standard_normal(out[name].shape)
        drawn = base * np.exp(spread * noise) if base else spread * noise
        out[name] = jnp.asarray(drawn.astype(out[name].dtype))
    for name, factor in factors.items():
        out[name] = (out[name] * factor).astype(out[name].dtype)
    return out
```

```python
from contextlib import ExitStack

import concourse.bass as bass
import numpy as np
from concourse import mybir

P = 128
F32 = mybir.dt.float32
U32 = mybir.dt.uint32
I32 = mybir.dt.int32
ALU = mybir.AluOpType
ACT = mybir.ActivationFunctionType
AX = mybir.AxisListType.X
EPS = 1e-5


class Signal:

    def __init__(self, sem, per, unit=1):
        self.sem, self.per, self.unit = sem, per, unit

    def at(self, b, k=None):
        k = self.per - 1 if k is None else k
        return (b * self.per + (k + 1)) * self.unit


def wait(eng, sig, b, k=None):
    if isinstance(b, int) and b < 0:
        return
    eng.wait_ge(sig.sem, sig.at(b, k))


def decoder_layer(nc, x, ctx_in, w_qkv, w_out, wq, bq, wk, bk, wv, bv, wo, bo, router_w, w1, b1, w2, b2, out):
    B, S, D = x.shape
    K2 = ctx_in.shape[1]
    E, _, F = w1.shape
    H = 16
    DH = D // H
    SEG = 128
    NSEG = S // SEG
    KEYS = SEG // 2
    KC = D // P
    FC = F // P
    HH = H // KC
    NT = B * S // P
    TPB = S // P
    NTILE = NT + E - 1
    SCALE = float(DH) ** -0.5
    CH = -(-HH * K2 // P)
    LASTROWS = HH * K2 - (CH - 1) * P
    G0 = [min(c * P // (2 * K2), HH // 2 - 2) for c in range(CH)]
    assert (KC, NSEG, TPB, HH, DH, SEG // 2 * HH) == (2, 2, 2, 8, 16, 512) and 4 * K2 <= 512
    for g in range(HH // 2):
        lo, hi = 2 * g * K2 // P, (2 * (g + 1) * K2 - 1) // P
        assert hi == lo + 1 and all(0 <= g - G0[c] <= 1 for c in (lo, hi))

    with ExitStack() as top:
        def alloc(stack, name, shape, dt=F32):
            return stack.enter_context(nc.sbuf_tensor(name, shape, dt))

        def psum(name, shape):
            return top.enter_context(nc.psum_tensor(name, shape, F32))

        def signal(name, per, unit=1):
            return Signal(top.enter_context(nc.semaphore(name)), per, unit)

        ps_s = psum("ps_s", [P, 2, 512])
        ps_t = psum("ps_t", [P, 2, 512])
        ps_m = psum("ps_m", [P, 2, 512])
        ps_or = psum("ps_or", [P, 2, 512])
        ps_o, ps_r = ps_or[:, 0, :], ps_or[:, 1, :]

        w1s = alloc(top, "w1s", [P, E, KC, F])
        w2s = alloc(top, "w2s", [P, E, FC, D])
        logits = alloc(top, "logits", [P, NT, E])
        ident = alloc(top, "ident", [P, P])
        ones = alloc(top, "ones", [P, P])
        b1t = alloc(top, "b1t", [P, E * FC])
        eps = alloc(top, "eps", [P, 1])
        neg_half = alloc(top, "neg_half", [P, 1])

        with ExitStack() as part1:
            def sb1(name, shape, dt=F32):
                return alloc(part1, name, shape, dt)

            wqkv_s = sb1("wqkv_s", [P, KC, 3 * D])
            wout_s = sb1("wout_s", [P, KC, D])
            wT = sb1("wT", [P, 4, KC, D])
            router_s = sb1("router_s", [P, KC, E])
            bq_s = sb1("bq_s", [P, KC])
            bk_s = sb1("bk_s", [P, KC])
            bv_s = sb1("bv_s", [P, KC])
            bo_s = sb1("bo_s", [P, D])
            kmask = sb1("kmask", [P, HH])
            vmask = sb1("vmask", [P, CH, 64])
            xs = sb1("xs", [P, TPB, D])
            xres = sb1("xres", [P, TPB, D])
            xT = sb1("xT", [P, KC, S])
            xkT = sb1("xkT", [P, KC, NSEG, 2, KEYS])
            qT = sb1("qT", [P, KC, S])
            kT = sb1("kT", [P, KC, NSEG, KEYS])
            kblk = sb1("kblk", [P, KC, NSEG, HH, KEYS])
            vA = sb1("vA", [P, NSEG, D])
            prob = sb1("prob", [P, 2, 1024])
            probT = sb1("probT", [P, 2, 1024])
            mx = sb1("mx", [P, 2, H])
            den = sb1("den", [P, 2, H])
            rden = sb1("rden", [P, 2, H])
            rden_s = sb1("rden_s", [P, 2, H, DH])
            r_s = sb1("r_s", [P, 2 * P])
            oTa = sb1("oTa", [P, KC, S])
            oTx = sb1("oTx", [P, KC, S])
            sum1 = sb1("sum1", [P, D])
            sum2 = sb1("sum2", [P, D])
            sum1b = sb1("sum1b", [P, D])
            sum2b = sb1("sum2b", [P, D])
            st = sb1("st", [P, 4, 6])
            mv = sb1("mv", [P, 4, 2])
            ve = sb1("ve", [P, 4])
            rstd = sb1("rstd", [P, 4])
            x1 = sb1("x1", [P, TPB, D])
            x1r = sb1("x1r", [P, TPB, D])
            x1T = sb1("x1T", [P, KC, S])
            qxT = sb1("qxT", [P, KC, S])
            ctx_s = sb1("ctx_s", [P, D])
            ctxT3 = sb1("ctxT3", [P, KC, 3, K2])
            kxT = sb1("kxT", [P, KC, K2])
            kxblk = sb1("kxblk", [P, KC, HH, K2])
            vX = sb1("vX", [P, CH, KC, 64])
            x2s = sb1("x2s", [P, TPB, D])
            x2T = sb1("x2T", [P, KC, S])
        w_raw = [prob, probT]

        NG = NT * E
        XR = 4
        with ExitStack() as part2:
            def sb2(name, shape, dt=F32):
                return alloc(part2, name, shape, dt)

            lmax = sb2("lmax", [P, NT])
            lexp = sb2("lexp", [P, NT, E])
            gate = sb2("gate", [P, NT])
            onehot = sb2("onehot", [P, NT, E])
            tmp_a = sb2("tmp_a", [P, NT, E])
            rev = sb2("rev", [P, E])
            best = sb2("best", [P, NT])
            tri = sb2("tri", [P, P])
            cnt = sb2("cnt", [P, E, NT])
            scan = sb2("scan", [P, E, NT])
            steps = sb2("steps", [P, NT])
            cmp = sb2("cmp", [P, E, NT])
            zeros = sb2("zeros", [P, E, NT])
            n_e = sb2("n_e", [P, E])
            t_e = sb2("t_e", [P, E])
            tb_e = sb2("tb_e", [P, E])
            base_e = sb2("base_e", [P, E])
            slot = sb2("slot", [P, NT])
            slot_i = sb2("slot_i", [P, NT], I32)
            row_i = sb2("row_i", [P, NT], I32)
            tile_i = sb2("tile_i", [P, NT], I32)
            row_f = sb2("row_f", [P, NT])
            tile_f = sb2("tile_f", [P, NT])
            iota_r = sb2("iota_r", [P, P])
            iota_t = sb2("iota_t", [P, NTILE])
            token = sb2("token", [P, NT])
            hot_r = sb2("hot_r", [P, 4, P])
            entry = sb2("entry", [P, NT, 3, NTILE])
            table = sb2("table", [P, 3, NTILE])
            e_cmp = sb2("e_cmp", [P, NTILE, E])
            e_f = sb2("e_f", [P, NTILE])
            e_i = sb2("e_i", [P, NTILE], I32)
            idx_g = sb2("idx_g", [P, XR], U32)
            idx_s = sb2("idx_s", [P, XR], U32)
            xg = sb2("xg", [P, XR, D])
            xgT = sb2("xgT", [P, 2, D])
            hs = sb2("hs", [P, 2, F])
            hT = sb2("hT", [P, 2, FC, P])
            b2r = sb2("b2r", [P, XR, D])
            yb = sb2("yb", [P, 2, D])
            ys = sb2("ys", [P, 2, D])
            st3 = sb2("st3", [P, 2, 6])
            mv3 = sb2("mv3", [P, 2, 2])
            ve3 = sb2("ve3", [P, 2])
            rs3 = sb2("rs3", [P, 2])
            yo = sb2("yo", [P, XR, D])

        x2_dram = nc.dram_tensor("x2_rows", (B * S, D), F32, kind="Internal").ap()

        w_loaded = signal("w_loaded", 1, 16)
        consts_made = signal("consts_made", 1)
        consts_ready = signal("consts_ready", 1)
        wT_ready = signal("wT_ready", 1)
        wT_drained = signal("wT_drained", 1)
        bo_ready = signal("bo_ready", 1)
        carried = signal("carried", 1)
        x_loaded = signal("x_loaded", 1, 16)
        xres_loaded = signal("xres_loaded", 1, 16)
        ctx_loaded = signal("ctx_loaded", 1, 16)
        experts_loaded = signal("experts_loaded", 2, 16)
        x2_stored = [signal(f"x2_stored{t}", 1, 16) for t in range(TPB)]
        UN = {"a": 2, "x": 4}
        sc_done = {u: signal(f"sc_done_{u}", n) for u, n in UN.items()}
        pT_done = {u: signal(f"pT_done_{u}", n) for u, n in UN.items()}
        spread_done = {u: signal(f"spread_done_{u}", n) for u, n in UN.items()}
        r_done = {u: signal(f"r_done_{u}", n) for u, n in UN.items()}
        pv_done = {u: signal(f"pv_done_{u}", n) for u, n in UN.items()}
        max_done = {u: signal(f"max_done_{u}", n) for u, n in UN.items()}
        sub_done = {u: signal(f"sub_done_{u}", n) for u, n in UN.items()}
        exp_done = {u: signal(f"exp_done_{u}", n) for u, n in UN.items()}
        sum_done = {u: signal(f"sum_done_{u}", n) for u, n in UN.items()}
        rec_done = {u: signal(f"rec_done_{u}", n) for u, n in UN.items()}
        pT_copied = {u: signal(f"pT_copied_{u}", n) for u, n in UN.items()}
        r_copied = {u: signal(f"r_copied_{u}", n) for u, n in UN.items()}
        norm_done = {u: signal(f"norm_done_{u}", n) for u, n in UN.items()}
        JN = {"xT": 2, "q": 2, "k": 1, "v": 2, "oa": 2, "x1T": 2, "ctxT": 1, "kx": 1, "qx": 2, "vx": 3, "ox": 2,
              "x2T": 2, "rt": 2}
        computed = {j: signal(f"computed_{j}", n) for j, n in JN.items()}
        taken = {j: signal(f"taken_{j}", n) for j, n in JN.items()}
        kblk_made = signal("kblk_made", 1)
        kxblk_made = signal("kxblk_made", 1)
        x1r_made = signal("x1r_made", 1)
        stats_done = {n: signal(f"stats_done{n}", 2) for n in (1, 2)}
        mean_done = {n: signal(f"mean_done{n}", 2) for n in (1, 2)}
        eps_added = {n: signal(f"eps_added{n}", 2) for n in (1, 2)}
        rstd_done = {n: signal(f"rstd_done{n}", 2) for n in (1, 2)}
        ln_done = {n: signal(f"ln_done{n}", 2) for n in (1, 2)}
        part1_signals = [x_loaded, xres_loaded, ctx_loaded, *x2_stored, kblk_made, kxblk_made, x1r_made]
        for group in (spread_done, sc_done, pT_done, r_done, pv_done, max_done, sub_done, exp_done, sum_done, rec_done, pT_copied,
                      r_copied, norm_done, computed, taken, stats_done, mean_done, eps_added, rstd_done, ln_done):
            part1_signals += group.values()
        pool2 = signal("pool2", 1)
        dve2 = signal("dve2", 1)
        exp2_done = signal("exp2_done", 1)
        counts_done = signal("counts_done", 1)
        hot_done = signal("hot_done", 1)
        entry_done = signal("entry_done", 1)
        hot_used = signal("hot_used", 1)
        table_done = signal("table_done", 1)
        table_ready = signal("table_ready", 1)
        f_names = ("idx_g_made", "idx_s_made", "xgT_done", "xgT_copied", "h_done", "h_copied", "hT_done", "gelu_done", "y_done",
                   "bias_added", "res_done", "st3_done", "mv3_done", "ve3_done", "rs3_done", "ln3_done")
        f = {n: signal(n, 1) for n in f_names}
        gathered = [signal(f"gathered{m}", 1, 16) for m in range(XR)]
        b2_loaded = [signal(f"b2_loaded{m}", 1, 16) for m in range(XR)]
        stored = [signal(f"stored{m}", 1, 16) for m in range(XR)]

        def wait_ring(eng, ring, g, m, behind=0):
            wait(eng, ring[(m - behind) % XR], g + (m - behind) // XR)

        def exists(b):
            return not isinstance(b, int) or 0 <= b < B

        JOBS = [
            [("ctxT", 0, 2), ("ox", 0, 3), ("kx", 0, 2), ("x1T", 1, 2)],
            [("qx", 0, 2), ("qx", 1, 2)],
            [("ox", 1, 3), ("vx", 0, 2), ("vx", 1, 2), ("vx", 2, 2)],
            [("oa", 0, 1), ("x2T", 0, 3), ("xT", 0, 0), ("xT", 1, 0), ("rt", 0, 3)],
            [("oa", 1, 1), ("q", 0, 0), ("q", 1, 0), ("k", 0, 0)],
            [("x2T", 1, 3), ("v", 0, 0), ("v", 1, 0), ("x1T", 0, 1), ("rt", 1, 3)],
        ]
        FLAT = [j for step in JOBS for j in step]
        assert len(FLAT) % 2 == 0
        UNITS = [("a", 0), ("a", 1), ("x", 0), ("x", 1), ("x", 2), ("x", 3)]
        LAG = {"a": 1, "x": 2}
        LAST_LAG = 3
        FIRST_FULL = LAST_LAG + 1

        def job_before(n, i):
            for back in range(2, 4 * len(FLAT), 2):
                m, it = (n - back) % len(FLAT), i + (n - back) // len(FLAT)
                if exists(it - FLAT[m][2]):
                    return FLAT[m][0], FLAT[m][1], it - FLAT[m][2]
            return None

        def unit_at(n, i):
            it = i + n // 6
            kind, k = UNITS[n % 6]
            return kind, k, it - LAG[kind], (n % 6) % 2

        def unit_before(n, i, by):
            for back in range(by, 24, by):
                u = unit_at(n - back, i)
                if exists(u[2]):
                    return u[:3]
            return None

        def wait_for(eng, signals, event):
            if event is not None:
                wait(eng, signals[event[0]], event[2], event[1])

        def bank_of(n):
            return ps_m[:, n % 2, 0:256]

        def jobs_of(step, i):
            start = sum(len(s) for s in JOBS[:step])
            for n, (job, k, lag) in enumerate(JOBS[step], start):
                if exists(i - lag):
                    yield n, job, k, i - lag

        block = top.enter_context(nc.Block())
        DVE_LEXP, DVE_ONEHOT, POOL2 = 3, 7, 4
        out_rows = out.rearrange("b s d -> (b s) d")

        def tail_of_part1(eng):
            for sig in part1_signals:
                wait(eng, sig, B - 1)

        N_LOADS = 12

        def for_tiles(eng, one, extra):
            first, last = 2 * XR, (NTILE - 2) // XR * XR
            for j in range(first):
                one(j, j // XR, j % XR)
            with eng.Fori(first // XR, last // XR) as g:
                for m in range(XR):
                    one(g * XR + m, g, m)
            for j in range(last, NTILE + extra):
                one(j, j // XR, j % XR)

        def loop_batches(eng, iteration):
            for i in range(FIRST_FULL):
                iteration(eng, i)
            with eng.Fori(FIRST_FULL, B) as i:
                iteration(eng, i)
            for i in range(B, B + LAST_LAG):
                iteration(eng, i)


        def settled(eng):
            eng.sem_inc(carried.sem, 1)

        def sp_iteration(sp, i):
            p, a, c, z = i, i - 1, i - 2, i - 3
            if exists(a):
                wait(sp, taken["oa"], a - 1, 1)
                sp.dma_start(xres[:], x_tiles(a)).then_inc(xres_loaded.sem, 16)
                wait(sp, computed["ctxT"], a - 1)
                sp.dma_start(ctx_s[0:K2, :], row_of(ctx_in, a)).then_inc(ctx_loaded.sem, 16)
            if exists(z):
                wait(sp, ln_done[2], z, 0)
                sp.dma_start(x2_tile(z, 0), x2s[:, 0, :]).then_inc(x2_stored[0].sem, 16)
                wait(sp, ln_done[2], z, 1)
                sp.dma_start(x2_tile(z, 1), x2s[:, 1, :]).then_inc(x2_stored[1].sem, 16)
            if not isinstance(i, int) or i < B - 1:
                wait(sp, computed["xT"], p)
                sp.dma_start(xs[:], x_tiles(p + 1)).then_inc(x_loaded.sem, 16)

        def row_of(t, b):
            if isinstance(b, int):
                return t[b]
            return t[bass.ds(b, 1)].rearrange("a s d -> (a s) d")

        def x_tiles(b):
            return row_of(x, b).rearrange("(t p) d -> p t d", p=P)

        def x2_tile(b, t):
            v = x2_dram.rearrange("(b t p) d -> b t p d", t=TPB, p=P)
            if isinstance(b, int):
                return v[b, t]
            return v[bass.ds(b, 1), t].rearrange("a p d -> (a p) d")

        def load_experts(sp, e):
            if isinstance(e, int):
                d1, d2, s1, s2 = w1s[:, e], w2s[:, e], w1[e], w2[e]
            else:
                d1 = w1s[:, bass.ds(e, 1)].rearrange("p a c f -> p (a c) f")
                d2 = w2s[:, bass.ds(e, 1)].rearrange("p a c f -> p (a c) f")
                s1 = w1[bass.ds(e, 1)].rearrange("a d f -> (a d) f")
                s2 = w2[bass.ds(e, 1)].rearrange("a d f -> (a d) f")
            sp.dma_start(d1, s1.rearrange("(c p) f -> p c f", p=P)).then_inc(experts_loaded.sem, 16)
            sp.dma_start(d2, s2.rearrange("(c p) d -> p c d", p=P)).then_inc(experts_loaded.sem, 16)

        @block.sync
        def _(sp):
            def load(dst, src):
                sp.dma_start(dst, src).then_inc(w_loaded.sem, 16)

            sp.dma_start(xs[:], x_tiles(0)).then_inc(x_loaded.sem, 16)
            load(wqkv_s[:], w_qkv.rearrange("(c p) n -> p c n", p=P))
            for n, w in enumerate((wq, wk, wv, wo)):
                raw = w_raw[n // 2][:, n % 2, 0:KC * D].rearrange("p (c d) -> p c d", c=KC)
                load(raw, w.rearrange("(c p) d -> p c d", p=P))
            load(wout_s[:], w_out.rearrange("(c p) n -> p c n", p=P))
            load(router_s[:], router_w.rearrange("(c p) n -> p c n", p=P))
            for dst, src in ((bq_s, bq), (bk_s, bk), (bv_s, bv)):
                with nc.allow_non_contiguous_dma("a bias of 256 values, by partition"):
                    load(dst[:], src.rearrange("(c p) -> p c", p=P))
            load(bo_s[:], bo.rearrange("(a d) -> a d", a=1).to_broadcast([P, D]))
            load(oTa[0:E * FC, 0, 0:P], b1.rearrange("e (c p) -> (e c) p", p=P))
            early = E - (B - 1 - FIRST_FULL)
            for i in range(FIRST_FULL):
                sp_iteration(sp, i)
                if i < early:
                    load_experts(sp, i)
            with sp.Fori(FIRST_FULL, B - 1) as i:
                sp_iteration(sp, i)
                load_experts(sp, i - (FIRST_FULL - early))
            for i in range(B - 1, B + LAST_LAG):
                sp_iteration(sp, i)
            sp.wait_ge(table_ready.sem, 2)

            def b2_load(j, g, m):
                e = sp.value_load(e_i[0:1, j:j + 1] if isinstance(j, int) else e_i[0:1, bass.ds(j, 1)],
                                  min_val=0, max_val=E - 1)
                wait(sp, f["bias_added"], j - XR)
                src = b2[bass.ds(e, 1), :].to_broadcast([P, D])
                sp.dma_start(b2r[:, m, :], src).then_inc(b2_loaded[m].sem, 16)

            for_tiles(sp, b2_load, 0)

        def transpose(dst, src):
            return nc.tensor.transpose(dst, src, ident[:])

        def pe_scores(pe, n, i):
            kind, k, b, par = unit_at(n, i)
            if not exists(b):
                return
            wait_for(pe, sub_done, unit_before(n, i, 1))
            if kind == "a":
                wait(pe, taken["q"], b)
                wait(pe, kblk_made, b)
                for h in range(KC):
                    last = nc.tensor.matmul(ps_s[:, h, :], qT[:, h, k * SEG:(k + 1) * SEG],
                                            kblk[:, h, k].rearrange("p h k -> p (h k)"), start=True, stop=True)
            else:
                wait(pe, taken["qx"], b)
                wait(pe, kxblk_made, b)
                t, h = k // 2, k % 2
                for q in range(2):
                    last = nc.tensor.matmul(ps_s[:, q, 0:4 * K2], qxT[:, h, t * P:(t + 1) * P],
                                            kxblk[:, h, 4 * q:4 * q + 4].rearrange("p h k -> p (h k)"),
                                            start=True, stop=True)
            last.then_inc(sc_done[kind].sem, 1)

        def pe_probT(pe, n, i):
            kind, k, b, par = unit_at(n, i)
            if not exists(b):
                return
            wait(pe, exp_done[kind], b, k)
            wait_for(pe, pT_copied, unit_before(n, i, 1))
            width = H * KEYS if kind == "a" else HH * K2
            for c in range(-(-width // P)):
                cols = min(P, width - c * P)
                last = transpose(ps_t[0:cols, c // 4, (c % 4) * P:(c % 4) * P + P],
                                 prob[:, par, c * P:c * P + cols])
            last.then_inc(pT_done[kind].sem, 1)

        def pe_attend(pe, n, i):
            kind, k, b, par = unit_at(n, i)
            if not exists(b):
                return
            wait_for(pe, norm_done, unit_before(n, i, 1))
            wait(pe, spread_done[kind], b, k)
            for h in range(KC if kind == "a" else 1):
                last = transpose(ps_r[:, h * P:(h + 1) * P],
                                 rden_s[:, par, h * HH:(h + 1) * HH].rearrange("p h d -> p (h d)"))
            last.then_inc(r_done[kind].sem, 1)
            wait(pe, pT_copied[kind], b, k)
            if kind == "a":
                wait(pe, taken["v"], b)
                for pair in range(H // 2):
                    g, h = pair % 4, pair // 4
                    last = nc.tensor.matmul(ps_o[32 * g:32 * g + 32, h * P:(h + 1) * P],
                                            vA[:, k, 32 * pair:32 * pair + 32],
                                            probT[:, par, pair * P:(pair + 1) * P], start=True, stop=True)
            else:
                wait(pe, taken["vx"], b)
                h = k % 2
                for part in range(2):
                    for g in range(HH // 2):
                        c = 2 * g * K2 // P + part
                        rows = LASTROWS if c == CH - 1 else P
                        off = 32 * (g - G0[c])
                        last = nc.tensor.matmul(ps_o[32 * g:32 * g + 32, 0:P], vX[0:rows, c, h, off:off + 32],
                                                probT[0:rows, par, c * P:(c + 1) * P],
                                                start=(part == 0), stop=(part == 1))
            last.then_inc(pv_done[kind].sem, 1)

        def pe_job(pe, n, job, k, b, i):
            dst = bank_of(n)
            wait_for(pe, taken, job_before(n, i))

            def project(lhs, rhs, dst=dst, width=D):
                for c in range(KC):
                    last = nc.tensor.matmul(dst[:, 0:width], lhs(c), rhs(c), start=(c == 0), stop=(c == KC - 1))
                return last

            cols = slice(k * P, (k + 1) * P)
            if job == "xT":
                wait(pe, x_loaded, b)
                for c in range(KC):
                    last = transpose(dst[:, c * P:(c + 1) * P], xs[:, k, c * P:(c + 1) * P])
            elif job == "x1T":
                wait(pe, ln_done[1], b, k)
                for c in range(KC):
                    last = transpose(dst[:, c * P:(c + 1) * P], x1[:, k, c * P:(c + 1) * P])
            elif job == "x2T":
                wait(pe, ln_done[2], b, k)
                for c in range(KC):
                    last = transpose(dst[:, c * P:(c + 1) * P], x2s[:, k, c * P:(c + 1) * P])
            elif job == "ctxT":
                wait(pe, ctx_loaded, b)
                for c in range(KC):
                    last = nc.tensor.transpose(dst[:, c * P:c * P + K2], ctx_s[0:K2, c * P:(c + 1) * P],
                                               ident[0:K2, 0:K2])
            elif job == "q":
                wait(pe, taken["xT"], b)
                last = project(lambda c: wqkv_s[:, c, cols], lambda c: xT[:, c, :])
            elif job == "k":
                for h in range(KC):
                    last = project(lambda c: wqkv_s[:, c, D + h * P:D + (h + 1) * P],
                                   lambda c: xkT[:, c, :, 0, :], dst[:, h * P:], P)
            elif job == "v":
                wait(pe, taken["xT"], b)
                last = project(lambda c: xkT[:, c, k].rearrange("p w k -> p (w k)"),
                               lambda c: wqkv_s[:, c, 2 * D:3 * D])
            elif job == "oa":
                wait(pe, norm_done["a"], b, k)
                last = project(lambda c: oTa[:, c, cols], lambda c: wout_s[:, c, :])
            elif job == "qx":
                wait(pe, taken["x1T"], b)
                last = project(lambda c: wT[:, 0, c, cols], lambda c: x1T[:, c, :])
            elif job == "kx":
                wait(pe, taken["ctxT"], b)
                for h in range(KC):
                    last = project(lambda c: wT[:, 1, c, h * P:(h + 1) * P],
                                   lambda c: ctxT3[:, c].rearrange("p r k -> p (r k)")[:, 0:P], dst[:, h * P:], P)
            elif job == "vx":
                wait(pe, taken["ctxT"], b)
                for m, ch in enumerate(range(2 * k, min(2 * k + 2, CH))):
                    off = ch * P % K2
                    last = project(
                        lambda c: ctxT3[:, c].rearrange("p r k -> p (r k)")[:, off:off + P],
                        lambda c: wT[:, 2, c].rearrange("p (h j) -> p h j", h=KC)[:, :, 32 * G0[ch]:32 * G0[ch] + 64],
                        dst[:, m * P:], P)
            elif job == "ox":
                wait(pe, norm_done["x"], b, 2 * k + 1)
                last = project(lambda c: oTx[:, c, cols], lambda c: wT[:, 3, c, :])
            elif job == "rt":
                wait(pe, taken["x2T"], b, k)
                last = project(lambda c: x2T[:, c, cols], lambda c: router_s[:, c, :], dst, E)
            last.then_inc(computed[job].sem, 1)

        def pe_iteration(pe, i):
            for s in range(6):
                pe_scores(pe, s, i)
                pe_probT(pe, s - 1, i)
                pe_attend(pe, s - 2, i)
                for n, job, k, b in jobs_of(s, i):
                    pe_job(pe, n, job, k, b, i)

        @block.tensor
        def _(pe):
            pe.wait_ge(w_loaded.sem, 16 * N_LOADS)
            pe.wait_ge(consts_ready.sem, 1)
            for n in range(4):
                raw = w_raw[n // 2][:, n % 2, 0:KC * D].rearrange("p (c d) -> p c d", c=KC)
                ps = (ps_s, ps_t)[n // 2][:, n % 2, :]
                for c in range(KC):
                    for r in range(KC):
                        last = transpose(ps[:, c * D + r * P:c * D + (r + 1) * P], raw[:, r, c * P:(c + 1) * P])
            nc.tensor.transpose(ps_o[:, 0:E * FC], oTa[0:E * FC, 0, 0:P],
                                ident[0:E * FC, 0:E * FC]).then_inc(wT_ready.sem, 1)
            pe.wait_ge(wT_drained.sem, 1)
            for c in range(KC):
                last = nc.tensor.matmul(ps_m[:, 0, 0:D], bv_s[:, c:c + 1].to_broadcast([P, P]), wT[:, 3, c, :],
                                        start=(c == 0), stop=(c == KC - 1))
            last.then_inc(wT_ready.sem, 1)
            pe.wait_ge(bo_ready.sem, 1)
            loop_batches(pe, pe_iteration)

            pe.wait_ge(pool2.sem, POOL2)
            pe.wait_ge(dve2.sem, DVE_ONEHOT)
            hot = onehot[:].rearrange("p t e -> p (t e)")
            nc.tensor.matmul(ps_s[:, 0, 0:NG], tri[:], hot, start=True, stop=True)
            nc.tensor.matmul(ps_s[:, 1, 0:NG], ones[:], hot, start=True, stop=True).then_inc(counts_done.sem, 1)
            pe.wait_ge(entry_done.sem, 1)
            for t in range(NT):
                pe.wait_ge(hot_done.sem, t + 1)
                nc.tensor.matmul(ps_m[:, 0, 0:3 * NTILE], hot_r[:, t % 4, :],
                                 entry[:, t].rearrange("p c j -> p (c j)"),
                                 start=(t == 0), stop=(t == NT - 1)).then_inc(hot_used.sem, 1)
            pe.wait_ge(table_ready.sem, 2)
            pe.wait_ge(experts_loaded.sem, 32 * E)

            def gathered_rows(j, g, m):
                wait_ring(pe, gathered, g, m)
                wait(pe, f["xgT_copied"], j - 2)
                for c in range(KC):
                    last = transpose(ps_or[:, m % 2, c * P:(c + 1) * P], xg[:, m, c * P:(c + 1) * P])
                last.then_inc(f["xgT_done"].sem, 1)

            def expert_of(j):
                return pe.value_load(e_i[0:1, j:j + 1] if isinstance(j, int) else e_i[0:1, bass.ds(j, 1)],
                                     min_val=0, max_val=E - 1)

            def one(j, g, m):
                if not isinstance(j, int) or 1 <= j <= NTILE:
                    wait(pe, f["h_copied"], j - 1)
                    wait(pe, f["gelu_done"], j - 3)
                    for c in range(FC):
                        last = transpose(ps_t[:, (m - 1) % 2, c * P:(c + 1) * P],
                                         hs[:, (m - 1) % 2, c * P:(c + 1) * P])
                    last.then_inc(f["hT_done"].sem, 1)
                if not isinstance(j, int) or j < NTILE:
                    e = expert_of(j)
                    wait(pe, f["xgT_copied"], j)
                    wait(pe, f["h_copied"], j - 2)
                    for c in range(KC):
                        last = nc.tensor.matmul(ps_s[:, m % 2, :], xgT[:, m % 2, c * P:(c + 1) * P],
                                                w1s[:, bass.ds(e, 1), c, :].rearrange("p a f -> p (a f)"),
                                                start=(c == 0), stop=(c == KC - 1))
                    last.then_inc(f["h_done"].sem, 1)
                if not isinstance(j, int) or j + 1 < NTILE:
                    gathered_rows(j + 1, g + (m + 1) // XR, (m + 1) % XR)
                if not isinstance(j, int) or 1 <= j <= NTILE:
                    e = expert_of(j - 1)
                    wait(pe, f["gelu_done"], j - 1)
                    wait(pe, f["bias_added"], j - 3)
                    for c in range(FC):
                        last = nc.tensor.matmul(ps_m[:, (m - 1) % 2, 0:D], hT[:, (m - 1) % 2, c, :],
                                                w2s[:, bass.ds(e, 1), c, :].rearrange("p a f -> p (a f)"),
                                                start=(c == 0), stop=(c == FC - 1))
                    last.then_inc(f["y_done"].sem, 1)

            gathered_rows(0, 0, 0)
            for_tiles(pe, one, 1)

        def act_probT(act, n, i):
            kind, k, b, par = unit_at(n, i)
            if not exists(b):
                return
            wait(act, pT_done[kind], b, k)
            wait_for(act, pv_done, unit_before(n, i, 2))
            if kind == "a":
                last = nc.scalar.copy(probT[:, par, :], ps_t[:].rearrange("p b n -> p (b n)"))
            else:
                nc.scalar.copy(probT[:, par, 0:512], ps_t[:, 0, :])
                last = nc.scalar.copy(probT[0:LASTROWS, par, 512:640], ps_t[0:LASTROWS, 1, 0:P])
            last.then_inc(pT_copied[kind].sem, 1)

        def act_spread(act, n, i):
            kind, k, b, par = unit_at(n, i)
            if not exists(b):
                return
            heads = H if kind == "a" else HH
            wait(act, rec_done[kind], b, k)
            wait_for(act, r_done, unit_before(n, i, 2))
            nc.scalar.copy(rden_s[:, par, 0:heads],
                           rden[:, par, 0:heads, None].to_broadcast([P, heads, DH])).then_inc(
                               spread_done[kind].sem, 1)

        def act_rden(act, n, i):
            kind, k, b, par = unit_at(n, i)
            if not exists(b):
                return
            wait(act, r_done[kind], b, k)
            wait_for(act, norm_done, unit_before(n, i, 1))
            width = KC * P if kind == "a" else P
            nc.scalar.copy(r_s[:, 0:width], ps_r[:, 0:width]).then_inc(r_copied[kind].sem, 1)

        def act_exp(act, n, i):
            kind, k, b, par = unit_at(n, i)
            if not exists(b):
                return
            width = H * KEYS if kind == "a" else HH * K2
            wait(act, sub_done[kind], b, k)
            nc.scalar.activation(prob[:, par, 0:width], prob[:, par, 0:width], ACT.Exp,
                                 scale=SCALE).then_inc(exp_done[kind].sem, 1)

        def act_take(act, n, job, k, b):
            src = bank_of(n)
            wait(act, computed[job], b, k)
            pair = src.rearrange("p (c n) -> p c n", c=KC)
            cols = slice(k * P, (k + 1) * P)
            if job == "xT":
                wait(act, computed["q"], b - 1)
                wait(act, computed["v"], b - 1)
                nc.scalar.copy(xT[:, :, cols], pair)
                grid = pair.rearrange("p c (r o k e) -> p c r o k e", o=2, k=8, e=2)
                dst = xkT[:, :, k].rearrange("p c w (r o k) -> p c w r o k", o=2, k=8)
                for o in range(2):
                    for c in range(KC):
                        keys = grid[:, c, None, :, o, :, o].to_broadcast([P, 2, SEG // 32, 8])
                        last = nc.scalar.copy(dst[:, c, :, :, o, :], keys)
            elif job == "q":
                wait(act, sc_done["a"], b - 1)
                last = nc.scalar.copy(qT[:, k, :], src)
            elif job == "k":
                wait(act, kblk_made, b - 1)
                last = nc.scalar.copy(kT[:].rearrange("p c s k -> p (c s k)"), src)
            elif job == "v":
                wait(act, pv_done["a"], b - 1)
                dst = vA[:, k, :].rearrange("p (g o d) -> p g o d", o=2, d=DH)
                s4 = src.rearrange("p (g o d) -> p g o d", o=2, d=DH)
                for o in range(2):
                    rows = slice(o * KEYS, (o + 1) * KEYS)
                    last = nc.scalar.copy(dst[rows, :, o, :], s4[rows, :, o, :])
            elif job == "x1T":
                wait(act, computed["qx"], b - 1)
                last = nc.scalar.copy(x1T[:, :, cols], pair)
            elif job == "ctxT":
                wait(act, computed["kx"], b - 1)
                wait(act, computed["vx"], b - 1)
                for c in range(KC):
                    last = nc.scalar.copy(ctxT3[:, c], pair[:, c, None, 0:K2].to_broadcast([P, 3, K2]))
            elif job == "kx":
                wait(act, kxblk_made, b - 1)
                for c in range(KC):
                    last = nc.scalar.activation(kxT[:, c, :], pair[:, c, 0:K2], ACT.Identity, bias=bk_s[:, c:c + 1])
            elif job == "qx":
                wait(act, sc_done["x"], b - 1)
                last = nc.scalar.activation(qxT[:, k, :], src, ACT.Identity, bias=bq_s[:, k:k + 1])
            elif job == "x2T":
                wait(act, computed["rt"], b - 1, k)
                last = nc.scalar.copy(x2T[:, :, cols], pair)
            elif job == "rt":
                t = b * TPB + k
                dst = logits[:, t, :] if isinstance(t, int) else logits[:, bass.ds(t, 1), :].rearrange("p a e -> p (a e)")
                last = nc.scalar.copy(dst, src[:, 0:E])
            last.then_inc(taken[job].sem, 1)

        BY_DVE = ("oa", "ox", "vx")

        def act_iteration(act, i):
            for s in range(6):
                act_probT(act, s - 1, i)
                act_rden(act, s - 2, i)
                act_spread(act, s - 1, i)
                mine = [j for j in jobs_of(s, i) if j[1] not in BY_DVE]
                for j in mine[:1]:
                    act_take(act, *j)
                act_exp(act, s, i)
                for j in mine[1:]:
                    act_take(act, *j)

        @block.scalar
        def _(act):
            act.wait_ge(wT_ready.sem, 1)
            for n in range(4):
                ps = (ps_s, ps_t)[n // 2][:, n % 2, :]
                nc.scalar.copy(wT[:, n].rearrange("p c d -> p (c d)"), ps)
            nc.scalar.copy(b1t[:], ps_o[:, 0:E * FC]).then_inc(wT_drained.sem, 1)
            act.wait_ge(consts_ready.sem, 1)
            loop_batches(act, act_iteration)
            act.wait_ge(dve2.sem, DVE_LEXP)
            nc.scalar.activation(lexp[:].rearrange("p t e -> p (t e)"), tmp_a[:].rearrange("p t e -> p (t e)"),
                                 ACT.Exp).then_inc(exp2_done.sem, 1)
            act.wait_ge(table_ready.sem, 2)

            def rows_copy(j, m):
                wait(act, f["xgT_done"], j)
                wait(act, f["h_done"], j - 2)
                nc.scalar.copy(xgT[:, m % 2, :], ps_or[:, m % 2, 0:D]).then_inc(f["xgT_copied"].sem, 1)

            def one(j, g, m):
                if not isinstance(j, int) or 1 <= j <= NTILE:
                    e = act.value_load(e_i[0:1, j - 1:j] if isinstance(j, int) else e_i[0:1, bass.ds(j - 1, 1)],
                                       min_val=0, max_val=E - 1)
                    wait(act, f["hT_done"], j - 1)
                    wait(act, f["y_done"], j - 3)
                    for c in range(FC):
                        last = nc.scalar.activation(hT[:, (m - 1) % 2, c, :],
                                                    ps_t[:, (m - 1) % 2, c * P:(c + 1) * P], ACT.Gelu,
                                                    bias=b1t[:, bass.ds(e * FC + c, 1)])
                    last.then_inc(f["gelu_done"].sem, 1)
                if not isinstance(j, int) or j + 1 < NTILE:
                    rows_copy(j + 1, m + 1)

            rows_copy(0, 0)
            for_tiles(act, one, 1)

        def unit_views(kind, par):
            if kind == "a":
                return (ps_s[:].rearrange("p b (h k) -> p (b h) k", k=KEYS),
                        prob[:, par, :].rearrange("p (h k) -> p h k", k=KEYS), H, mx[:, par, :],
                        mx[:, par, :, None].to_broadcast([P, H, KEYS]))
            return (ps_s[:, :, 0:4 * K2].rearrange("p b (h k) -> p b h k", k=K2),
                    prob[:, par, 0:HH * K2].rearrange("p (b h k) -> p b h k", b=2, k=K2), HH,
                    mx[:, par, 0:HH].rearrange("p (b h) -> p b h", b=2),
                    mx[:, par, 0:HH].rearrange("p (b h) -> p b h", b=2)[:, :, :, None].to_broadcast([P, 2, 4, K2]))

        def dve_softmax(dve, n, i):
            kind, k, b, par = unit_at(n, i)
            if not exists(b):
                return
            s, p, _, m, mb = unit_views(kind, par)
            wait(dve, sc_done[kind], b, k)
            nc.vector.tensor_reduce(m, s, axis=AX, op=ALU.max).then_inc(max_done[kind].sem, 1)
            wait(dve, max_done[kind], b, k)
            wait_for(dve, pT_done, unit_before(n, i, 2))
            nc.vector.tensor_tensor(p, s, mb, ALU.subtract).then_inc(sub_done[kind].sem, 1)

        def dve_denominator(dve, n, i):
            kind, k, b, par = unit_at(n, i)
            if not exists(b):
                return
            heads, width = (H, KEYS) if kind == "a" else (HH, K2)
            wait(dve, exp_done[kind], b, k)
            nc.vector.tensor_reduce(den[:, par, 0:heads],
                                    prob[:, par, 0:heads * width].rearrange("p (h k) -> p h k", k=width),
                                    axis=AX, op=ALU.add).then_inc(sum_done[kind].sem, 1)
            wait(dve, sum_done[kind], b, k)
            wait_for(dve, spread_done, unit_before(n, i, 2))
            nc.vector.reciprocal(rden[:, par, 0:heads], den[:, par, 0:heads]).then_inc(rec_done[kind].sem, 1)

        def dve_normalise(dve, n, i):
            kind, k, b, par = unit_at(n, i)
            if not exists(b):
                return
            wait(dve, pv_done[kind], b, k)
            wait(dve, r_copied[kind], b, k)
            if kind == "a":
                wait(dve, computed["oa"], b - 1, k)
                last = nc.vector.tensor_tensor(oTa[:, :, k * SEG:(k + 1) * SEG],
                                               ps_o[:, 0:256].rearrange("p (c n) -> p c n", c=KC),
                                               r_s[:].rearrange("p (c n) -> p c n", c=KC), ALU.mult)
            else:
                t, h = k // 2, k % 2
                wait(dve, computed["ox"], b - 1, t)
                last = nc.vector.tensor_tensor(oTx[:, h, t * P:(t + 1) * P], ps_o[:, 0:P], r_s[:, 0:P], ALU.mult)
            last.then_inc(norm_done[kind].sem, 1)

        def dve_take(dve, n, job, k, b):
            src = bank_of(n)
            wait(dve, computed[job], b, k)
            if job == "vx":
                wait(dve, pv_done["x"], b - 1)
                chunks = slice(2 * k, min(2 * k + 2, CH))
                m = chunks.stop - chunks.start
                nc.vector.tensor_tensor(vX[:, chunks], src[:, 0:m * P].rearrange("p (c h j) -> p c h j", c=m, h=KC),
                                        vmask[:, chunks, None, :].to_broadcast([P, m, KC, 64]),
                                        ALU.mult).then_inc(taken[job].sem, 1)
                return
            which = 1 if job == "oa" else 2
            s = sums(which, k)
            q = 2 * (which - 1) + k
            if job == "oa":
                wait(dve, xres_loaded, b)
                add = xres[:, k, :]
            else:
                wait(dve, x1r_made, b)
                add = x1r[:, k, :]
            nc.vector.tensor_tensor(s[:], src, add, ALU.add).then_inc(taken[job].sem, 1)
            wait(dve, taken[job], b, k)
            nc.vector.bn_stats(st[:, q, :], s[:]).then_inc(stats_done[which].sem, 1)
            wait(dve, stats_done[which], b, k)
            wait(dve, eps_added[which], b - 1, k)
            settled(dve)
            nc.vector.bn_aggr(mv[:, q, :], st[:, q, :]).then_inc(mean_done[which].sem, 1)

        def sums(which, k):
            return ((sum1, sum1b), (sum2, sum2b))[which - 1][k]

        def dve_layernorm(dve, which, k, b):
            if not exists(b):
                return
            q = 2 * (which - 1) + k
            wait(dve, rstd_done[which], b, k)
            if which == 1:
                wait(dve, computed["x1T"], b - 1, 1)
                wait(dve, x1r_made, b - 1)
                dst = x1
            else:
                wait(dve, computed["x2T"], b - 1, k)
                wait(dve, x2_stored[k], b - 1)
                dst = x2s
            nc.vector.tensor_scalar(dst[:, k, :], sums(which, k)[:], mv[:, q, 0:1], rstd[:, q:q + 1],
                                    ALU.subtract, ALU.mult).then_inc(ln_done[which].sem, 1)

        def dve_iteration(dve, i):
            for s in range(6):
                dve_denominator(dve, s - 1, i)
                dve_softmax(dve, s, i)
                if s in (4, 5):
                    dve_layernorm(dve, 1, s - 4, i - 1)
                if s in (1, 3):
                    dve_layernorm(dve, 2, s // 2, i - 3)
                dve_normalise(dve, s - 2, i)
                for n, job, k, b in jobs_of(s, i):
                    if job in BY_DVE:
                        dve_take(dve, n, job, k, b)

        @block.vector
        def _(dve):
            nc.vector.memset(vA[:].rearrange("p s d -> p (s d)"), 0.0)
            nc.vector.memset(eps[:], EPS)
            nc.vector.memset(neg_half[:], -0.5).then_inc(dve2.sem, 1)
            dve.wait_ge(wT_ready.sem, 2)
            dve.wait_ge(w_loaded.sem, 16 * N_LOADS)
            nc.vector.tensor_tensor(bo_s[:], ps_m[:, 0, 0:D], bo_s[:], ALU.add).then_inc(bo_ready.sem, 1)
            dve.wait_ge(consts_ready.sem, 1)
            loop_batches(dve, dve_iteration)

            chain = [1]

            def link(ins):
                chain[0] += 1
                ins.then_inc(dve2.sem, 1)
                dve.wait_ge(dve2.sem, chain[0])
                return chain[0]

            flat = lambda t: t[:].rearrange("p a b -> p (a b)")
            tail_of_part1(dve)
            dve.wait_ge(pool2.sem, POOL2)
            link(nc.vector.tensor_reduce(lmax[:], logits[:], axis=AX, op=ALU.max))
            n = link(nc.vector.tensor_tensor(tmp_a[:], logits[:], lmax[:, :, None].to_broadcast([P, NT, E]),
                                             ALU.subtract))
            assert n == DVE_LEXP
            link(nc.vector.tensor_tensor(onehot[:], logits[:], lmax[:, :, None].to_broadcast([P, NT, E]),
                                         ALU.is_equal))
            link(nc.vector.tensor_tensor(onehot[:], onehot[:], rev[:, None, :].to_broadcast([P, NT, E]), ALU.mult))
            link(nc.vector.tensor_reduce(best[:], onehot[:], axis=AX, op=ALU.max))
            n = link(nc.vector.tensor_tensor(onehot[:], rev[:, None, :].to_broadcast([P, NT, E]),
                                             best[:, :, None].to_broadcast([P, NT, E]), ALU.is_equal))
            assert n == DVE_ONEHOT
            dve.wait_ge(exp2_done.sem, 1)
            link(nc.vector.tensor_reduce(gate[:], lexp[:], axis=AX, op=ALU.add))
            link(nc.vector.reciprocal(gate[:], gate[:]))
            dve.wait_ge(counts_done.sem, 1)
            link(nc.vector.tensor_copy(cnt[:], ps_s[:, 1, 0:NG].rearrange("p (t e) -> p e t", e=E)))
            link(nc.vector.tensor_tensor_scan(flat(scan), flat(zeros), flat(cnt), 0.0, ALU.add, ALU.add))
            link(nc.vector.tensor_tensor(scan[:], scan[:], cnt[:], ALU.subtract))
            link(nc.vector.tensor_reduce(n_e[:], cnt[:], axis=AX, op=ALU.add))
            link(nc.vector.tensor_tensor(cmp[:], n_e[:, :, None].to_broadcast([P, E, NT]),
                                         steps[:, None, :].to_broadcast([P, E, NT]), ALU.is_gt))
            link(nc.vector.tensor_reduce(t_e[:], cmp[:], axis=AX, op=ALU.add))
            link(nc.vector.tensor_tensor_scan(tb_e[:], zeros[:, 0, 0:E], t_e[:], 0.0, ALU.add, ALU.add))
            link(nc.vector.tensor_tensor(base_e[:], tb_e[:], t_e[:], ALU.subtract))
            link(nc.vector.scalar_tensor_tensor(base_e[:], base_e[:], float(P), scan[:, :, 0], ALU.mult, ALU.subtract))
            link(nc.vector.tensor_tensor(scan[:], scan[:], base_e[:, :, None].to_broadcast([P, E, NT]), ALU.add))
            link(nc.vector.tensor_tensor(tmp_a[:], ps_s[:, 0, 0:NG].rearrange("p (t e) -> p t e", e=E),
                                         scan[:].rearrange("p e t -> p t e"), ALU.add))
            link(nc.vector.tensor_tensor(tmp_a[:], tmp_a[:], onehot[:], ALU.mult))
            link(nc.vector.tensor_reduce(slot[:], tmp_a[:], axis=AX, op=ALU.add))
            link(nc.vector.tensor_copy(slot_i[:], slot[:]))
            link(nc.vector.tensor_scalar(row_i[:], slot_i[:], P - 1, None, ALU.bitwise_and))
            link(nc.vector.tensor_scalar(tile_i[:], slot_i[:], 7, None, ALU.logical_shift_right))
            link(nc.vector.tensor_copy(row_f[:], row_i[:]))
            link(nc.vector.tensor_copy(tile_f[:], tile_i[:]))
            link(nc.vector.tensor_tensor(e_cmp[:], tb_e[:, None, :].to_broadcast([P, NTILE, E]),
                                         iota_t[:, :, None].to_broadcast([P, NTILE, E]), ALU.is_le))
            link(nc.vector.tensor_reduce(e_f[:], e_cmp[:], axis=AX, op=ALU.add))
            link(nc.vector.tensor_scalar(e_f[:], e_f[:], float(E - 1), None, ALU.min))
            dve_ins = nc.vector.tensor_copy(e_i[:], e_f[:])
            dve_ins.then_inc(table_ready.sem, 1)
            link(nc.vector.tensor_tensor(entry[:, :, 2, :], tile_f[:, :, None].to_broadcast([P, NT, NTILE]),
                                         iota_t[:, None, :].to_broadcast([P, NT, NTILE]), ALU.is_equal))
            link(nc.vector.tensor_tensor(entry[:, :, 0, :], entry[:, :, 2, :],
                                         token[:, :, None].to_broadcast([P, NT, NTILE]), ALU.mult))
            nc.vector.tensor_tensor(entry[:, :, 1, :], entry[:, :, 2, :],
                                    gate[:, :, None].to_broadcast([P, NT, NTILE]), ALU.mult).then_inc(
                                        entry_done.sem, 1)
            for t in range(NT):
                if t >= 4:
                    dve.wait_ge(hot_used.sem, t - 3)
                nc.vector.tensor_scalar(hot_r[:, t % 4, :], iota_r[:], row_f[:, t:t + 1], None,
                                        ALU.is_equal).then_inc(hot_done.sem, 1)
            dve.wait_ge(hot_used.sem, NT)
            link(nc.vector.tensor_copy(table[:].rearrange("p c j -> p (c j)"), ps_m[:, 0, 0:3 * NTILE]))
            link(nc.vector.tensor_scalar(table[:, 2, :], table[:, 2, :], -float(B * S), float(B * S),
                                         ALU.mult, ALU.add))
            nc.vector.tensor_tensor(table[:, 2, :], table[:, 2, :], table[:, 0, :], ALU.add).then_inc(
                table_ready.sem, 1)
            dve.wait_ge(table_ready.sem, 2)

            def one(j, g, m):
                if not isinstance(j, int) or 2 <= j <= NTILE + 1:
                    q, r = (m - 2) % 2, (m - 2) % XR
                    wait(dve, f["y_done"], j - 2)
                    wait_ring(dve, b2_loaded, g, m, 2)
                    nc.vector.tensor_tensor(yb[:, q, :], ps_m[:, q, 0:D], b2r[:, r, :], ALU.add).then_inc(
                        f["bias_added"].sem, 1)
                    wait(dve, f["bias_added"], j - 2)
                    gates = (table[:, 1, j - 2:j - 1] if isinstance(j, int)
                             else table[:, 1, bass.ds(j - 2, 1)])
                    nc.vector.scalar_tensor_tensor(ys[:, q, :], yb[:, q, :], gates, xg[:, r, :], ALU.mult,
                                                   ALU.add).then_inc(f["res_done"].sem, 1)
                    wait(dve, f["res_done"], j - 2)
                    nc.vector.bn_stats(st3[:, q, :], ys[:, q, :]).then_inc(f["st3_done"].sem, 1)
                    wait(dve, f["st3_done"], j - 2)
                    settled(dve)
                    nc.vector.bn_aggr(mv3[:, q, :], st3[:, q, :]).then_inc(f["mv3_done"].sem, 1)
                if not isinstance(j, int) or j < NTILE:
                    wait(dve, f["h_done"], j)
                    wait(dve, f["hT_done"], j - 2)
                    nc.vector.tensor_copy(hs[:, m % 2, :], ps_s[:, m % 2, :]).then_inc(f["h_copied"].sem, 1)
                if not isinstance(j, int) or 2 <= j <= NTILE + 1:
                    q, r = (m - 2) % 2, (m - 2) % XR
                    wait(dve, f["rs3_done"], j - 2)
                    wait_ring(dve, stored, g, m, 2 + XR)
                    nc.vector.tensor_scalar(yo[:, r, :], ys[:, q, :], mv3[:, q, 0:1], rs3[:, q:q + 1],
                                            ALU.subtract, ALU.mult).then_inc(f["ln3_done"].sem, 1)

            for_tiles(dve, one, 3)

        def pool_rstd(pool, which, k, b):
            if not exists(b):
                return
            q = 2 * (which - 1) + k
            wait(pool, mean_done[which], b, k)
            wait(pool, ln_done[which], b - 1, k)
            nc.gpsimd.tensor_tensor(ve[:, q:q + 1], mv[:, q, 1:2], eps[:], ALU.add).then_inc(eps_added[which].sem, 1)
            wait(pool, eps_added[which], b, k)
            nc.gpsimd.tensor_tensor(rstd[:, q:q + 1], ve[:, q:q + 1], neg_half[:], ALU.pow).then_inc(
                rstd_done[which].sem, 1)

        def pool_iteration(pool, i):
            p, a, c, z = i, i - 1, i - 2, i - 3
            pool_rstd(pool, 2, 0, z)
            if exists(c):
                wait(pool, taken["kx"], c)
                wait(pool, sc_done["x"], c - 1)
                for h in range(KC):
                    last = nc.gpsimd.tensor_tensor(kxblk[:, h], kxT[:, h, None, :].to_broadcast([P, HH, K2]),
                                                   kmask[:, :, None].to_broadcast([P, HH, K2]), ALU.mult)
                last.then_inc(kxblk_made.sem, 1)
            pool_rstd(pool, 2, 1, z)
            if exists(c):
                wait(pool, ln_done[1], c)
                wait(pool, taken["ox"], c - 1)
                nc.gpsimd.tensor_tensor(x1r[:], x1[:], bo_s[:, None, :].to_broadcast([P, TPB, D]),
                                        ALU.add).then_inc(x1r_made.sem, 1)
            pool_rstd(pool, 1, 0, a)
            pool_rstd(pool, 1, 1, a)
            if exists(p):
                wait(pool, taken["k"], p)
                wait(pool, sc_done["a"], p - 1)
                for h in range(KC):
                    last = nc.gpsimd.tensor_tensor(
                        kblk[:, h], kT[:, h, :, None, :].to_broadcast([P, NSEG, HH, KEYS]),
                        kmask[:, None, :, None].to_broadcast([P, NSEG, HH, KEYS]), ALU.mult)
                last.then_inc(kblk_made.sem, 1)

        @block.gpsimd
        def _(pool):
            made = [0]

            def link(ins):
                made[0] += 1
                ins.then_inc(consts_made.sem, 1)
                pool.wait_ge(consts_made.sem, made[0])

            g = nc.gpsimd
            link(g.memset(ident[:], 0.0))
            link(g.memset(ones[:], 1.0))
            link(g.memset(kmask[:], 1.0))
            link(g.memset(vmask[:].rearrange("p c j -> p (c j)"), 1.0))
            link(g.affine_select(out=ident[:], in_=ident[:], compare_op=ALU.not_equal, fill=1.0, base=0,
                                 pattern=[[-1, P]], channel_multiplier=1))
            link(g.affine_select(out=kmask[:], in_=kmask[:], compare_op=ALU.is_ge, fill=0.0, base=0,
                                 pattern=[[-DH, HH]], channel_multiplier=1))
            link(g.affine_select(out=kmask[:], in_=kmask[:], compare_op=ALU.is_ge, fill=0.0, base=DH - 1,
                                 pattern=[[DH, HH]], channel_multiplier=-1))
            for c in range(CH):
                v = vmask[:, c, :].rearrange("p (h d) -> p h d", d=DH)
                off = c * P - 2 * G0[c] * K2
                link(g.affine_select(out=v, in_=v, compare_op=ALU.is_ge, fill=0.0, base=off,
                                     pattern=[[-K2, 4], [0, DH]], channel_multiplier=1))
                link(g.affine_select(out=v, in_=v, compare_op=ALU.is_ge, fill=0.0, base=K2 - 1 - off,
                                     pattern=[[K2, 4], [0, DH]], channel_multiplier=-1))
            pool.wait_ge(dve2.sem, 1)
            g.memset(ve[:], 0.0).then_inc(consts_ready.sem, 1)
            pool.wait_ge(bo_ready.sem, 1)
            loop_batches(pool, pool_iteration)

            tail_of_part1(pool)
            g.iota(rev[:], pattern=[[-1, E]], base=E, channel_multiplier=0, allow_small_or_imprecise_dtypes=True)
            g.iota(steps[:], pattern=[[P, NT]], base=0, channel_multiplier=0, allow_small_or_imprecise_dtypes=True)
            g.iota(iota_r[:], pattern=[[1, P]], base=0, channel_multiplier=0, allow_small_or_imprecise_dtypes=True)
            g.iota(iota_t[:], pattern=[[1, NTILE]], base=0, channel_multiplier=0,
                   allow_small_or_imprecise_dtypes=True)
            g.iota(token[:], pattern=[[P, NT]], base=0, channel_multiplier=1, allow_small_or_imprecise_dtypes=True)
            g.memset(zeros[:].rearrange("p e t -> p (e t)"), 0.0).then_inc(pool2.sem, 1)
            g.memset(tri[:], 1.0).then_inc(pool2.sem, 1)
            pool.wait_ge(pool2.sem, 2)
            g.affine_select(out=tri[:], in_=tri[:], compare_op=ALU.is_gt, fill=0.0, base=0, pattern=[[1, P]],
                            channel_multiplier=-1).then_inc(pool2.sem, 1)
            pool.wait_ge(pool2.sem, 3)
            g.memset(idx_g[:, 0:1], 0).then_inc(pool2.sem, 1)
            pool.wait_ge(table_ready.sem, 2)
            for t in range(TPB):
                pool.wait_ge(x2_stored[t].sem, 16 * B)

            def column(c, j):
                return table[:, c, j:j + 1] if isinstance(j, int) else table[:, c, bass.ds(j, 1)]

            def gather(j, g, m):
                wait(pool, f["res_done"], j - XR)
                wait(pool, f["xgT_done"], j - XR)
                wait_ring(pool, gathered, g, m, XR)
                nc.gpsimd.tensor_copy(idx_g[:, m:m + 1], column(0, j)).then_inc(f["idx_g_made"].sem, 1)
                wait(pool, f["idx_g_made"], j)
                settled(pool)
                nc.gpsimd.indirect_dma_start(xg[:, m, :], None, x2_dram,
                                             bass.IndirectOffsetOnAxis(ap=idx_g[:, m:m + 1], axis=0),
                                             bounds_check=B * S - 1, oob_is_err=False).then_inc(gathered[m].sem, 16)

            def one(j, g, m):
                if not isinstance(j, int) or j >= 3:
                    r = (m - 3) % XR
                    wait_ring(pool, stored, g, m, 3 + XR)
                    nc.gpsimd.tensor_copy(idx_s[:, r:r + 1], column(2, j - 3)).then_inc(f["idx_s_made"].sem, 1)
                    wait(pool, f["ln3_done"], j - 3)
                    wait(pool, f["idx_s_made"], j - 3)
                    settled(pool)
                    nc.gpsimd.indirect_dma_start(out_rows, bass.IndirectOffsetOnAxis(ap=idx_s[:, r:r + 1], axis=0),
                                                 yo[:, r, :], None, bounds_check=B * S - 1,
                                                 oob_is_err=False).then_inc(stored[r].sem, 16)
                if not isinstance(j, int) or 2 <= j <= NTILE + 1:
                    q = (m - 2) % 2
                    wait(pool, f["mv3_done"], j - 2)
                    wait(pool, f["ln3_done"], j - 4)
                    nc.gpsimd.tensor_tensor(ve3[:, q:q + 1], mv3[:, q, 1:2], eps[:], ALU.add).then_inc(f["ve3_done"].sem, 1)
                    wait(pool, f["ve3_done"], j - 2)
                    nc.gpsimd.tensor_tensor(rs3[:, q:q + 1], ve3[:, q:q + 1], neg_half[:], ALU.pow).then_inc(
                        f["rs3_done"].sem, 1)
                if not isinstance(j, int) or j + 2 < NTILE:
                    gather(j + 2, g + (m + 2) // XR, (m + 2) % XR)

            gather(0, 0, 0)
            gather(1, 0, 1)
            for_tiles(pool, one, 3)
            for j in range(NTILE - XR, NTILE):
                wait_ring(pool, stored, j // XR, j % XR)



_INS = ["x", "ctx_1024", "L0_attn_W_qkv", "L0_attn_W_out", "L0_xattn_Wq", "L0_xattn_bq", "L0_xattn_Wk",
        "L0_xattn_bk", "L0_xattn_Wv", "L0_xattn_bv", "L0_xattn_Wo", "L0_xattn_bo", "L0_ffn_router_w", "L0_ffn_w1",
        "L0_ffn_b1", "L0_ffn_w2", "L0_ffn_b2"]


def kernel(**inputs):
    import concourse.bacc as bacc
    from concourse.bass_utils import run_bass_kernel_spmd

    nc = bacc.Bacc("TRN2", target_bir_lowering=False, num_devices=1)
    arrays, args = {}, []
    for name in _INS:
        a = np.ascontiguousarray(inputs[name])
        arrays[f"in_{name}"] = a
        args.append(nc.dram_tensor(f"in_{name}", a.shape, mybir.dt.from_np(a.dtype), kind="ExternalInput").ap())
    shape = inputs["x"].shape
    args.append(nc.dram_tensor("out", shape, mybir.dt.float32, kind="ExternalOutput").ap())
    decoder_layer(nc, *args)
    r = run_bass_kernel_spmd(nc, [arrays], core_ids=[0])
    return r.results[0]["out"]
```

```python
from contextlib import ExitStack

import concourse.bass as bass
import numpy as np
from concourse import mybir

P = 128
F32 = mybir.dt.float32
U32 = mybir.dt.uint32
I32 = mybir.dt.int32
ALU = mybir.AluOpType
ACT = mybir.ActivationFunctionType
AX = mybir.AxisListType.X
EPS = 1e-5


class Signal:

    def __init__(self, sem, per, unit=1):
        self.sem, self.per, self.unit = sem, per, unit

    def at(self, b, k=None):
        k = self.per - 1 if k is None else k
        return (b * self.per + (k + 1)) * self.unit


def wait(eng, sig, b, k=None):
    if isinstance(b, int) and b < 0:
        return
    eng.wait_ge(sig.sem, sig.at(b, k))


def decoder_layer(nc, x, ctx_in, w_qkv, w_out, wq, bq, wk, bk, wv, bv, wo, bo, router_w, w1, b1, w2, b2, out):
    B, S, D = x.shape
    K2 = ctx_in.shape[1]
    E, _, F = w1.shape
    H = 16
    DH = D // H
    SEG = 128
    NSEG = S // SEG
    KEYS = SEG // 2
    KC = D // P
    FC = F // P
    HH = H // KC
    NT = B * S // P
    TPB = S // P
    NTILE = NT + E - 1
    LIST = B * S
    LIST_ROWS = E * LIST + (E - 1) * P
    RW = 64
    SCALE = float(DH) ** -0.5
    CH = -(-HH * K2 // P)
    LASTROWS = HH * K2 - (CH - 1) * P
    G0 = [min(c * P // (2 * K2), HH // 2 - 2) for c in range(CH)]
    assert (KC, NSEG, TPB, HH, DH, SEG // 2 * HH) == (2, 2, 2, 8, 16, 512) and 4 * K2 <= 512
    for g in range(HH // 2):
        lo, hi = 2 * g * K2 // P, (2 * (g + 1) * K2 - 1) // P
        assert hi == lo + 1 and all(0 <= g - G0[c] <= 1 for c in (lo, hi))

    with ExitStack() as top:
        def alloc(stack, name, shape, dt=F32):
            return stack.enter_context(nc.sbuf_tensor(name, shape, dt))

        def psum(name, shape):
            return top.enter_context(nc.psum_tensor(name, shape, F32))

        def signal(name, per, unit=1):
            return Signal(top.enter_context(nc.semaphore(name)), per, unit)

        ps_s = psum("ps_s", [P, 2, 512])
        ps_t = psum("ps_t", [P, 2, 512])
        ps_m = psum("ps_m", [P, 3, 512])
        ps_o = psum("ps_o", [P, 512])

        ps_x = [ps_o, ps_m[:, 2, :]]

        w1s = alloc(top, "w1s", [P, E, KC, F])
        w2s = alloc(top, "w2s", [P, E, FC, D])
        logits = alloc(top, "logits", [P, TPB, E])
        lmax = alloc(top, "lmax", [P, TPB])
        ldif = alloc(top, "ldif", [P, TPB, E])
        lexp = alloc(top, "lexp", [P, TPB, E])
        lsum = alloc(top, "lsum", [P, TPB])
        ismax = alloc(top, "ismax", [P, TPB, E])
        best = alloc(top, "best", [P, TPB])
        onehot = alloc(top, "onehot", [P, RW])
        before = alloc(top, "before", [P, RW])
        rank = alloc(top, "rank", [P, TPB, E])
        place = alloc(top, "place", [P, TPB])
        place_i = alloc(top, "place_i", [P, TPB], U32)
        member = alloc(top, "member", [P, TPB, 2])
        batch_step = alloc(top, "batch_step", [P, TPB])
        rev = alloc(top, "rev", [P, E])
        tri = alloc(top, "tri", [P, P])
        round_up = alloc(top, "round_up", [P, E])
        tile_no = alloc(top, "tile_no", [P, 1])
        ident = alloc(top, "ident", [P, P])
        ones = alloc(top, "ones", [P, P])
        b1t = alloc(top, "b1t", [P, E * FC])
        eps = alloc(top, "eps", [P, 1])
        neg_half = alloc(top, "neg_half", [P, 1])

        with ExitStack() as part1:
            def sb1(name, shape, dt=F32):
                return alloc(part1, name, shape, dt)

            wqkv_s = sb1("wqkv_s", [P, KC, 3 * D])
            wout_s = sb1("wout_s", [P, KC, D])
            wT = sb1("wT", [P, 4, KC, D])
            router_s = sb1("router_s", [P, KC, RW])
            bq_s = sb1("bq_s", [P, KC])
            bk_s = sb1("bk_s", [P, KC])
            bv_s = sb1("bv_s", [P, KC])
            bo_s = sb1("bo_s", [P, D])
            kmask = sb1("kmask", [P, HH])
            vmask = sb1("vmask", [P, CH, 64])
            xs = sb1("xs", [P, TPB, D])
            xres = sb1("xres", [P, TPB, D])
            xT = sb1("xT", [P, KC, S])
            xkT = sb1("xkT", [P, KC, NSEG, 2, KEYS])
            qT = sb1("qT", [P, KC, S])
            kT = sb1("kT", [P, KC, NSEG, KEYS])
            kblk = sb1("kblk", [P, KC, NSEG, HH, KEYS])
            vA = sb1("vA", [P, NSEG, D])
            prob = sb1("prob", [P, 3, 1024])
            probT = sb1("probT", [P, 2, 1024])
            mx = sb1("mx", [P, 2, H])
            den = sb1("den", [P, 2, H])
            rden = sb1("rden", [P, 2, H])
            oTa = sb1("oTa", [P, KC, S])
            oTx = sb1("oTx", [P, KC, S])
            sum1 = sb1("sum1", [P, D])
            sum2 = sb1("sum2", [P, D])
            sum1b = sb1("sum1b", [P, D])
            sum2b = sb1("sum2b", [P, D])
            st = sb1("st", [P, 4, 6])
            mv = sb1("mv", [P, 4, 2])
            ve = sb1("ve", [P, 4])
            rstd = sb1("rstd", [P, 4])
            x1 = sb1("x1", [P, TPB, D])
            x1r = sb1("x1r", [P, TPB, D])
            x1T = sb1("x1T", [P, KC, S])
            qxT = sb1("qxT", [P, KC, S])
            ctx_s = sb1("ctx_s", [P, D])
            ctxT3 = sb1("ctxT3", [P, KC, 3, K2])
            kxT = sb1("kxT", [P, KC, K2])
            kxblk = sb1("kxblk", [P, KC, HH, K2])
            vX = sb1("vX", [P, CH, KC, 64])
            x2s = sb1("x2s", [P, TPB, D])
            x2T = sb1("x2T", [P, KC, S])
        fill = x2T[:].rearrange("p c s -> p (c s)")
        assert LIST_ROWS % P == 0
        w_raw = [prob, probT]

        XR = 4
        with ExitStack() as part2:
            def sb2(name, shape, dt=F32):
                return alloc(part2, name, shape, dt)

            t_i = sb2("t_i", [P, E], I32)
            n_e = sb2("n_e", [P, E])
            t_e = sb2("t_e", [P, E])
            tb_e = sb2("tb_e", [P, E])
            zeros = sb2("zeros", [P, E])
            ended = sb2("ended", [P, E])
            ended_t = sb2("ended_t", [P, E])
            e_f = sb2("e_f", [P, 1])
            start_f = sb2("start_f", [P, 1])
            plan_f = sb2("plan_f", [P, 2])
            plan_i = sb2("plan_i", [P, 2, NTILE], I32)
            row_i, e_i = plan_i[:, 0, :], plan_i[:, 1, :]
            slots = sb2("slots", [P, NTILE, 2])
            idx_g = sb2("idx_g", [P, XR], U32)
            idx_s = sb2("idx_s", [P, XR], U32)
            xg = sb2("xg", [P, XR, D])
            xgT = sb2("xgT", [P, 2, D])
            hs = sb2("hs", [P, 2, F])
            hT = sb2("hT", [P, 2, FC, P])
            b2r = sb2("b2r", [P, XR, D])
            yb = sb2("yb", [P, 2, D])
            ys = sb2("ys", [P, 2, D])
            st3 = sb2("st3", [P, 2, 6])
            mv3 = sb2("mv3", [P, 2, 2])
            ve3 = sb2("ve3", [P, 2])
            rs3 = sb2("rs3", [P, 2])
            yo = sb2("yo", [P, XR, D])

        lists = nc.dram_tensor("token_lists", (LIST_ROWS, 2), F32, kind="Internal").ap()
        x2_dram = nc.dram_tensor("x2_rows", (B * S, D), F32, kind="Internal").ap()

        square_loaded = signal("square_loaded", 4, 16)
        qkv_loaded = signal("qkv_loaded", 1, 16)
        w_loaded = signal("w_loaded", 1, 16)
        ident_made = signal("ident_made", 1)
        squares_done = signal("squares_done", 1)
        b1_done = signal("b1_done", 1)
        b1_copied = signal("b1_copied", 1)
        consts_made = signal("consts_made", 1)
        consts_ready = signal("consts_ready", 1)
        wT_ready = signal("wT_ready", 1)
        wT_drained = signal("wT_drained", 1)
        bo_ready = signal("bo_ready", 1)
        carried = signal("carried", 1)
        x_loaded = signal("x_loaded", 1, 16)
        xres_loaded = signal("xres_loaded", 1, 16)
        ctx_loaded = signal("ctx_loaded", 1, 16)
        experts_loaded = signal("experts_loaded", 2, 16)
        x2_stored = [signal(f"x2_stored{t}", 1, 16) for t in range(TPB)]
        UN = {"a": 2, "x": 4}
        sc_done = {u: signal(f"sc_done_{u}", n) for u, n in UN.items()}
        pT_done = {u: signal(f"pT_done_{u}", n) for u, n in UN.items()}
        pv_done = {u: signal(f"pv_done_{u}", n) for u, n in UN.items()}
        max_done = {u: signal(f"max_done_{u}", n) for u, n in UN.items()}
        sub_done = {u: signal(f"sub_done_{u}", n) for u, n in UN.items()}
        exp_done = {u: signal(f"exp_done_{u}", n) for u, n in UN.items()}
        sum_done = {u: signal(f"sum_done_{u}", n) for u, n in UN.items()}
        rec_done = {u: signal(f"rec_done_{u}", n) for u, n in UN.items()}
        pT_copied = {u: signal(f"pT_copied_{u}", n) for u, n in UN.items()}
        scaled = {u: signal(f"scaled_{u}", n) for u, n in UN.items()}
        o_taken = {u: signal(f"o_taken_{u}", n) for u, n in UN.items()}
        JN = {"xT": 2, "q": 2, "k": 1, "v": 2, "oa": 2, "x1T": 2, "ctxT": 1, "kx": 1, "qx": 2, "vx": 3, "ox": 2,
              "x2T": 2, "rt": 1, "rk": 1}
        computed = {j: signal(f"computed_{j}", n) for j, n in JN.items()}
        taken = {j: signal(f"taken_{j}", n) for j, n in JN.items()}
        kblk_made = signal("kblk_made", 1)
        kxblk_made = signal("kxblk_made", 1)
        x1r_made = signal("x1r_made", 1)
        stats_done = {n: signal(f"stats_done{n}", 2) for n in (1, 2)}
        mean_done = {n: signal(f"mean_done{n}", 2) for n in (1, 2)}
        eps_added = {n: signal(f"eps_added{n}", 2) for n in (1, 2)}
        rstd_done = {n: signal(f"rstd_done{n}", 2) for n in (1, 2)}
        ln_done = {n: signal(f"ln_done{n}", 2) for n in (1, 2)}
        STAGES = ("max", "less_max", "is_max", "weigh", "first", "count", "onehot", "count_tile", "gate_sum", "gate",
                  "pick", "place")
        routed = signal("routed", len(STAGES))
        gate_exp_done = signal("gate_exp_done", 1)
        place_taken = signal("place_taken", 1)
        token_stepped = signal("token_stepped", 1)
        entered = [signal(f"entered{t}", 1, 16) for t in range(TPB)]
        part1_signals = [routed, gate_exp_done, place_taken, token_stepped, x_loaded, xres_loaded, ctx_loaded, *x2_stored, kblk_made, kxblk_made, x1r_made]
        for group in (sc_done, pT_done, pv_done, max_done, sub_done, exp_done, sum_done, rec_done, pT_copied,
                      scaled, o_taken, computed, taken, stats_done, mean_done, eps_added, rstd_done, ln_done):
            part1_signals += group.values()
        dve2 = signal("dve2", 1)
        fill_made = signal("fill_made", 1)
        lists_filled = signal("lists_filled", 2, 16)
        total_done = signal("total_done", 1)
        plan_made = signal("plan_made", 2)
        plan_spread = signal("plan_spread", 1)
        plan_ready = signal("plan_ready", 1)
        f_names = ("idx_g_made", "idx_s_made", "xgT_done", "xgT_copied", "h_done", "h_copied", "hT_done", "gelu_done", "y_done",
                   "bias_added", "res_done", "st3_done", "mv3_done", "ve3_done", "rs3_done", "ln3_done")
        f = {n: signal(n, 1) for n in f_names}
        gathered = [signal(f"gathered{m}", 1, 16) for m in range(XR)]
        b2_loaded = [signal(f"b2_loaded{m}", 1, 16) for m in range(XR)]
        slots_loaded = [signal(f"slots_loaded{m}", 1, 16) for m in range(XR)]
        stored = [signal(f"stored{m}", 1, 16) for m in range(XR)]

        def wait_ring(eng, ring, g, m, behind=0):
            wait(eng, ring[(m - behind) % XR], g + (m - behind) // XR)

        def exists(b):
            return not isinstance(b, int) or 0 <= b < B

        MB = 3
        JOBS = [
            [("ctxT", 0, 2), ("ox", 0, 3), ("kx", 0, 2), ("x1T", 1, 2)],
            [("qx", 0, 2), ("vx", 0, 2), ("qx", 1, 2)],
            [("vx", 1, 2), ("vx", 2, 2), ("ox", 1, 3)],
            [("x2T", 0, 3), ("oa", 0, 1), ("xT", 0, 0), ("xT", 1, 0), ("rk", 0, 4)],
            [("v", 0, 0), ("oa", 1, 1), ("k", 0, 0), ("q", 1, 0), ("q", 0, 0)],
            [("x2T", 1, 3), ("v", 1, 0), ("x1T", 0, 1), ("rt", 0, 3)],
        ]
        PE_ORDER = [
            ("scores", "attend", "probT", "job"),
            ("attend", "scores", "probT"),
            ("attend", "probT", "scores"),
            ("attend", "probT", "scores"),
            ("attend", "probT", "scores"),
            ("attend", "probT", "scores"),
        ]
        ACT_ORDER = [
            ("take_o", "job", "probT", "exp", "job"),
            ("probT", "take_o", "job", "exp", "job"),
            ("probT", "take_o", "job", "exp", "job", "gate_exp"),
            ("probT", "take_o", "job", "exp", "job"),
            ("probT", "take_o", "job", "exp", "job"),
            ("probT", "take_o", "job", "job", "exp", "job"),
        ]
        DVE_ORDER = [
            ("denominator", "route", "softmax", "layernorm11", "route"),
            ("denominator", "softmax", "route", "layernorm20", "route"),
            ("route", "denominator", "softmax", "route"),
            ("denominator", "softmax", "route", "route"),
            ("denominator", "layernorm21", "route", "softmax", "layernorm10", "route"),
            ("denominator", "softmax", "route", "route"),
        ]
        POOL_ORDER = [
            ("rstd11", "scale"),
            ("rstd20", "kxblk", "scale"),
            ("scale",),
            ("scale", "x1r", "rstd21"),
            ("scale", "rstd10"),
            ("kblk", "scale", "enter"),
        ]
        FLAT = [j for step in JOBS for j in step]
        assert len(FLAT) % MB == 0
        UNITS = [("a", 0), ("a", 1), ("x", 0), ("x", 1), ("x", 2), ("x", 3)]
        LAG = {"a": 1, "x": 2}
        LAST_LAG = 4
        FIRST_FULL = LAST_LAG + 1

        def job_before(n, i):
            for back in range(MB, 4 * len(FLAT), MB):
                m, it = (n - back) % len(FLAT), i + (n - back) // len(FLAT)
                if exists(it - FLAT[m][2]):
                    return FLAT[m][0], FLAT[m][1], it - FLAT[m][2]
            return None

        def unit_at(n, i):
            it = i + n // 6
            kind, k = UNITS[n % 6]
            return kind, k, it - LAG[kind], (n % 6) % 2

        def unit_before(n, i, by):
            for back in range(by, 24, by):
                u = unit_at(n - back, i)
                if exists(u[2]):
                    return u[:3]
            return None

        def wait_for(eng, signals, event):
            if event is not None:
                wait(eng, signals[event[0]], event[2], event[1])

        def bank_of(n):
            return ps_m[:, n % MB, 0:256]

        def norm_of(what):
            return int(what[-2]), int(what[-1])

        def norm_batch(which, s, i):
            return i - (3 if which == 2 else 1 if s >= 3 else 2)

        def step_of(order, step, i, mine=lambda job: True):
            start = sum(len(s) for s in JOBS[:step])
            jobs = [(n, job, k, lag) for n, (job, k, lag) in enumerate(JOBS[step], start) if mine(job)]
            places = list(order) + ["job"] * (len(jobs) - order.count("job"))
            for what in places:
                if what != "job":
                    yield what, None
                elif jobs:
                    n, job, k, lag = jobs.pop(0)
                    if exists(i - lag):
                        yield what, (n, job, k, i - lag)

        block = top.enter_context(nc.Block())
        out_rows = out.rearrange("b s d -> (b s) d")

        def tail_of_part1(eng):
            for sig in part1_signals:
                wait(eng, sig, B - 1)

        N_LOADS = 7

        def for_tiles(eng, one, extra):
            first, last = 2 * XR, (NTILE - 2) // XR * XR
            for j in range(first):
                one(j, j // XR, j % XR)
            with eng.Fori(first // XR, last // XR) as g:
                for m in range(XR):
                    one(g * XR + m, g, m)
            for j in range(last, NTILE + extra):
                one(j, j // XR, j % XR)

        def loop_batches(eng, iteration, after_first):
            iteration(eng, 0)
            after_first()
            for i in range(1, FIRST_FULL):
                iteration(eng, i)
            with eng.Fori(FIRST_FULL, B) as i:
                iteration(eng, i)
            for i in range(B, B + LAST_LAG):
                iteration(eng, i)


        def settled(eng):
            eng.sem_inc(carried.sem, 1)

        def sp_iteration(sp, i):
            p, a, c, z = i, i - 1, i - 2, i - 3
            if exists(a):
                wait(sp, taken["oa"], a - 1, 1)
                sp.dma_start(xres[:], x_tiles(a)).then_inc(xres_loaded.sem, 16)
                wait(sp, computed["ctxT"], a - 1)
                sp.dma_start(ctx_s[0:K2, :], row_of(ctx_in, a)).then_inc(ctx_loaded.sem, 16)
            if exists(z):
                wait(sp, ln_done[2], z, 0)
                sp.dma_start(x2_tile(z, 0), x2s[:, 0, :]).then_inc(x2_stored[0].sem, 16)
                wait(sp, ln_done[2], z, 1)
                sp.dma_start(x2_tile(z, 1), x2s[:, 1, :]).then_inc(x2_stored[1].sem, 16)
            if not isinstance(i, int) or i < B - 1:
                wait(sp, computed["xT"], p)
                sp.dma_start(xs[:], x_tiles(p + 1)).then_inc(x_loaded.sem, 16)

        def row_of(t, b):
            if isinstance(b, int):
                return t[b]
            return t[bass.ds(b, 1)].rearrange("a s d -> (a s) d")

        def x_tiles(b):
            return row_of(x, b).rearrange("(t p) d -> p t d", p=P)

        def x2_tile(b, t):
            v = x2_dram.rearrange("(b t p) d -> b t p d", t=TPB, p=P)
            if isinstance(b, int):
                return v[b, t]
            return v[bass.ds(b, 1), t].rearrange("a p d -> (a p) d")

        def load_experts(sp, e):
            if isinstance(e, int):
                d1, d2, s1, s2 = w1s[:, e], w2s[:, e], w1[e], w2[e]
            else:
                d1 = w1s[:, bass.ds(e, 1)].rearrange("p a c f -> p (a c) f")
                d2 = w2s[:, bass.ds(e, 1)].rearrange("p a c f -> p (a c) f")
                s1 = w1[bass.ds(e, 1)].rearrange("a d f -> (a d) f")
                s2 = w2[bass.ds(e, 1)].rearrange("a d f -> (a d) f")
            sp.dma_start(d1, s1.rearrange("(c p) f -> p c f", p=P)).then_inc(experts_loaded.sem, 16)
            sp.dma_start(d2, s2.rearrange("(c p) d -> p c d", p=P)).then_inc(experts_loaded.sem, 16)

        @block.sync
        def _(sp):
            def load(dst, src):
                sp.dma_start(dst, src).then_inc(w_loaded.sem, 16)

            sp.dma_start(xs[:], x_tiles(0)).then_inc(x_loaded.sem, 16)
            for n, w in enumerate((wq, wk, wv, wo)):
                raw = w_raw[n // 2][:, n % 2, 0:KC * D].rearrange("p (c d) -> p c d", c=KC)
                sp.dma_start(raw, w.rearrange("(c p) d -> p c d", p=P)).then_inc(square_loaded.sem, 16)
            sp.dma_start(wqkv_s[:], w_qkv.rearrange("(c p) n -> p c n", p=P)).then_inc(qkv_loaded.sem, 16)
            load(wout_s[:], w_out.rearrange("(c p) n -> p c n", p=P))
            load(router_s[:, :, 0:E], router_w.rearrange("(c p) n -> p c n", p=P))
            for dst, src in ((bq_s, bq), (bk_s, bk), (bv_s, bv)):
                with nc.allow_non_contiguous_dma("a bias of 256 values, by partition"):
                    load(dst[:], src.rearrange("(c p) -> p c", p=P))
            load(bo_s[:], bo.rearrange("(a d) -> a d", a=1).to_broadcast([P, D]))
            load(oTa[0:E * FC, 0, 0:P], b1.rearrange("e (c p) -> (e c) p", p=P))
            sp.wait_ge(fill_made.sem, 1)
            flat_lists = lists.rearrange("(p r) c -> p (r c)", p=P)
            half = LIST_ROWS // P // 2 * 2
            sp.dma_start(flat_lists[:, 0:half], fill[:, 0:half]).then_inc(lists_filled.sem, 16)
            sp.dma_start(flat_lists[:, half:], fill[:, 0:2 * (LIST_ROWS // P) - half]).then_inc(lists_filled.sem, 16)
            early = E - (B - 1 - FIRST_FULL)
            for i in range(FIRST_FULL):
                sp_iteration(sp, i)
                if i < early:
                    load_experts(sp, i)
            with sp.Fori(FIRST_FULL, B - 1) as i:
                sp_iteration(sp, i)
                load_experts(sp, i - (FIRST_FULL - early))
            for i in range(B - 1, B + LAST_LAG):
                sp_iteration(sp, i)
            sp.wait_ge(plan_ready.sem, 1)
            for sig in entered:
                wait(sp, sig, B - 1)

            def slots_load(j, g, m):
                row = sp.value_load(row_i[0:1, j:j + 1] if isinstance(j, int) else row_i[0:1, bass.ds(j, 1)],
                                    min_val=0, max_val=LIST_ROWS - P)
                dst = slots[:, j] if isinstance(j, int) else slots[:, bass.ds(j, 1)].rearrange("p a c -> p (a c)")
                wait_ring(sp, slots_loaded, g, m, XR)
                with nc.allow_non_contiguous_dma("a token's number and weight"):
                    sp.dma_start(dst, lists[bass.ds(row, P), :]).then_inc(slots_loaded[m].sem, 16)

            def one(j, g, m):
                if not isinstance(j, int) or j + 2 < NTILE:
                    slots_load(j + 2, g + (m + 2) // XR, (m + 2) % XR)
                e = sp.value_load(e_i[0:1, j:j + 1] if isinstance(j, int) else e_i[0:1, bass.ds(j, 1)],
                                  min_val=0, max_val=E - 1)
                wait(sp, f["bias_added"], j - XR)
                src = b2[bass.ds(e, 1), :].to_broadcast([P, D])
                sp.dma_start(b2r[:, m, :], src).then_inc(b2_loaded[m].sem, 16)

            slots_load(0, 0, 0)
            slots_load(1, 0, 1)
            for_tiles(sp, one, 0)

        def transpose(dst, src):
            return nc.tensor.transpose(dst, src, ident[:])

        def pe_scores(pe, n, i):
            kind, k, b, par = unit_at(n, i)
            if not exists(b):
                return
            wait_for(pe, sub_done, unit_before(n, i, 1))
            if kind == "a":
                wait(pe, taken["q"], b)
                wait(pe, kblk_made, b)
                for h in range(KC):
                    last = nc.tensor.matmul(ps_s[:, h, :], qT[:, h, k * SEG:(k + 1) * SEG],
                                            kblk[:, h, k].rearrange("p h k -> p (h k)"), start=True, stop=True)
            else:
                wait(pe, taken["qx"], b)
                wait(pe, kxblk_made, b)
                t, h = k // 2, k % 2
                for q in range(2):
                    last = nc.tensor.matmul(ps_s[:, q, 0:4 * K2], qxT[:, h, t * P:(t + 1) * P],
                                            kxblk[:, h, 4 * q:4 * q + 4].rearrange("p h k -> p (h k)"),
                                            start=True, stop=True)
            last.then_inc(sc_done[kind].sem, 1)

        def pe_probT(pe, n, i):
            kind, k, b, par = unit_at(n, i)
            if not exists(b):
                return
            wait(pe, scaled[kind], b, k)
            wait_for(pe, pT_copied, unit_before(n, i, 1))
            width = H * KEYS if kind == "a" else HH * K2
            for c in range(-(-width // P)):
                cols = min(P, width - c * P)
                last = transpose(ps_t[0:cols, c // 4, (c % 4) * P:(c % 4) * P + P],
                                 prob[:, n % 3, c * P:c * P + cols])
            last.then_inc(pT_done[kind].sem, 1)

        def pe_attend(pe, n, i):
            kind, k, b, par = unit_at(n, i)
            if not exists(b):
                return
            wait_for(pe, o_taken, unit_before(n, i, 1))
            wait(pe, pT_copied[kind], b, k)
            if kind == "a":
                wait(pe, taken["v"], b)
                for pair in range(H // 2):
                    g, h = pair % 4, pair // 4
                    last = nc.tensor.matmul(ps_o[32 * g:32 * g + 32, h * P:(h + 1) * P],
                                            vA[:, k, 32 * pair:32 * pair + 32],
                                            probT[:, par, pair * P:(pair + 1) * P], start=True, stop=True)
            else:
                wait(pe, taken["vx"], b)
                h = k % 2
                for part in range(2):
                    for g in range(HH // 2):
                        c = 2 * g * K2 // P + part
                        rows = LASTROWS if c == CH - 1 else P
                        off = 32 * (g - G0[c])
                        last = nc.tensor.matmul(ps_o[32 * g:32 * g + 32, 0:P], vX[0:rows, c, h, off:off + 32],
                                                probT[0:rows, par, c * P:(c + 1) * P],
                                                start=(part == 0), stop=(part == 1))
            last.then_inc(pv_done[kind].sem, 1)

        def pe_job(pe, n, job, k, b, i):
            dst = bank_of(n)
            wait_for(pe, taken, job_before(n, i))

            def project(lhs, rhs, dst=dst, width=D):
                for c in range(KC):
                    last = nc.tensor.matmul(dst[:, 0:width], lhs(c), rhs(c), start=(c == 0), stop=(c == KC - 1))
                return last

            cols = slice(k * P, (k + 1) * P)
            if job == "xT":
                wait(pe, x_loaded, b)
                for c in range(KC):
                    last = transpose(dst[:, c * P:(c + 1) * P], xs[:, k, c * P:(c + 1) * P])
            elif job == "x1T":
                wait(pe, ln_done[1], b, k)
                for c in range(KC):
                    last = transpose(dst[:, c * P:(c + 1) * P], x1[:, k, c * P:(c + 1) * P])
            elif job == "x2T":
                wait(pe, ln_done[2], b, k)
                for c in range(KC):
                    last = transpose(dst[:, c * P:(c + 1) * P], x2s[:, k, c * P:(c + 1) * P])
            elif job == "ctxT":
                wait(pe, ctx_loaded, b)
                for c in range(KC):
                    last = nc.tensor.transpose(dst[:, c * P:c * P + K2], ctx_s[0:K2, c * P:(c + 1) * P],
                                               ident[0:K2, 0:K2])
            elif job == "q":
                wait(pe, taken["xT"], b)
                last = project(lambda c: wqkv_s[:, c, cols], lambda c: xT[:, c, :])
            elif job == "k":
                for h in range(KC):
                    last = project(lambda c: wqkv_s[:, c, D + h * P:D + (h + 1) * P],
                                   lambda c: xkT[:, c, :, 0, :], dst[:, h * P:], P)
            elif job == "v":
                wait(pe, taken["xT"], b)
                last = project(lambda c: xkT[:, c, k].rearrange("p w k -> p (w k)"),
                               lambda c: wqkv_s[:, c, 2 * D:3 * D])
            elif job == "oa":
                wait(pe, o_taken["a"], b, k)
                last = project(lambda c: oTa[:, c, cols], lambda c: wout_s[:, c, :])
            elif job == "qx":
                wait(pe, taken["x1T"], b)
                last = project(lambda c: wT[:, 0, c, cols], lambda c: x1T[:, c, :])
            elif job == "kx":
                wait(pe, taken["ctxT"], b)
                for h in range(KC):
                    last = project(lambda c: wT[:, 1, c, h * P:(h + 1) * P],
                                   lambda c: ctxT3[:, c].rearrange("p r k -> p (r k)")[:, 0:P], dst[:, h * P:], P)
            elif job == "vx":
                wait(pe, taken["ctxT"], b)
                for m, ch in enumerate(range(2 * k, min(2 * k + 2, CH))):
                    off = ch * P % K2
                    last = project(
                        lambda c: ctxT3[:, c].rearrange("p r k -> p (r k)")[:, off:off + P],
                        lambda c: wT[:, 2, c].rearrange("p (h j) -> p h j", h=KC)[:, :, 32 * G0[ch]:32 * G0[ch] + 64],
                        dst[:, m * P:], P)
            elif job == "ox":
                wait(pe, o_taken["x"], b, 2 * k + 1)
                last = project(lambda c: oTx[:, c, cols], lambda c: wT[:, 3, c, :])
            elif job == "rt":
                wait(pe, taken["x2T"], b)
                for t in range(TPB):
                    last = project(lambda c: x2T[:, c, t * P:(t + 1) * P], lambda c: router_s[:, c, :],
                                   dst[:, t * RW:], RW)
            elif job == "rk":
                wait(pe, routed, b, STAGES.index("count_tile"))
                nc.tensor.matmul(dst[:, 0:RW], tri[:], onehot[:], start=True, stop=False)
                last = nc.tensor.matmul(dst[:, 0:RW], ones[:], before[:], start=False, stop=True)
            last.then_inc(computed[job].sem, 1)

        def pe_iteration(pe, i):
            for s in range(6):
                for what, job in step_of(PE_ORDER[s], s, i):
                    if what == "scores":
                        pe_scores(pe, s, i)
                    elif what == "probT":
                        pe_probT(pe, s - 2, i)
                    elif what == "attend":
                        pe_attend(pe, s - 3, i)
                    else:
                        pe_job(pe, *job, i)

        @block.tensor
        def _(pe):
            pe.wait_ge(ident_made.sem, 1)
            wait(pe, square_loaded, 0)
            for n in range(4):
                raw = w_raw[n // 2][:, n % 2, 0:KC * D].rearrange("p (c d) -> p c d", c=KC)
                ps = (ps_s, ps_t)[n // 2][:, n % 2, :]
                for c in range(KC):
                    for r in range(KC):
                        last = transpose(ps[:, c * D + r * P:c * D + (r + 1) * P], raw[:, r, c * P:(c + 1) * P])
            last.then_inc(squares_done.sem, 1)
            wait(pe, qkv_loaded, 0)

            def biases():
                pe.wait_ge(w_loaded.sem, 16 * N_LOADS)
                nc.tensor.transpose(ps_o[:, 0:E * FC], oTa[0:E * FC, 0, 0:P],
                                    ident[0:E * FC, 0:E * FC]).then_inc(b1_done.sem, 1)
                pe.wait_ge(wT_drained.sem, 1)
                for c in range(KC):
                    last = nc.tensor.matmul(ps_s[:, 0, 0:D], bv_s[:, c:c + 1].to_broadcast([P, P]), wT[:, 3, c, :],
                                            start=(c == 0), stop=(c == KC - 1))
                last.then_inc(wT_ready.sem, 1)
                pe.wait_ge(consts_ready.sem, 1)
                pe.wait_ge(b1_copied.sem, 1)
                pe.wait_ge(bo_ready.sem, 1)

            loop_batches(pe, pe_iteration, biases)

            pe.wait_ge(dve2.sem, 2)
            nc.tensor.matmul(ps_s[:, 0, 0:RW], ones[:], before[:], start=True, stop=True).then_inc(total_done.sem, 1)
            pe.wait_ge(plan_made.sem, 2)
            for c in range(2):
                last = nc.tensor.matmul(ps_s[:, 1, c * RW:(c + 1) * RW], plan_f[:, c:c + 1].to_broadcast([P, P]),
                                        ident[:, 0:RW], start=True, stop=True)
            last.then_inc(plan_spread.sem, 1)
            pe.wait_ge(plan_ready.sem, 1)
            pe.wait_ge(experts_loaded.sem, 32 * E)

            def gathered_rows(j, g, m):
                wait_ring(pe, gathered, g, m)
                wait(pe, f["xgT_copied"], j - 2)
                for c in range(KC):
                    last = transpose(ps_x[m % 2][:, c * P:(c + 1) * P], xg[:, m, c * P:(c + 1) * P])
                last.then_inc(f["xgT_done"].sem, 1)

            def expert_of(j):
                return pe.value_load(e_i[0:1, j:j + 1] if isinstance(j, int) else e_i[0:1, bass.ds(j, 1)],
                                     min_val=0, max_val=E - 1)

            def one(j, g, m):
                if not isinstance(j, int) or 1 <= j <= NTILE:
                    e_before = expert_of(j - 1)
                if not isinstance(j, int) or j < NTILE:
                    e_now = expert_of(j)
                if not isinstance(j, int) or 1 <= j <= NTILE:
                    wait(pe, f["h_copied"], j - 1)
                    wait(pe, f["gelu_done"], j - 3)
                    for c in range(FC):
                        last = transpose(ps_t[:, (m - 1) % 2, c * P:(c + 1) * P],
                                         hs[:, (m - 1) % 2, c * P:(c + 1) * P])
                    last.then_inc(f["hT_done"].sem, 1)
                if not isinstance(j, int) or j < NTILE:
                    wait(pe, f["xgT_copied"], j)
                    wait(pe, f["h_copied"], j - 2)
                    for c in range(KC):
                        last = nc.tensor.matmul(ps_s[:, m % 2, :], xgT[:, m % 2, c * P:(c + 1) * P],
                                                w1s[:, bass.ds(e_now, 1), c, :].rearrange("p a f -> p (a f)"),
                                                start=(c == 0), stop=(c == KC - 1))
                    last.then_inc(f["h_done"].sem, 1)
                if not isinstance(j, int) or j + 1 < NTILE:
                    gathered_rows(j + 1, g + (m + 1) // XR, (m + 1) % XR)
                if not isinstance(j, int) or 1 <= j <= NTILE:
                    wait(pe, f["gelu_done"], j - 1)
                    wait(pe, f["bias_added"], j - 3)
                    for c in range(FC):
                        last = nc.tensor.matmul(ps_m[:, (m - 1) % 2, 0:D], hT[:, (m - 1) % 2, c, :],
                                                w2s[:, bass.ds(e_before, 1), c, :].rearrange("p a f -> p (a f)"),
                                                start=(c == 0), stop=(c == FC - 1))
                    last.then_inc(f["y_done"].sem, 1)

            gathered_rows(0, 0, 0)
            for_tiles(pe, one, 1)

        def act_probT(act, n, i):
            kind, k, b, par = unit_at(n, i)
            if not exists(b):
                return
            wait(act, pT_done[kind], b, k)
            wait_for(act, pv_done, unit_before(n, i, 2))
            if kind == "a":
                last = nc.scalar.copy(probT[:, par, :], ps_t[:].rearrange("p b n -> p (b n)"))
            else:
                nc.scalar.copy(probT[:, par, 0:512], ps_t[:, 0, :])
                last = nc.scalar.copy(probT[0:LASTROWS, par, 512:640], ps_t[0:LASTROWS, 1, 0:P])
            last.then_inc(pT_copied[kind].sem, 1)

        def act_take_o(act, n, i):
            kind, k, b, par = unit_at(n, i)
            if not exists(b):
                return
            wait(act, pv_done[kind], b, k)
            if kind == "a":
                wait(act, computed["oa"], b - 1, k)
                last = nc.scalar.copy(oTa[:, :, k * SEG:(k + 1) * SEG],
                                      ps_o[:, 0:256].rearrange("p (c n) -> p c n", c=KC))
            else:
                t, h = k // 2, k % 2
                wait(act, computed["ox"], b - 1, t)
                last = nc.scalar.copy(oTx[:, h, t * P:(t + 1) * P], ps_o[:, 0:P])
            last.then_inc(o_taken[kind].sem, 1)

        def act_exp(act, n, i):
            kind, k, b, par = unit_at(n, i)
            if not exists(b):
                return
            width = H * KEYS if kind == "a" else HH * K2
            wait(act, sub_done[kind], b, k)
            nc.scalar.activation(prob[:, n % 3, 0:width], prob[:, n % 3, 0:width], ACT.Exp,
                                 scale=SCALE).then_inc(exp_done[kind].sem, 1)

        def act_take(act, n, job, k, b):
            src = bank_of(n)
            wait(act, computed[job], b, k)
            pair = src.rearrange("p (c n) -> p c n", c=KC)
            cols = slice(k * P, (k + 1) * P)
            if job == "xT":
                wait(act, computed["q"], b - 1)
                wait(act, computed["v"], b - 1)
                nc.scalar.copy(xT[:, :, cols], pair)
                grid = pair.rearrange("p c (r o k e) -> p c r o k e", o=2, k=8, e=2)
                dst = xkT[:, :, k].rearrange("p c w (r o k) -> p c w r o k", o=2, k=8)
                for o in range(2):
                    for c in range(KC):
                        keys = grid[:, c, None, :, o, :, o].to_broadcast([P, 2, SEG // 32, 8])
                        last = nc.scalar.copy(dst[:, c, :, :, o, :], keys)
            elif job == "q":
                wait(act, sc_done["a"], b - 1)
                last = nc.scalar.copy(qT[:, k, :], src)
            elif job == "k":
                wait(act, kblk_made, b - 1)
                last = nc.scalar.copy(kT[:].rearrange("p c s k -> p (c s k)"), src)
            elif job == "v":
                wait(act, pv_done["a"], b - 1)
                dst = vA[:, k, :].rearrange("p (g o d) -> p g o d", o=2, d=DH)
                s4 = src.rearrange("p (g o d) -> p g o d", o=2, d=DH)
                for o in range(2):
                    rows = slice(o * KEYS, (o + 1) * KEYS)
                    last = nc.scalar.copy(dst[rows, :, o, :], s4[rows, :, o, :])
            elif job == "x1T":
                wait(act, computed["qx"], b - 1)
                last = nc.scalar.copy(x1T[:, :, cols], pair)
            elif job == "ctxT":
                wait(act, computed["kx"], b - 1)
                wait(act, computed["vx"], b - 1)
                for c in range(KC):
                    last = nc.scalar.copy(ctxT3[:, c], pair[:, c, None, 0:K2].to_broadcast([P, 3, K2]))
            elif job == "kx":
                wait(act, kxblk_made, b - 1)
                for c in range(KC):
                    last = nc.scalar.activation(kxT[:, c, :], pair[:, c, 0:K2], ACT.Identity, bias=bk_s[:, c:c + 1])
            elif job == "qx":
                wait(act, sc_done["x"], b - 1)
                last = nc.scalar.activation(qxT[:, k, :], src, ACT.Identity, bias=bq_s[:, k:k + 1])
            elif job == "x2T":
                wait(act, computed["rt"], b - 1)
                last = nc.scalar.copy(x2T[:, :, cols], pair)
            elif job == "rt":
                wait(act, routed, b - 1, STAGES.index("is_max"))
                last = nc.scalar.copy(logits[:], src[:, 0:TPB * RW].rearrange("p (t e) -> p t e", t=TPB)[:, :, 0:E])
            last.then_inc(taken[job].sem, 1)

        BY_DVE = ("oa", "ox", "vx", "rk")

        def act_gate_exp(act, b):
            if not exists(b):
                return
            wait(act, routed, b, STAGES.index("less_max"))
            wait(act, routed, b - 1, STAGES.index("gate_sum"))
            nc.scalar.activation(lexp[:].rearrange("p t e -> p (t e)"), ldif[:].rearrange("p t e -> p (t e)"),
                                 ACT.Exp).then_inc(gate_exp_done.sem, 1)

        def act_iteration(act, i):
            for s in range(6):
                for what, job in step_of(ACT_ORDER[s], s, i, lambda j: j not in BY_DVE):
                    if what == "probT":
                        act_probT(act, s - 2, i)
                    elif what == "take_o":
                        act_take_o(act, s - 3, i)
                    elif what == "exp":
                        act_exp(act, s, i)
                    elif what == "gate_exp":
                        act_gate_exp(act, i - 4)
                    else:
                        act_take(act, *job)

        @block.scalar
        def _(act):
            act.wait_ge(squares_done.sem, 1)
            for n in range(4):
                ps = (ps_s, ps_t)[n // 2][:, n % 2, :]
                last = nc.scalar.copy(wT[:, n].rearrange("p c d -> p (c d)"), ps)
            last.then_inc(wT_drained.sem, 1)
            act.wait_ge(dve2.sem, 1)

            def biases():
                act.wait_ge(b1_done.sem, 1)
                nc.scalar.copy(b1t[:], ps_o[:, 0:E * FC]).then_inc(b1_copied.sem, 1)
                act.wait_ge(consts_ready.sem, 1)
                wait(act, lists_filled, 0)

            loop_batches(act, act_iteration, biases)
            act.wait_ge(plan_ready.sem, 1)

            def rows_copy(j, m):
                wait(act, f["xgT_done"], j)
                wait(act, f["h_done"], j - 2)
                nc.scalar.copy(xgT[:, m % 2, :], ps_x[m % 2][:, 0:D]).then_inc(f["xgT_copied"].sem, 1)

            def one(j, g, m):
                if not isinstance(j, int) or 1 <= j <= NTILE:
                    e = act.value_load(e_i[0:1, j - 1:j] if isinstance(j, int) else e_i[0:1, bass.ds(j - 1, 1)],
                                       min_val=0, max_val=E - 1)
                    wait(act, f["hT_done"], j - 1)
                    wait(act, f["y_done"], j - 3)
                    for c in range(FC):
                        last = nc.scalar.activation(hT[:, (m - 1) % 2, c, :],
                                                    ps_t[:, (m - 1) % 2, c * P:(c + 1) * P], ACT.Gelu,
                                                    bias=b1t[:, bass.ds(e * FC + c, 1)])
                    last.then_inc(f["gelu_done"].sem, 1)
                if not isinstance(j, int) or j + 1 < NTILE:
                    rows_copy(j + 1, m + 1)

            rows_copy(0, 0)
            for_tiles(act, one, 1)

        def unit_views(kind, par, third):
            if kind == "a":
                return (ps_s[:].rearrange("p b (h k) -> p (b h) k", k=KEYS),
                        prob[:, third, :].rearrange("p (h k) -> p h k", k=KEYS), H, mx[:, par, :],
                        mx[:, par, :, None].to_broadcast([P, H, KEYS]))
            return (ps_s[:, :, 0:4 * K2].rearrange("p b (h k) -> p b h k", k=K2),
                    prob[:, third, 0:HH * K2].rearrange("p (b h k) -> p b h k", b=2, k=K2), HH,
                    mx[:, par, 0:HH].rearrange("p (b h) -> p b h", b=2),
                    mx[:, par, 0:HH].rearrange("p (b h) -> p b h", b=2)[:, :, :, None].to_broadcast([P, 2, 4, K2]))

        def dve_softmax(dve, n, i):
            kind, k, b, par = unit_at(n, i)
            if not exists(b):
                return
            s, p, _, m, mb = unit_views(kind, par, n % 3)
            wait(dve, sc_done[kind], b, k)
            nc.vector.tensor_reduce(m, s, axis=AX, op=ALU.max).then_inc(max_done[kind].sem, 1)
            wait(dve, max_done[kind], b, k)
            wait_for(dve, pT_done, unit_before(n, i, 3))
            nc.vector.tensor_tensor(p, s, mb, ALU.subtract).then_inc(sub_done[kind].sem, 1)

        def dve_denominator(dve, n, i):
            kind, k, b, par = unit_at(n, i)
            if not exists(b):
                return
            heads, width = (H, KEYS) if kind == "a" else (HH, K2)
            wait(dve, exp_done[kind], b, k)
            nc.vector.tensor_reduce(den[:, par, 0:heads],
                                    prob[:, n % 3, 0:heads * width].rearrange("p (h k) -> p h k", k=width),
                                    axis=AX, op=ALU.add).then_inc(sum_done[kind].sem, 1)
            wait(dve, sum_done[kind], b, k)
            wait_for(dve, scaled, unit_before(n, i, 2))
            nc.vector.reciprocal(rden[:, par, 0:heads], den[:, par, 0:heads]).then_inc(rec_done[kind].sem, 1)

        def dve_take(dve, n, job, k, b):
            src = bank_of(n)
            wait(dve, computed[job], b, k)
            if job == "vx":
                wait(dve, pv_done["x"], b - 1)
                chunks = slice(2 * k, min(2 * k + 2, CH))
                m = chunks.stop - chunks.start
                nc.vector.tensor_tensor(vX[:, chunks], src[:, 0:m * P].rearrange("p (c h j) -> p c h j", c=m, h=KC),
                                        vmask[:, chunks, None, :].to_broadcast([P, m, KC, 64]),
                                        ALU.mult).then_inc(taken[job].sem, 1)
                return
            if job == "rk":
                nc.vector.tensor_copy(rank[:], src[:, 0:TPB * E].rearrange("p (t e) -> p t e", t=TPB)).then_inc(
                    taken[job].sem, 1)
                return
            which = 1 if job == "oa" else 2
            s = sums(which, k)
            q = 2 * (which - 1) + k
            if job == "oa":
                wait(dve, xres_loaded, b)
                add = xres[:, k, :]
            else:
                wait(dve, x1r_made, b)
                add = x1r[:, k, :]
            nc.vector.tensor_tensor(s[:], src, add, ALU.add).then_inc(taken[job].sem, 1)
            wait(dve, taken[job], b, k)
            nc.vector.bn_stats(st[:, q, :], s[:]).then_inc(stats_done[which].sem, 1)
            wait(dve, stats_done[which], b, k)
            wait(dve, eps_added[which], b - 1, k)
            settled(dve)
            nc.vector.bn_aggr(mv[:, q, :], st[:, q, :]).then_inc(mean_done[which].sem, 1)

        def sums(which, k):
            return ((sum1, sum1b), (sum2, sum2b))[which - 1][k]

        def dve_layernorm(dve, which, k, b):
            if not exists(b):
                return
            q = 2 * (which - 1) + k
            wait(dve, rstd_done[which], b, k)
            if which == 1:
                wait(dve, computed["x1T"], b - 1, 1)
                wait(dve, x1r_made, b - 1)
                dst = x1
            else:
                wait(dve, computed["x2T"], b - 1, k)
                wait(dve, x2_stored[k], b - 1)
                dst = x2s
            nc.vector.tensor_scalar(dst[:, k, :], sums(which, k)[:], mv[:, q, 0:1], rstd[:, q:q + 1],
                                    ALU.subtract, ALU.mult).then_inc(ln_done[which].sem, 1)

        def dve_route(dve, stage, b):
            if not exists(b):
                return
            n = STAGES.index(stage)
            if n == 0:
                wait(dve, taken["rt"], b)
                wait(dve, routed, b - 1)
            else:
                wait(dve, routed, b, n - 1)
            rows = rev[:, None, :].to_broadcast([P, TPB, E])
            hot = onehot[:, 0:TPB * E].rearrange("p (t e) -> p t e", t=TPB)
            if stage == "max":
                last = nc.vector.tensor_reduce(lmax[:], logits[:], axis=AX, op=ALU.max)
            elif stage == "less_max":
                wait(dve, gate_exp_done, b - 1)
                last = nc.vector.tensor_tensor(ldif[:], logits[:], lmax[:, :, None].to_broadcast([P, TPB, E]),
                                               ALU.subtract)
            elif stage == "is_max":
                last = nc.vector.tensor_tensor(ismax[:], logits[:], lmax[:, :, None].to_broadcast([P, TPB, E]),
                                               ALU.is_equal)
            elif stage == "weigh":
                last = nc.vector.tensor_tensor(ismax[:], ismax[:], rows, ALU.mult)
            elif stage == "first":
                last = nc.vector.tensor_reduce(best[:], ismax[:], axis=AX, op=ALU.max)
            elif stage == "count":
                last = nc.vector.tensor_tensor(before[:, 0:E], before[:, E:2 * E], onehot[:, E:2 * E], ALU.add)
            elif stage == "onehot":
                last = nc.vector.tensor_tensor(hot, rows, best[:, :, None].to_broadcast([P, TPB, E]), ALU.is_equal)
            elif stage == "count_tile":
                last = nc.vector.tensor_tensor(before[:, E:2 * E], before[:, 0:E], onehot[:, 0:E], ALU.add)
            elif stage == "gate_sum":
                wait(dve, gate_exp_done, b)
                last = nc.vector.tensor_reduce(lsum[:], lexp[:], axis=AX, op=ALU.add)
            elif stage == "gate":
                for t in range(TPB):
                    wait(dve, entered[t], b - 1)
                last = nc.vector.reciprocal(member[:, :, 1], lsum[:])
            elif stage == "pick":
                wait(dve, taken["rk"], b)
                last = nc.vector.tensor_tensor(rank[:], rank[:], hot, ALU.mult)
            elif stage == "place":
                wait(dve, place_taken, b - 1)
                last = nc.vector.tensor_reduce(place[:], rank[:], axis=AX, op=ALU.add)
            last.then_inc(routed.sem, 1)

        def dve_iteration(dve, i):
            stages = iter(STAGES)
            for s in range(6):
                for what, job in step_of(DVE_ORDER[s], s, i, lambda j: j in BY_DVE):
                    if what == "route":
                        dve_route(dve, next(stages), i - 4)
                    elif what == "denominator":
                        dve_denominator(dve, s - 1, i)
                    elif what == "softmax":
                        dve_softmax(dve, s, i)
                    elif what.startswith("layernorm"):
                        which, k = norm_of(what)
                        dve_layernorm(dve, which, k, norm_batch(which, s, i))
                    else:
                        dve_take(dve, *job)

        @block.vector
        def _(dve):
            nc.vector.memset(vA[:].rearrange("p s d -> p (s d)"), 0.0)
            nc.vector.memset(router_s[:, :, E:], 0.0)
            nc.vector.memset(onehot[:], 0.0)
            nc.vector.memset(batch_step[:], float(S))
            nc.vector.memset(eps[:], EPS)
            nc.vector.memset(neg_half[:], -0.5).then_inc(dve2.sem, 1)

            def biases():
                dve.wait_ge(wT_ready.sem, 1)
                dve.wait_ge(w_loaded.sem, 16 * N_LOADS)
                nc.vector.tensor_tensor(bo_s[:], ps_s[:, 0, 0:D], bo_s[:], ALU.add).then_inc(bo_ready.sem, 1)
                dve.wait_ge(consts_ready.sem, 1)

            loop_batches(dve, dve_iteration, biases)

            chain = [1]

            def link(ins):
                chain[0] += 1
                ins.then_inc(dve2.sem, 1)
                dve.wait_ge(dve2.sem, chain[0])

            wait(dve, routed, B - 1)
            link(nc.vector.tensor_tensor(before[:, 0:E], before[:, E:2 * E], onehot[:, E:2 * E], ALU.add))
            tail_of_part1(dve)
            nc.vector.memset(zeros[:], 0.0)
            nc.vector.memset(xg[:].rearrange("p m d -> p (m d)"), 0.0)
            dve.wait_ge(total_done.sem, 1)
            link(nc.vector.tensor_tensor(n_e[:], ps_s[:, 0, 0:E], round_up[:], ALU.add))
            link(nc.vector.tensor_copy(t_i[:], n_e[:]))
            link(nc.vector.tensor_scalar(t_i[:], t_i[:], 7, None, ALU.logical_shift_right))
            link(nc.vector.tensor_copy(t_e[:], t_i[:]))
            link(nc.vector.tensor_tensor_scan(tb_e[:], zeros[:], t_e[:], 0.0, ALU.add, ALU.add))
            link(nc.vector.tensor_scalar(ended[:], tb_e[:], tile_no[:], None, ALU.is_le))
            link(nc.vector.scalar_tensor_tensor(ended_t[:], tb_e[:], tile_no[:], t_e[:], ALU.is_le, ALU.mult))
            link(nc.vector.tensor_reduce(e_f[:], ended[:], axis=AX, op=ALU.add))
            link(nc.vector.tensor_reduce(start_f[:], ended_t[:], axis=AX, op=ALU.add))
            link(nc.vector.tensor_tensor(start_f[:], tile_no[:], start_f[:], ALU.subtract))
            link(nc.vector.scalar_tensor_tensor(start_f[:], e_f[:], float(LIST // P), start_f[:], ALU.mult, ALU.add))
            nc.vector.tensor_scalar(plan_f[:, 1:2], e_f[:], float(E - 1), None, ALU.min).then_inc(plan_made.sem, 1)
            nc.vector.tensor_scalar(plan_f[:, 0:1], start_f[:], float(P), None, ALU.mult).then_inc(plan_made.sem, 1)
            dve.wait_ge(plan_spread.sem, 1)
            nc.vector.tensor_copy(plan_i[:], ps_s[:, 1, 0:2 * RW].rearrange("p (c j) -> p c j", c=2)[:, :, 0:NTILE]).then_inc(
                plan_ready.sem, 1)
            dve.wait_ge(plan_ready.sem, 1)

            def one(j, g, m):
                if not isinstance(j, int) or 2 <= j <= NTILE + 1:
                    q, r = (m - 2) % 2, (m - 2) % XR
                    wait(dve, f["y_done"], j - 2)
                    wait_ring(dve, b2_loaded, g, m, 2)
                    nc.vector.tensor_tensor(yb[:, q, :], ps_m[:, q, 0:D], b2r[:, r, :], ALU.add).then_inc(
                        f["bias_added"].sem, 1)
                    wait(dve, f["bias_added"], j - 2)
                    gates = (slots[:, j - 2, 1:2] if isinstance(j, int)
                             else slots[:, bass.ds(j - 2, 1), 1:2].rearrange("p a c -> p (a c)"))
                    nc.vector.scalar_tensor_tensor(ys[:, q, :], yb[:, q, :], gates, xg[:, r, :], ALU.mult,
                                                   ALU.add).then_inc(f["res_done"].sem, 1)
                    wait(dve, f["res_done"], j - 2)
                    nc.vector.bn_stats(st3[:, q, :], ys[:, q, :]).then_inc(f["st3_done"].sem, 1)
                    wait(dve, f["st3_done"], j - 2)
                    settled(dve)
                    nc.vector.bn_aggr(mv3[:, q, :], st3[:, q, :]).then_inc(f["mv3_done"].sem, 1)
                if not isinstance(j, int) or j < NTILE:
                    wait(dve, f["h_done"], j)
                    wait(dve, f["hT_done"], j - 2)
                    nc.vector.tensor_copy(hs[:, m % 2, :], ps_s[:, m % 2, :]).then_inc(f["h_copied"].sem, 1)
                if not isinstance(j, int) or 2 <= j <= NTILE + 1:
                    q, r = (m - 2) % 2, (m - 2) % XR
                    wait(dve, f["rs3_done"], j - 2)
                    wait_ring(dve, stored, g, m, 2 + XR)
                    nc.vector.tensor_scalar(yo[:, r, :], ys[:, q, :], mv3[:, q, 0:1], rs3[:, q:q + 1],
                                            ALU.subtract, ALU.mult).then_inc(f["ln3_done"].sem, 1)

            for_tiles(dve, one, 3)

        def pool_rstd(pool, which, k, b):
            if not exists(b):
                return
            q = 2 * (which - 1) + k
            wait(pool, mean_done[which], b, k)
            wait(pool, ln_done[which], b - 1, k)
            nc.gpsimd.tensor_tensor(ve[:, q:q + 1], mv[:, q, 1:2], eps[:], ALU.add).then_inc(eps_added[which].sem, 1)
            wait(pool, eps_added[which], b, k)
            nc.gpsimd.tensor_tensor(rstd[:, q:q + 1], ve[:, q:q + 1], neg_half[:], ALU.pow).then_inc(
                rstd_done[which].sem, 1)

        def pool_scale(pool, n, i):
            kind, k, b, par = unit_at(n, i)
            if not exists(b):
                return
            heads, width = (H, KEYS) if kind == "a" else (HH, K2)
            wait(pool, rec_done[kind], b, k)
            p = prob[:, n % 3, 0:heads * width].rearrange("p (h k) -> p h k", k=width)
            nc.gpsimd.tensor_tensor(p, p, rden[:, par, 0:heads, None].to_broadcast([P, heads, width]),
                                    ALU.mult).then_inc(scaled[kind].sem, 1)

        def pool_kxblk(pool, b):
            if not exists(b):
                return
            wait(pool, taken["kx"], b)
            wait(pool, sc_done["x"], b - 1)
            for h in range(KC):
                last = nc.gpsimd.tensor_tensor(kxblk[:, h], kxT[:, h, None, :].to_broadcast([P, HH, K2]),
                                               kmask[:, :, None].to_broadcast([P, HH, K2]), ALU.mult)
            last.then_inc(kxblk_made.sem, 1)

        def pool_x1r(pool, b):
            if not exists(b):
                return
            wait(pool, ln_done[1], b)
            wait(pool, taken["ox"], b - 1)
            nc.gpsimd.tensor_tensor(x1r[:], x1[:], bo_s[:, None, :].to_broadcast([P, TPB, D]),
                                    ALU.add).then_inc(x1r_made.sem, 1)

        def pool_kblk(pool, b):
            if not exists(b):
                return
            wait(pool, taken["k"], b)
            wait(pool, sc_done["a"], b - 1)
            for h in range(KC):
                last = nc.gpsimd.tensor_tensor(
                    kblk[:, h], kT[:, h, :, None, :].to_broadcast([P, NSEG, HH, KEYS]),
                    kmask[:, None, :, None].to_broadcast([P, NSEG, HH, KEYS]), ALU.mult)
            last.then_inc(kblk_made.sem, 1)

        def pool_iteration(pool, i):
            for s in range(6):
                for what in POOL_ORDER[s]:
                    if what == "scale":
                        pool_scale(pool, s - 1, i)
                    elif what == "kxblk":
                        pool_kxblk(pool, i - 2)
                    elif what == "x1r":
                        pool_x1r(pool, i - 2)
                    elif what == "kblk":
                        pool_kblk(pool, i)
                    elif what == "enter":
                        pool_enter(pool, i - 4)
                    else:
                        which, k = norm_of(what)
                        pool_rstd(pool, which, k, norm_batch(which, s, i))

        def pool_enter(pool, b):
            if not exists(b):
                return
            wait(pool, routed, b)
            for t in range(TPB):
                wait(pool, entered[t], b - 1)
            settled(pool)
            nc.gpsimd.tensor_copy(place_i[:], place[:]).then_inc(place_taken.sem, 1)
            nc.gpsimd.tensor_tensor(member[:, :, 0], member[:, :, 0], batch_step[:], ALU.add).then_inc(
                token_stepped.sem, 1)
            for t in range(TPB):
                wait(pool, place_taken, b)
                wait(pool, token_stepped, b)
                settled(pool)
                nc.gpsimd.indirect_dma_start(lists, bass.IndirectOffsetOnAxis(ap=place_i[:, t:t + 1], axis=0),
                                             member[:, t, :], None, bounds_check=LIST_ROWS - 1,
                                             oob_is_err=False).then_inc(entered[t].sem, 16)

        @block.gpsimd
        def _(pool):
            made = [0]

            def link(ins):
                made[0] += 1
                ins.then_inc(consts_made.sem, 1)
                pool.wait_ge(consts_made.sem, made[0])

            g = nc.gpsimd
            link(g.memset(ident[:], 0.0))
            link(g.affine_select(out=ident[:], in_=ident[:], compare_op=ALU.not_equal, fill=1.0, base=0,
                                 pattern=[[-1, P]], channel_multiplier=1))
            pool.sem_inc(ident_made.sem, 1)
            pairs = fill.rearrange("p (r c) -> p r c", c=2)
            link(g.memset(pairs[:, :, 0], float(B * S)))
            g.memset(pairs[:, :, 1], 0.0).then_inc(fill_made.sem, 1)
            link(g.memset(ones[:], 1.0))
            link(g.memset(kmask[:], 1.0))
            link(g.memset(vmask[:].rearrange("p c j -> p (c j)"), 1.0))
            link(g.affine_select(out=kmask[:], in_=kmask[:], compare_op=ALU.is_ge, fill=0.0, base=0,
                                 pattern=[[-DH, HH]], channel_multiplier=1))
            link(g.affine_select(out=kmask[:], in_=kmask[:], compare_op=ALU.is_ge, fill=0.0, base=DH - 1,
                                 pattern=[[DH, HH]], channel_multiplier=-1))
            for c in range(CH):
                v = vmask[:, c, :].rearrange("p (h d) -> p h d", d=DH)
                off = c * P - 2 * G0[c] * K2
                link(g.affine_select(out=v, in_=v, compare_op=ALU.is_ge, fill=0.0, base=off,
                                     pattern=[[-K2, 4], [0, DH]], channel_multiplier=1))
                link(g.affine_select(out=v, in_=v, compare_op=ALU.is_ge, fill=0.0, base=K2 - 1 - off,
                                     pattern=[[K2, 4], [0, DH]], channel_multiplier=-1))
            link(g.memset(tri[:], 1.0))
            link(g.affine_select(out=tri[:], in_=tri[:], compare_op=ALU.is_gt, fill=0.0, base=0, pattern=[[1, P]],
                                 channel_multiplier=-1))
            link(g.iota(rev[:], pattern=[[-1, E]], base=E, channel_multiplier=0, allow_small_or_imprecise_dtypes=True))
            link(g.iota(member[:, :, 0], pattern=[[P, TPB]], base=-S, channel_multiplier=1,
                        allow_small_or_imprecise_dtypes=True))
            link(g.iota(tile_no[:], pattern=[[0, 1]], base=0, channel_multiplier=1,
                        allow_small_or_imprecise_dtypes=True))
            link(g.memset(before[:], 0.0))
            link(g.iota(before[0:1, E:2 * E], pattern=[[LIST, E]], base=0, channel_multiplier=0,
                        allow_small_or_imprecise_dtypes=True))
            link(g.iota(round_up[:], pattern=[[-LIST, E]], base=P - 1, channel_multiplier=0,
                        allow_small_or_imprecise_dtypes=True))
            pool.wait_ge(dve2.sem, 1)
            g.memset(ve[:], 0.0).then_inc(consts_ready.sem, 1)

            def biases():
                pool.wait_ge(bo_ready.sem, 1)
                wait(pool, lists_filled, 0)

            loop_batches(pool, pool_iteration, biases)

            tail_of_part1(pool)
            pool.wait_ge(plan_ready.sem, 1)
            for t in range(TPB):
                pool.wait_ge(x2_stored[t].sem, 16 * B)

            def token(j):
                return slots[:, j, 0:1] if isinstance(j, int) else slots[:, bass.ds(j, 1), 0:1].rearrange("p a c -> p (a c)")

            def gather(j, g, m):
                wait(pool, f["res_done"], j - XR)
                wait(pool, f["xgT_done"], j - XR)
                wait_ring(pool, gathered, g, m, XR)
                wait_ring(pool, slots_loaded, g, m)
                settled(pool)
                nc.gpsimd.tensor_copy(idx_g[:, m:m + 1], token(j)).then_inc(f["idx_g_made"].sem, 1)
                wait(pool, f["idx_g_made"], j)
                settled(pool)
                nc.gpsimd.indirect_dma_start(xg[:, m, :], None, x2_dram,
                                             bass.IndirectOffsetOnAxis(ap=idx_g[:, m:m + 1], axis=0),
                                             bounds_check=B * S - 1, oob_is_err=False).then_inc(gathered[m].sem, 16)

            def one(j, g, m):
                if not isinstance(j, int) or j >= 3:
                    r = (m - 3) % XR
                    wait_ring(pool, stored, g, m, 3 + XR)
                    nc.gpsimd.tensor_copy(idx_s[:, r:r + 1], token(j - 3)).then_inc(f["idx_s_made"].sem, 1)
                    wait(pool, f["ln3_done"], j - 3)
                    wait(pool, f["idx_s_made"], j - 3)
                    settled(pool)
                    nc.gpsimd.indirect_dma_start(out_rows, bass.IndirectOffsetOnAxis(ap=idx_s[:, r:r + 1], axis=0),
                                                 yo[:, r, :], None, bounds_check=B * S - 1,
                                                 oob_is_err=False).then_inc(stored[r].sem, 16)
                if not isinstance(j, int) or 2 <= j <= NTILE + 1:
                    q = (m - 2) % 2
                    wait(pool, f["mv3_done"], j - 2)
                    wait(pool, f["ln3_done"], j - 4)
                    nc.gpsimd.tensor_tensor(ve3[:, q:q + 1], mv3[:, q, 1:2], eps[:], ALU.add).then_inc(f["ve3_done"].sem, 1)
                    wait(pool, f["ve3_done"], j - 2)
                    nc.gpsimd.tensor_tensor(rs3[:, q:q + 1], ve3[:, q:q + 1], neg_half[:], ALU.pow).then_inc(
                        f["rs3_done"].sem, 1)
                if not isinstance(j, int) or j + 2 < NTILE:
                    gather(j + 2, g + (m + 2) // XR, (m + 2) % XR)

            gather(0, 0, 0)
            gather(1, 0, 1)
            for_tiles(pool, one, 3)
            for j in range(NTILE - XR, NTILE):
                wait_ring(pool, stored, j // XR, j % XR)



_INS = ["x", "ctx_1024", "L0_attn_W_qkv", "L0_attn_W_out", "L0_xattn_Wq", "L0_xattn_bq", "L0_xattn_Wk",
        "L0_xattn_bk", "L0_xattn_Wv", "L0_xattn_bv", "L0_xattn_Wo", "L0_xattn_bo", "L0_ffn_router_w", "L0_ffn_w1",
        "L0_ffn_b1", "L0_ffn_w2", "L0_ffn_b2"]


def kernel(**inputs):
    import concourse.bacc as bacc
    from concourse.bass_utils import run_bass_kernel_spmd

    nc = bacc.Bacc("TRN2", target_bir_lowering=False, num_devices=1)
    arrays, args = {}, []
    for name in _INS:
        a = np.ascontiguousarray(inputs[name])
        arrays[f"in_{name}"] = a
        args.append(nc.dram_tensor(f"in_{name}", a.shape, mybir.dt.from_np(a.dtype), kind="ExternalInput").ap())
    shape = inputs["x"].shape
    args.append(nc.dram_tensor("out", shape, mybir.dt.float32, kind="ExternalOutput").ap())
    decoder_layer(nc, *args)
    r = run_bass_kernel_spmd(nc, [arrays], core_ids=[0])
    return r.results[0]["out"]
```

```python
from contextlib import ExitStack

import concourse.bass as bass
import numpy as np
from concourse import mybir

P = 128
F32 = mybir.dt.float32
U32 = mybir.dt.uint32
I32 = mybir.dt.int32
ALU = mybir.AluOpType
ACT = mybir.ActivationFunctionType
AX = mybir.AxisListType.X
EPS = 1e-5


class Signal:

    def __init__(self, sem, per, unit=1):
        self.sem, self.per, self.unit = sem, per, unit

    def at(self, b, k=None):
        k = self.per - 1 if k is None else k
        return (b * self.per + (k + 1)) * self.unit


def wait(eng, sig, b, k=None):
    if isinstance(b, int) and b < 0:
        return
    eng.wait_ge(sig.sem, sig.at(b, k))


def decoder_layer(nc, x, ctx_in, w_qkv, w_out, wq, bq, wk, bk, wv, bv, wo, bo, router_w, w1, b1, w2, b2, out):
    B, S, D = x.shape
    K2 = ctx_in.shape[1]
    E, _, F = w1.shape
    H = 16
    DH = D // H
    SEG = 128
    NSEG = S // SEG
    KEYS = SEG // 2
    KC = D // P
    FC = F // P
    HH = H // KC
    NT = B * S // P
    TPB = S // P
    NTILE = NT + E - 1
    LIST = B * S
    LIST_ROWS = E * LIST + (E - 1) * P
    RW = 64
    SCALE = float(DH) ** -0.5
    CH = -(-HH * K2 // P)
    LASTROWS = HH * K2 - (CH - 1) * P
    G0 = [min(c * P // (2 * K2), HH // 2 - 2) for c in range(CH)]
    assert (KC, NSEG, TPB, HH, DH, SEG // 2 * HH) == (2, 2, 2, 8, 16, 512) and 4 * K2 <= 512
    for g in range(HH // 2):
        lo, hi = 2 * g * K2 // P, (2 * (g + 1) * K2 - 1) // P
        assert hi == lo + 1 and all(0 <= g - G0[c] <= 1 for c in (lo, hi))

    with ExitStack() as top:
        def alloc(stack, name, shape, dt=F32):
            return stack.enter_context(nc.sbuf_tensor(name, shape, dt))

        def psum(name, shape):
            return top.enter_context(nc.psum_tensor(name, shape, F32))

        def signal(name, per, unit=1):
            return Signal(top.enter_context(nc.semaphore(name)), per, unit)

        ps_s = psum("ps_s", [P, 2, 512])
        ps_t = psum("ps_t", [P, 2, 512])
        ps_m = psum("ps_m", [P, 3, 512])
        ps_o = psum("ps_o", [P, 512])

        ps_x = [ps_o, ps_m[:, 2, :]]

        w_banks = [ps_t[:, 0, :], ps_t[:, 1, :], ps_o[:], ps_m[:, 0, :]]

        w1s = alloc(top, "w1s", [P, E, KC, F])
        w2s = alloc(top, "w2s", [P, E, FC, D])
        logits = alloc(top, "logits", [P, TPB, E])
        lmax = alloc(top, "lmax", [P, TPB])
        ldif = alloc(top, "ldif", [P, TPB, E])
        lexp = alloc(top, "lexp", [P, TPB, E])
        lsum = alloc(top, "lsum", [P, TPB])
        ismax = alloc(top, "ismax", [P, TPB, E])
        best = alloc(top, "best", [P, TPB])
        onehot = alloc(top, "onehot", [P, RW])
        before = alloc(top, "before", [P, RW])
        rank = alloc(top, "rank", [P, TPB, E])
        place = alloc(top, "place", [P, TPB])
        place_i = alloc(top, "place_i", [P, TPB], U32)
        member = alloc(top, "member", [P, TPB, 2])
        batch_step = alloc(top, "batch_step", [P, TPB])
        rev = alloc(top, "rev", [P, E])
        tri = alloc(top, "tri", [P, P])
        t_i = alloc(top, "t_i", [P, E], I32)
        n_e = alloc(top, "n_e", [P, E])
        t_e = alloc(top, "t_e", [P, E])
        tb_e = alloc(top, "tb_e", [P, E])
        zeros = alloc(top, "zeros", [P, E])
        ended = alloc(top, "ended", [P, E])
        ended_t = alloc(top, "ended_t", [P, E])
        e_f = alloc(top, "e_f", [P, 1])
        start_f = alloc(top, "start_f", [P, 1])
        plan_f = alloc(top, "plan_f", [P, 2])
        plan_i = alloc(top, "plan_i", [P, 2, NTILE], I32)
        row_i, e_i = plan_i[:, 0, :], plan_i[:, 1, :]
        round_up = alloc(top, "round_up", [P, E])
        tile_no = alloc(top, "tile_no", [P, 1])
        ident = alloc(top, "ident", [P, P])
        ones = alloc(top, "ones", [P, P])
        b1t = alloc(top, "b1t", [P, E * FC])
        eps = alloc(top, "eps", [P, 1])
        neg_half = alloc(top, "neg_half", [P, 1])

        with ExitStack() as part1:
            def sb1(name, shape, dt=F32):
                return alloc(part1, name, shape, dt)

            wqkv_s = sb1("wqkv_s", [P, KC, 3 * D])
            wout_s = sb1("wout_s", [P, KC, D])
            wT = sb1("wT", [P, 4, KC, D])
            router_s = sb1("router_s", [P, KC, RW])
            bq_s = sb1("bq_s", [P, KC])
            bk_s = sb1("bk_s", [P, KC])
            bv_s = sb1("bv_s", [P, KC])
            bo_s = sb1("bo_s", [P, D])
            kmask = sb1("kmask", [P, HH])
            vmask = sb1("vmask", [P, CH, 64])
            xs = sb1("xs", [P, TPB, D])
            xres = sb1("xres", [P, TPB, D])
            xT = sb1("xT", [P, KC, S])
            xkT = sb1("xkT", [P, KC, NSEG, KEYS])
            qT = sb1("qT", [P, KC, S])
            kT = sb1("kT", [P, KC, NSEG, KEYS])
            kblk = sb1("kblk", [P, KC, NSEG, HH, KEYS])
            vA = sb1("vA", [P, NSEG, D])
            prob = sb1("prob", [P, 3, 1024])
            probT = sb1("probT", [P, 2, 1024])
            mx = sb1("mx", [P, 2, H])
            den = sb1("den", [P, 2, H])
            rden = sb1("rden", [P, 2, H])
            oTa = sb1("oTa", [P, KC, S])
            oTx = sb1("oTx", [P, KC, S])
            sum1 = sb1("sum1", [P, D])
            sum2 = sb1("sum2", [P, D])
            sum1b = sb1("sum1b", [P, D])
            sum2b = sb1("sum2b", [P, D])
            st = sb1("st", [P, 4, 6])
            mv = sb1("mv", [P, 4, 2])
            ve = sb1("ve", [P, 4])
            rstd = sb1("rstd", [P, 4])
            x1 = sb1("x1", [P, TPB, D])
            x1r = sb1("x1r", [P, TPB, D])
            x1T = sb1("x1T", [P, KC, S])
            qxT = sb1("qxT", [P, KC, S])
            ctx_s = sb1("ctx_s", [P, D])
            ctxT = sb1("ctxT", [P, KC, K2])
            vT3 = sb1("vT3", [P, KC, 3, K2])
            kxT = sb1("kxT", [P, KC, K2])
            kxblk = sb1("kxblk", [P, KC, HH, K2])
            vX = sb1("vX", [P, CH, KC, 64])
            x2s = sb1("x2s", [P, TPB, D])
            x2T = sb1("x2T", [P, KC, S])
        fill = x2T[:].rearrange("p c s -> p (c s)")
        assert LIST_ROWS % P == 0
        w_raw = [qxT, oTx, x1r, x2s]

        XR = 6
        SLOTS_AHEAD, ROWS_AHEAD = 4, 3
        with ExitStack() as part2:
            def sb2(name, shape, dt=F32):
                return alloc(part2, name, shape, dt)

            slots = sb2("slots", [P, NTILE, 2])
            idx_g = sb2("idx_g", [P, XR], U32)
            idx_s = sb2("idx_s", [P, XR], U32)
            xg = sb2("xg", [P, XR, D])
            xgT = sb2("xgT", [P, 2, D])
            w1b = sb2("w1b", [P, 2, KC, F])
            hT = sb2("hT", [P, 2, FC, P])
            b2r = sb2("b2r", [P, XR, D])
            yb = sb2("yb", [P, 2, D])
            ys = sb2("ys", [P, 2, D])
            st3 = sb2("st3", [P, 2, 6])
            mv3 = sb2("mv3", [P, 2, 2])
            ve3 = sb2("ve3", [P, 2])
            rs3 = sb2("rs3", [P, 2])
            yo = sb2("yo", [P, XR, D])

        lists = nc.dram_tensor("token_lists", (LIST_ROWS, 2), F32, kind="Internal").ap()
        x2_dram = nc.dram_tensor("x2_rows", (B * S, D), F32, kind="Internal").ap()

        square_loaded = signal("square_loaded", 4, 16)
        qkv_loaded = signal("qkv_loaded", 1, 16)
        w_loaded = signal("w_loaded", 1, 16)
        ident_made = signal("ident_made", 1)
        squares_done = signal("squares_done", 1)
        consts_made = signal("consts_made", 1)
        consts_ready = signal("consts_ready", 1)
        wT_ready = signal("wT_ready", 1)
        wT_drained = signal("wT_drained", 1)
        bo_ready = signal("bo_ready", 1)
        carried = signal("carried", 1)
        x_loaded = signal("x_loaded", 1, 16)
        xres_loaded = signal("xres_loaded", 1, 16)
        ctx_loaded = signal("ctx_loaded", 1, 16)
        experts_loaded = signal("experts_loaded", 2, 16)
        x2_stored = [signal(f"x2_stored{t}", 1, 16) for t in range(TPB)]
        UN = {"a": 2, "x": 4}
        sc_done = {u: signal(f"sc_done_{u}", n) for u, n in UN.items()}
        pT_done = {u: signal(f"pT_done_{u}", n) for u, n in UN.items()}
        pv_done = {u: signal(f"pv_done_{u}", n) for u, n in UN.items()}
        max_done = {u: signal(f"max_done_{u}", n) for u, n in UN.items()}
        sub_done = {u: signal(f"sub_done_{u}", n) for u, n in UN.items()}
        exp_done = {u: signal(f"exp_done_{u}", n) for u, n in UN.items()}
        sum_done = {u: signal(f"sum_done_{u}", n) for u, n in UN.items()}
        rec_done = {u: signal(f"rec_done_{u}", n) for u, n in UN.items()}
        pT_copied = {u: signal(f"pT_copied_{u}", n) for u, n in UN.items()}
        scaled = {u: signal(f"scaled_{u}", n) for u, n in UN.items()}
        o_taken = {u: signal(f"o_taken_{u}", n) for u, n in UN.items()}
        JN = {"xT": 2, "q": 2, "k": 1, "v": 2, "oa": 2, "x1T": 2, "ctxT": 1, "kx": 1, "qx": 2, "vT": 1, "vx": 2, "ox": 2,
              "x2T": 2, "rt": 1, "rk": 1}
        computed = {j: signal(f"computed_{j}", n) for j, n in JN.items()}
        taken = {j: signal(f"taken_{j}", n) for j, n in JN.items()}
        kblk_made = signal("kblk_made", 1)
        kxblk_made = signal("kxblk_made", 1)
        x1r_made = signal("x1r_made", 1)
        stats_done = {n: signal(f"stats_done{n}", 2) for n in (1, 2)}
        mean_done = {n: signal(f"mean_done{n}", 2) for n in (1, 2)}
        eps_added = {n: signal(f"eps_added{n}", 2) for n in (1, 2)}
        rstd_done = {n: signal(f"rstd_done{n}", 2) for n in (1, 2)}
        ln_done = {n: signal(f"ln_done{n}", 2) for n in (1, 2)}
        STAGES = ("max", "less_max", "is_max", "weigh", "first", "count", "onehot", "count_tile", "gate_sum", "gate",
                  "pick", "place")
        routed = signal("routed", len(STAGES))
        gate_exp_done = signal("gate_exp_done", 1)
        place_taken = signal("place_taken", 1)
        token_stepped = signal("token_stepped", 1)
        entered = [signal(f"entered{t}", 1, 16) for t in range(TPB)]
        part1_signals = [routed, gate_exp_done, place_taken, token_stepped, x_loaded, xres_loaded,
                         ctx_loaded, *x2_stored, kblk_made, kxblk_made, x1r_made]
        for group in (sc_done, pT_done, pv_done, max_done, sub_done, exp_done, sum_done, rec_done, pT_copied,
                      scaled, o_taken, computed, taken, stats_done, mean_done, eps_added, rstd_done, ln_done):
            part1_signals += group.values()
        dve2 = signal("dve2", 1)
        fill_made = signal("fill_made", 1)
        lists_filled = signal("lists_filled", 2, 16)
        total_done = signal("total_done", 1)
        rows_cleared = signal("rows_cleared", 1)
        plan_made = signal("plan_made", 2)
        plan_spread = signal("plan_spread", 1)
        plan_ready = signal("plan_ready", 1)
        f_names = ("idx_g_made", "idx_s_made", "xgT_done", "xgT_copied", "h_done", "w1_copied_act", "w1_copied_dve",
                   "gelu_done", "y_done",
                   "bias_added", "res_done", "st3_done", "mv3_done", "ve3_done", "rs3_done", "ln3_done")
        f = {n: signal(n, 1) for n in f_names}
        gathered = [signal(f"gathered{m}", 1, 16) for m in range(XR)]
        b2_loaded = [signal(f"b2_loaded{m}", 1, 16) for m in range(XR)]
        slots_loaded = [signal(f"slots_loaded{m}", 1, 16) for m in range(XR)]
        stored = [signal(f"stored{m}", 1, 16) for m in range(XR)]

        def wait_ring(eng, ring, g, m, behind=0):
            wait(eng, ring[(m - behind) % XR], g + (m - behind) // XR)

        def exists(b):
            return not isinstance(b, int) or 0 <= b < B

        MB = 3
        JOBS = [
            [("ctxT", 0, 2), ("kx", 0, 2), ("ox", 0, 3), ("vT", 0, 2), ("x1T", 1, 2)],
            [("qx", 0, 2), ("qx", 1, 2), ("vx", 0, 2)],
            [("x2T", 0, 3), ("vx", 1, 2), ("ox", 1, 3)],
            [("oa", 0, 1), ("xT", 0, 0), ("xT", 1, 0)],
            [("k", 0, 0), ("rk", 0, 4), ("oa", 1, 1), ("v", 0, 0), ("q", 0, 0), ("q", 1, 0)],
            [("x2T", 1, 3), ("v", 1, 0), ("x1T", 0, 1), ("rt", 0, 3)],
        ]
        PE_ORDER = [
            ("job", "scores", "attend", "probT", "job"),
            ("scores", "attend", "probT"),
            ("attend", "probT", "scores"),
            ("attend", "scores", "probT"),
            ("attend", "probT", "scores", "job"),
            ("attend", "probT", "scores", "job"),
        ]
        ACT_ORDER = [
            ("job", "take_o", "probT", "job", "exp", "job"),
            ("take_o", "gate_exp", "probT", "job", "job", "exp", "job", "job"),
            ("probT", "take_o", "exp", "job", "job", "job"),
            ("take_o", "probT", "job", "job", "job", "exp", "job"),
            ("take_o", "probT", "job", "job", "exp", "job", "job"),
            ("probT", "take_o", "job", "job", "exp", "job", "job"),
        ]
        DVE_ORDER = [
            ("sum", "route", "reciprocal", "max", "route", "route", "less_max", "layernorm11", "job", "stats20", "mean20"),
            ("sum", "route", "reciprocal", "max", "route", "less_max", "layernorm20", "job"),
            ("sum", "route", "reciprocal", "max", "route", "less_max", "job", "job", "stats21", "mean21"),
            ("sum", "route", "reciprocal", "max", "route", "less_max", "job", "job", "stats10", "mean10"),
            ("sum", "reciprocal", "layernorm10", "max", "route", "less_max", "job", "job", "job", "stats11", "mean11"),
            ("layernorm21", "sum", "route", "reciprocal", "max", "route", "less_max"),
        ]
        POOL_ORDER = [
            ("rstd11", "scale"),
            ("rstd20", "scale", "kxblk"),
            ("scale",),
            ("scale", "x1r"),
            ("rstd10", "rstd21", "scale"),
            ("kblk", "scale", "enter"),
        ]
        FLAT = [j for step in JOBS for j in step]
        assert len(FLAT) % MB == 0
        UNITS = [("a", 0), ("a", 1), ("x", 0), ("x", 1), ("x", 2), ("x", 3)]
        LAG = {"a": 1, "x": 2}
        LAST_LAG = 4
        FIRST_FULL = LAST_LAG + 1

        def job_before(n, i):
            for back in range(MB, 4 * len(FLAT), MB):
                m, it = (n - back) % len(FLAT), i + (n - back) // len(FLAT)
                if exists(it - FLAT[m][2]):
                    return FLAT[m][0], FLAT[m][1], it - FLAT[m][2]
            return None

        def unit_at(n, i):
            it = i + n // 6
            kind, k = UNITS[n % 6]
            return kind, k, it - LAG[kind], (n % 6) % 2

        def unit_before(n, i, by):
            for back in range(by, 24, by):
                u = unit_at(n - back, i)
                if exists(u[2]):
                    return u[:3]
            return None

        def wait_for(eng, signals, event):
            if event is not None:
                wait(eng, signals[event[0]], event[2], event[1])

        V_CHUNKS = [range(0, 3), range(3, CH)]

        def v_dims(ch):
            lo = 32 * G0[ch] // 64 * 64
            return lo, 32 * G0[ch] + 64

        def v_column(n, ch, h):
            k = 0 if ch in V_CHUNKS[0] else 1
            width = lambda c: v_dims(c)[1] - v_dims(c)[0]
            return sum(KC * width(c) for c in V_CHUNKS[k] if c < ch) + h * width(ch)

        def bank_of(n):
            return ps_m[:, n % MB, 0:256]

        def norm_of(what):
            return int(what[-2]), int(what[-1])

        def norm_batch(which, s, i):
            return i - (3 if which == 2 else 1 if s >= 3 else 2)

        def step_of(order, step, i, mine=lambda job: True):
            start = sum(len(s) for s in JOBS[:step])
            jobs = [(n, job, k, lag) for n, (job, k, lag) in enumerate(JOBS[step], start) if mine(job)]
            places = list(order) + ["job"] * (len(jobs) - order.count("job"))
            for what in places:
                if what != "job":
                    yield what, None
                elif jobs:
                    n, job, k, lag = jobs.pop(0)
                    if exists(i - lag):
                        yield what, (n, job, k, i - lag)

        block = top.enter_context(nc.Block())
        out_rows = out.rearrange("b s d -> (b s) d")

        def tail_of_part1(eng):
            for sig in part1_signals:
                eng.wait_ge(sig.sem, sig.at(B - 1))

        N_LOADS = 7

        def for_tiles(eng, one, extra):
            first, last = 2 * XR, (NTILE - SLOTS_AHEAD) // XR * XR
            for j in range(first):
                one(j, j // XR, j % XR)
            with eng.Fori(first // XR, last // XR) as g:
                for m in range(XR):
                    one(g * XR + m, g, m)
            for j in range(last, NTILE + extra):
                one(j, j // XR, j % XR)

        def w1_copy(eng, copy, c, name, j, m):
            e = eng.value_load(e_i[0:1, j:j + 1] if isinstance(j, int) else e_i[0:1, bass.ds(j, 1)],
                               min_val=0, max_val=E - 1)
            wait(eng, f["h_done"], j - 2)
            copy(w1b[:, m % 2, c, :], w1s[:, bass.ds(e, 1), c, :].rearrange("p a f -> p (a f)")).then_inc(
                f[name].sem, 1)

        def loop_batches(eng, iteration):
            for i in range(FIRST_FULL):
                iteration(eng, i)
            with eng.Fori(FIRST_FULL, B) as i:
                iteration(eng, i)
            for i in range(B, B + LAST_LAG):
                iteration(eng, i)


        def settled(eng):
            eng.sem_inc(carried.sem, 1)

        def sp_iteration(sp, i):
            p, a, c, z = i, i - 1, i - 2, i - 3
            if exists(a):
                wait(sp, taken["oa"], a - 1, 1)
                sp.dma_start(xres[:], x_tiles(a)).then_inc(xres_loaded.sem, 16)
                wait(sp, computed["ctxT"], a - 1)
                sp.dma_start(ctx_s[0:K2, :], row_of(ctx_in, a)).then_inc(ctx_loaded.sem, 16)
            if exists(z):
                sp.wait_ge(ln_done[2].sem, ln_done[2].at(z, 0))
                sp.dma_start(x2_tile(z, 0), x2s[:, 0, :]).then_inc(x2_stored[0].sem, 16)
                sp.wait_ge(ln_done[2].sem, ln_done[2].at(z, 1))
                sp.dma_start(x2_tile(z, 1), x2s[:, 1, :]).then_inc(x2_stored[1].sem, 16)
            if not isinstance(i, int) or i < B - 1:
                sp.wait_ge(computed["xT"].sem, computed["xT"].at(p))
                sp.dma_start(xs[:], x_tiles(p + 1)).then_inc(x_loaded.sem, 16)

        def row_of(t, b):
            if isinstance(b, int):
                return t[b]
            return t[bass.ds(b, 1)].rearrange("a s d -> (a s) d")

        def x_tiles(b):
            return row_of(x, b).rearrange("(t p) d -> p t d", p=P)

        def x2_tile(b, t):
            v = x2_dram.rearrange("(b t p) d -> b t p d", t=TPB, p=P)
            if isinstance(b, int):
                return v[b, t]
            return v[bass.ds(b, 1), t].rearrange("a p d -> (a p) d")

        def load_experts(sp, e):
            if isinstance(e, int):
                d1, d2, s1, s2 = w1s[:, e], w2s[:, e], w1[e], w2[e]
            else:
                d1 = w1s[:, bass.ds(e, 1)].rearrange("p a c f -> p (a c) f")
                d2 = w2s[:, bass.ds(e, 1)].rearrange("p a c f -> p (a c) f")
                s1 = w1[bass.ds(e, 1)].rearrange("a d f -> (a d) f")
                s2 = w2[bass.ds(e, 1)].rearrange("a d f -> (a d) f")
            sp.dma_start(d1, s1.rearrange("(c p) f -> p c f", p=P)).then_inc(experts_loaded.sem, 16)
            sp.dma_start(d2, s2.rearrange("(c p) d -> p c d", p=P)).then_inc(experts_loaded.sem, 16)

        @block.sync
        def _(sp):
            def load(dst, src):
                sp.dma_start(dst, src).then_inc(w_loaded.sem, 16)

            sp.dma_start(xs[:], x_tiles(0)).then_inc(x_loaded.sem, 16)
            sp.dma_start(wqkv_s[:], w_qkv.rearrange("(c p) n -> p c n", p=P)).then_inc(qkv_loaded.sem, 16)
            for n, w in enumerate((wq, wk, wv, wo)):
                sp.dma_start(w_raw[n][:], w.rearrange("(c p) d -> p c d", p=P)).then_inc(square_loaded.sem, 16)
            load(wout_s[:], w_out.rearrange("(c p) n -> p c n", p=P))
            load(router_s[:, :, 0:E], router_w.rearrange("(c p) n -> p c n", p=P))
            for dst, src in ((bq_s, bq), (bk_s, bk), (bv_s, bv)):
                with nc.allow_non_contiguous_dma("a bias of 256 values, by partition"):
                    load(dst[:], src.rearrange("(c p) -> p c", p=P))
            load(bo_s[:], bo.rearrange("(a d) -> a d", a=1).to_broadcast([P, D]))
            load(oTa[0:E * FC, 0, 0:P], b1.rearrange("e (c p) -> (e c) p", p=P))
            sp.wait_ge(fill_made.sem, 1)
            flat_lists = lists.rearrange("(p r) c -> p (r c)", p=P)
            half = LIST_ROWS // P // 2 * 2
            sp.dma_start(flat_lists[:, 0:half], fill[:, 0:half]).then_inc(lists_filled.sem, 16)
            sp.dma_start(flat_lists[:, half:], fill[:, 0:2 * (LIST_ROWS // P) - half]).then_inc(lists_filled.sem, 16)
            early = E - (B - 1 - FIRST_FULL)
            for i in range(FIRST_FULL):
                sp_iteration(sp, i)
                if i < early:
                    load_experts(sp, i)
            with sp.Fori(FIRST_FULL, B - 1) as i:
                sp_iteration(sp, i)
                load_experts(sp, i - (FIRST_FULL - early))
            for i in range(B - 1, B + LAST_LAG):
                sp_iteration(sp, i)
            sp.wait_ge(plan_ready.sem, 1)
            tail_of_part1(sp)
            for sig in entered:
                sp.wait_ge(sig.sem, sig.at(B - 1))

            def slots_load(j, g, m):
                row = sp.value_load(row_i[0:1, j:j + 1] if isinstance(j, int) else row_i[0:1, bass.ds(j, 1)],
                                    min_val=0, max_val=LIST_ROWS - P)
                dst = slots[:, j] if isinstance(j, int) else slots[:, bass.ds(j, 1)].rearrange("p a c -> p (a c)")
                wait_ring(sp, slots_loaded, g, m, XR)
                with nc.allow_non_contiguous_dma("a token's number and weight"):
                    sp.dma_start(dst, lists[bass.ds(row, P), :]).then_inc(slots_loaded[m].sem, 16)

            def one(j, g, m):
                if not isinstance(j, int) or j + SLOTS_AHEAD < NTILE:
                    slots_load(j + SLOTS_AHEAD, g + (m + SLOTS_AHEAD) // XR, (m + SLOTS_AHEAD) % XR)
                e = sp.value_load(e_i[0:1, j:j + 1] if isinstance(j, int) else e_i[0:1, bass.ds(j, 1)],
                                  min_val=0, max_val=E - 1)
                wait(sp, f["bias_added"], j - XR)
                src = b2[bass.ds(e, 1), :].to_broadcast([P, D])
                sp.dma_start(b2r[:, m, :], src).then_inc(b2_loaded[m].sem, 16)

            for j in range(SLOTS_AHEAD):
                slots_load(j, 0, j)
            for_tiles(sp, one, 0)

        def transpose(dst, src):
            return nc.tensor.transpose(dst, src, ident[:])

        def pe_scores(pe, n, i):
            kind, k, b, par = unit_at(n, i)
            if not exists(b):
                return
            wait_for(pe, sub_done, unit_before(n, i, 1))
            if kind == "a":
                pe.wait_ge(taken["q"].sem, taken["q"].at(b))
                pe.wait_ge(kblk_made.sem, kblk_made.at(b))
                for h in range(KC):
                    last = nc.tensor.matmul(ps_s[:, h, :], qT[:, h, k * SEG:(k + 1) * SEG],
                                            kblk[:, h, k].rearrange("p h k -> p (h k)"), start=True, stop=True)
            else:
                pe.wait_ge(taken["qx"].sem, taken["qx"].at(b))
                pe.wait_ge(kxblk_made.sem, kxblk_made.at(b))
                t, h = k // 2, k % 2
                for q in range(2):
                    last = nc.tensor.matmul(ps_s[:, q, 0:4 * K2], qxT[:, h, t * P:(t + 1) * P],
                                            kxblk[:, h, 4 * q:4 * q + 4].rearrange("p h k -> p (h k)"),
                                            start=True, stop=True)
            last.then_inc(sc_done[kind].sem, 1)

        def pe_probT(pe, n, i):
            kind, k, b, par = unit_at(n, i)
            if not exists(b):
                return
            pe.wait_ge(scaled[kind].sem, scaled[kind].at(b, k))
            wait_for(pe, pT_copied, unit_before(n, i, 1))
            width = H * KEYS if kind == "a" else HH * K2
            for c in range(-(-width // P)):
                cols = min(P, width - c * P)
                last = transpose(ps_t[0:cols, c // 4, (c % 4) * P:(c % 4) * P + P],
                                 prob[:, n % 3, c * P:c * P + cols])
            last.then_inc(pT_done[kind].sem, 1)

        def pe_attend(pe, n, i):
            kind, k, b, par = unit_at(n, i)
            if not exists(b):
                return
            wait_for(pe, o_taken, unit_before(n, i, 1))
            pe.wait_ge(pT_copied[kind].sem, pT_copied[kind].at(b, k))
            if kind == "a":
                pe.wait_ge(taken["v"].sem, taken["v"].at(b))
                for pair in range(H // 2):
                    g, h = pair % 4, pair // 4
                    last = nc.tensor.matmul(ps_o[32 * g:32 * g + 32, h * P:(h + 1) * P],
                                            vA[:, k, 32 * pair:32 * pair + 32],
                                            probT[:, par, pair * P:(pair + 1) * P], start=True, stop=True)
            else:
                pe.wait_ge(taken["vx"].sem, taken["vx"].at(b))
                h = k % 2
                for part in range(2):
                    for g in range(HH // 2):
                        c = 2 * g * K2 // P + part
                        rows = LASTROWS if c == CH - 1 else P
                        off = 32 * (g - G0[c])
                        last = nc.tensor.matmul(ps_o[32 * g:32 * g + 32, 0:P], vX[0:rows, c, h, off:off + 32],
                                                probT[0:rows, par, c * P:(c + 1) * P],
                                                start=(part == 0), stop=(part == 1))
            last.then_inc(pv_done[kind].sem, 1)

        def pe_job(pe, n, job, k, b, i):
            dst = bank_of(n)
            wait_for(pe, taken, job_before(n, i))

            def project(lhs, rhs, dst=dst, width=D):
                for c in range(KC):
                    last = nc.tensor.matmul(dst[:, 0:width], lhs(c), rhs(c), start=(c == 0), stop=(c == KC - 1))
                return last

            cols = slice(k * P, (k + 1) * P)
            if job == "xT":
                pe.wait_ge(x_loaded.sem, x_loaded.at(b))
                for c in range(KC):
                    last = transpose(dst[:, c * P:(c + 1) * P], xs[:, k, c * P:(c + 1) * P])
            elif job == "x1T":
                pe.wait_ge(ln_done[1].sem, ln_done[1].at(b, k))
                for c in range(KC):
                    last = transpose(dst[:, c * P:(c + 1) * P], x1[:, k, c * P:(c + 1) * P])
            elif job == "x2T":
                pe.wait_ge(ln_done[2].sem, ln_done[2].at(b, k))
                for c in range(KC):
                    last = transpose(dst[:, c * P:(c + 1) * P], x2s[:, k, c * P:(c + 1) * P])
            elif job == "ctxT":
                pe.wait_ge(ctx_loaded.sem, ctx_loaded.at(b))
                for c in range(KC):
                    last = nc.tensor.transpose(dst[:, c * P:c * P + K2], ctx_s[0:K2, c * P:(c + 1) * P],
                                               ident[0:K2, 0:K2])
            elif job == "q":
                pe.wait_ge(taken["xT"].sem, taken["xT"].at(b))
                last = project(lambda c: wqkv_s[:, c, cols], lambda c: xT[:, c, :])
            elif job == "k":
                pe.wait_ge(taken["xT"].sem, taken["xT"].at(b))
                for h in range(KC):
                    last = project(lambda c: wqkv_s[:, c, D + h * P:D + (h + 1) * P],
                                   lambda c: xkT[:, c].rearrange("p s k -> p (s k)"), dst[:, h * P:], P)
            elif job == "v":
                pe.wait_ge(taken["xT"].sem, taken["xT"].at(b))
                for c in range(KC):
                    heads = wqkv_s[:, c, 2 * D:3 * D].rearrange("p (g o d) -> p g o d", o=2, d=DH)
                    for o in range(2):
                        last = nc.tensor.matmul(dst[o * KEYS:(o + 1) * KEYS, 0:P], xkT[:, c, k, :], heads[:, :, o, :],
                                                start=(c == 0), stop=(c == KC - 1))
            elif job == "oa":
                pe.wait_ge(o_taken["a"].sem, o_taken["a"].at(b, k))
                last = project(lambda c: oTa[:, c, cols], lambda c: wout_s[:, c, :])
            elif job == "qx":
                pe.wait_ge(taken["x1T"].sem, taken["x1T"].at(b))
                last = project(lambda c: wT[:, 0, c, cols], lambda c: x1T[:, c, :])
            elif job == "kx":
                pe.wait_ge(taken["ctxT"].sem, taken["ctxT"].at(b))
                for h in range(KC):
                    last = project(lambda c: wT[:, 1, c, h * P:(h + 1) * P],
                                   lambda c: ctxT[:, c, :], dst[:, h * P:], K2)
            elif job == "vT":
                pe.wait_ge(taken["ctxT"].sem, taken["ctxT"].at(b))
                for h in range(KC):
                    last = project(lambda c: wT[:, 2, c, h * P:(h + 1) * P], lambda c: ctxT[:, c, :], dst[:, h * P:], K2)
            elif job == "vx":
                pe.wait_ge(taken["vT"].sem, taken["vT"].at(b))
                settled(pe)
                for ch in V_CHUNKS[k]:
                    off = ch * P % K2
                    lo, hi = v_dims(ch)
                    for h in range(KC):
                        at = v_column(n, ch, h)
                        last = nc.tensor.transpose(ps_m[:, n % MB, at:at + hi - lo],
                                                   vT3[lo:hi, h].rearrange("p r k -> p (r k)")[:, off:off + P],
                                                   ident[lo:hi, lo:hi])
            elif job == "ox":
                pe.wait_ge(o_taken["x"].sem, o_taken["x"].at(b, 2 * k + 1))
                last = project(lambda c: oTx[:, c, cols], lambda c: wT[:, 3, c, :])
            elif job == "rt":
                pe.wait_ge(taken["x2T"].sem, taken["x2T"].at(b))
                for t in range(TPB):
                    last = project(lambda c: x2T[:, c, t * P:(t + 1) * P], lambda c: router_s[:, c, :],
                                   dst[:, t * RW:], RW)
            elif job == "rk":
                pe.wait_ge(routed.sem, routed.at(b, STAGES.index("count_tile")))
                nc.tensor.matmul(dst[:, 0:RW], tri[:], onehot[:], start=True, stop=False)
                last = nc.tensor.matmul(dst[:, 0:RW], ones[:], before[:], start=False, stop=True)
            last.then_inc(computed[job].sem, 1)

        def pe_weights(pe, s):
            if s == 0:
                pe.wait_ge(square_loaded.sem, square_loaded.at(0))
                pe.wait_ge(w_loaded.sem, 16 * N_LOADS)
                for job in ("xT", "q", "k", "v"):
                    pe.wait_ge(taken[job].sem, taken[job].at(0))
                for n in range(4):
                    for c in range(KC):
                        for r in range(KC):
                            last = transpose(w_banks[n][:, c * D + r * P:c * D + (r + 1) * P],
                                             w_raw[n][:, r, c * P:(c + 1) * P])
                last = nc.tensor.transpose(ps_m[:, 1, 0:E * FC], oTa[0:E * FC, 0, 0:P], ident[0:E * FC, 0:E * FC])
                last.then_inc(squares_done.sem, 1)
            elif s == 1:
                pe.wait_ge(wT_drained.sem, 1)
                for c in range(KC):
                    last = nc.tensor.matmul(ps_m[:, 2, 0:D], bv_s[:, c:c + 1].to_broadcast([P, P]), wT[:, 3, c, :],
                                            start=(c == 0), stop=(c == KC - 1))
                last.then_inc(wT_ready.sem, 1)
            elif s == 2:
                pe.wait_ge(consts_ready.sem, 1)
                pe.wait_ge(bo_ready.sem, 1)

        def pe_iteration(pe, i):
            for s in range(6):
                for what, job in step_of(PE_ORDER[s], s, i):
                    if what == "scores":
                        pe_scores(pe, s, i)
                    elif what == "probT":
                        pe_probT(pe, s - 2, i)
                    elif what == "attend":
                        pe_attend(pe, s - 3, i)
                    else:
                        pe_job(pe, *job, i)
                if isinstance(i, int) and i == 1:
                    pe_weights(pe, s)

        @block.tensor
        def _(pe):
            pe.wait_ge(ident_made.sem, 1)
            pe.wait_ge(qkv_loaded.sem, qkv_loaded.at(0))

            loop_batches(pe, pe_iteration)

            pe.wait_ge(sub_done["x"].sem, sub_done["x"].at(B - 1))
            nc.tensor.matmul(ps_s[:, 0, 0:RW], ones[:], before[:], start=True, stop=False)
            nc.tensor.matmul(ps_s[:, 0, 0:RW], ones[:], onehot[:], start=False, stop=True).then_inc(total_done.sem, 1)
            pe.wait_ge(plan_made.sem, 2)
            for c in range(2):
                last = nc.tensor.matmul(ps_s[:, 1, c * RW:(c + 1) * RW], plan_f[:, c:c + 1].to_broadcast([P, P]),
                                        ident[:, 0:RW], start=True, stop=True)
            last.then_inc(plan_spread.sem, 1)
            pe.wait_ge(plan_ready.sem, 1)
            pe.wait_ge(experts_loaded.sem, 32 * E)

            def gathered_rows(j, g, m):
                wait_ring(pe, gathered, g, m)
                wait(pe, f["xgT_copied"], j - 2)
                for c in range(KC):
                    last = transpose(ps_x[m % 2][:, c * P:(c + 1) * P], xg[:, m, c * P:(c + 1) * P])
                last.then_inc(f["xgT_done"].sem, 1)

            def expert_of(j):
                return pe.value_load(e_i[0:1, j:j + 1] if isinstance(j, int) else e_i[0:1, bass.ds(j, 1)],
                                     min_val=0, max_val=E - 1)

            def one(j, g, m):
                if not isinstance(j, int) or 1 <= j <= NTILE:
                    e_before = expert_of(j - 1)
                if not isinstance(j, int) or j < NTILE:
                    pe.wait_ge(f["xgT_copied"].sem, f["xgT_copied"].at(j))
                    pe.wait_ge(f["w1_copied_act"].sem, f["w1_copied_act"].at(j))
                    pe.wait_ge(f["w1_copied_dve"].sem, f["w1_copied_dve"].at(j))
                    wait(pe, f["gelu_done"], j - 2)
                    for u in range(FC):
                        for c in range(KC):
                            last = nc.tensor.matmul(ps_s[:, m % 2, u * P:(u + 1) * P],
                                                    w1b[:, m % 2, c, u * P:(u + 1) * P],
                                                    xgT[:, m % 2, c * P:(c + 1) * P],
                                                    start=(c == 0), stop=(c == KC - 1))
                    last.then_inc(f["h_done"].sem, 1)
                if not isinstance(j, int) or j + 1 < NTILE:
                    gathered_rows(j + 1, g + (m + 1) // XR, (m + 1) % XR)
                if not isinstance(j, int) or 1 <= j <= NTILE:
                    wait(pe, f["gelu_done"], j - 1)
                    wait(pe, f["bias_added"], j - 3)
                    for c in range(FC):
                        last = nc.tensor.matmul(ps_m[:, (m - 1) % 2, 0:D], hT[:, (m - 1) % 2, c, :],
                                                w2s[:, bass.ds(e_before, 1), c, :].rearrange("p a f -> p (a f)"),
                                                start=(c == 0), stop=(c == FC - 1))
                    last.then_inc(f["y_done"].sem, 1)

            for _ in range(5):
                nc.tensor.matmul(ps_t[:, 0, :], ident[:], w1s[:, 0, 0, :], start=True, stop=True)
            gathered_rows(0, 0, 0)
            for_tiles(pe, one, 1)

        def act_probT(act, n, i):
            kind, k, b, par = unit_at(n, i)
            if not exists(b):
                return
            act.wait_ge(pT_done[kind].sem, pT_done[kind].at(b, k))
            wait_for(act, pv_done, unit_before(n, i, 2))
            if kind == "a":
                last = nc.scalar.copy(probT[:, par, :], ps_t[:].rearrange("p b n -> p (b n)"))
            else:
                nc.scalar.copy(probT[:, par, 0:512], ps_t[:, 0, :])
                last = nc.scalar.copy(probT[0:LASTROWS, par, 512:640], ps_t[0:LASTROWS, 1, 0:P])
            last.then_inc(pT_copied[kind].sem, 1)

        def act_take_o(act, n, i):
            kind, k, b, par = unit_at(n, i)
            if not exists(b):
                return
            act.wait_ge(pv_done[kind].sem, pv_done[kind].at(b, k))
            if kind == "a":
                wait(act, computed["oa"], b - 1, k)
                last = nc.scalar.copy(oTa[:, :, k * SEG:(k + 1) * SEG],
                                      ps_o[:, 0:256].rearrange("p (c n) -> p c n", c=KC))
            else:
                t, h = k // 2, k % 2
                wait(act, computed["ox"], b - 1, t)
                last = nc.scalar.copy(oTx[:, h, t * P:(t + 1) * P], ps_o[:, 0:P])
            last.then_inc(o_taken[kind].sem, 1)

        def act_exp(act, n, i):
            kind, k, b, par = unit_at(n, i)
            if not exists(b):
                return
            width = H * KEYS if kind == "a" else HH * K2
            act.wait_ge(sub_done[kind].sem, sub_done[kind].at(b, k))
            nc.scalar.activation(prob[:, n % 3, 0:width], prob[:, n % 3, 0:width], ACT.Exp,
                                 scale=SCALE).then_inc(exp_done[kind].sem, 1)

        def act_take(act, n, job, k, b):
            src = bank_of(n)
            act.wait_ge(computed[job].sem, computed[job].at(b, k))
            pair = src.rearrange("p (c n) -> p c n", c=KC)
            cols = slice(k * P, (k + 1) * P)
            if job == "xT":
                wait(act, computed["q"], b - 1)
                wait(act, computed["v"], b - 1)
                nc.scalar.copy(xT[:, :, cols], pair)
                grid = pair.rearrange("p c (r o k e) -> p c r o k e", o=2, k=8, e=2)
                dst = xkT[:, :, k].rearrange("p c (r o k) -> p c r o k", o=2, k=8)
                for o in range(2):
                    last = nc.scalar.copy(dst[:, :, :, o, :], grid[:, :, :, o, :, o])
            elif job == "q":
                wait(act, sc_done["a"], b - 1)
                last = nc.scalar.copy(qT[:, k, :], src)
            elif job == "k":
                wait(act, kblk_made, b - 1)
                last = nc.scalar.copy(kT[:].rearrange("p c s k -> p (c s k)"), src)
            elif job == "v":
                wait(act, pv_done["a"], b - 1)
                if isinstance(b, int) and b == 0:
                    act.wait_ge(dve2.sem, 1)
                dst = vA[:, k, :].rearrange("p (g o d) -> p g o d", o=2, d=DH)
                for o in range(2):
                    rows = slice(o * KEYS, (o + 1) * KEYS)
                    last = nc.scalar.copy(dst[rows, :, o, :], src[rows, 0:P].rearrange("p (g d) -> p g d", d=DH))
            elif job == "x1T":
                wait(act, computed["qx"], b - 1)
                last = nc.scalar.copy(x1T[:, :, cols], pair)
            elif job == "ctxT":
                wait(act, computed["kx"], b - 1)
                wait(act, computed["vT"], b - 1)
                last = nc.scalar.copy(ctxT[:], pair[:, :, 0:K2])
            elif job == "vT":
                wait(act, computed["vx"], b - 1)
                for h in range(KC):
                    last = nc.scalar.copy(vT3[:, h], pair[:, h, None, 0:K2].to_broadcast([P, 3, K2]))
            elif job == "kx":
                wait(act, kxblk_made, b - 1)
                for c in range(KC):
                    last = nc.scalar.activation(kxT[:, c, :], pair[:, c, 0:K2], ACT.Identity, bias=bk_s[:, c:c + 1])
            elif job == "qx":
                wait(act, sc_done["x"], b - 1)
                last = nc.scalar.activation(qxT[:, k, :], src, ACT.Identity, bias=bq_s[:, k:k + 1])
            elif job == "x2T":
                wait(act, computed["rt"], b - 1)
                last = nc.scalar.copy(x2T[:, :, cols], pair)
            elif job == "rt":
                wait(act, routed, b - 1, STAGES.index("is_max"))
                last = nc.scalar.copy(logits[:], src[:, 0:TPB * RW].rearrange("p (t e) -> p t e", t=TPB)[:, :, 0:E])
            last.then_inc(taken[job].sem, 1)

        BY_DVE = ("oa", "ox", "vx", "rk")

        def act_gate_exp(act, b):
            if not exists(b):
                return
            act.wait_ge(routed.sem, routed.at(b, STAGES.index("less_max")))
            wait(act, routed, b - 1, STAGES.index("gate_sum"))
            nc.scalar.activation(lexp[:].rearrange("p t e -> p (t e)"), ldif[:].rearrange("p t e -> p (t e)"),
                                 ACT.Exp).then_inc(gate_exp_done.sem, 1)

        def act_weights(act, s):
            if s == 0:
                act.wait_ge(squares_done.sem, 1)
                for n in range(4):
                    nc.scalar.copy(wT[:, n].rearrange("p c d -> p (c d)"), w_banks[n])
                nc.scalar.copy(b1t[:], ps_m[:, 1, 0:E * FC]).then_inc(wT_drained.sem, 1)
                act.wait_ge(consts_ready.sem, 1)
                act.wait_ge(lists_filled.sem, lists_filled.at(0))

        def act_iteration(act, i):
            for s in range(6):
                for what, job in step_of(ACT_ORDER[s], s, i, lambda j: j not in BY_DVE):
                    if what == "probT":
                        act_probT(act, s - 2, i)
                    elif what == "take_o":
                        act_take_o(act, s - 3, i)
                    elif what == "exp":
                        act_exp(act, s, i)
                    elif what == "gate_exp":
                        act_gate_exp(act, i - 4)
                    else:
                        act_take(act, *job)
                if isinstance(i, int) and i == 1:
                    act_weights(act, s)

        @block.scalar
        def _(act):
            loop_batches(act, act_iteration)
            act.wait_ge(plan_ready.sem, 1)
            tail_of_part1(act)

            def rows_copy(j, m):
                act.wait_ge(f["xgT_done"].sem, f["xgT_done"].at(j))
                wait(act, f["h_done"], j - 2)
                nc.scalar.copy(xgT[:, m % 2, :], ps_x[m % 2][:, 0:D]).then_inc(f["xgT_copied"].sem, 1)

            def one(j, g, m):
                if not isinstance(j, int) or j + 1 < NTILE:
                    w1_copy(act, nc.scalar.copy, 0, "w1_copied_act", j + 1, m + 1)
                if not isinstance(j, int) or j < NTILE:
                    e = act.value_load(e_i[0:1, j:j + 1] if isinstance(j, int) else e_i[0:1, bass.ds(j, 1)],
                                       min_val=0, max_val=E - 1)
                    act.wait_ge(f["h_done"].sem, f["h_done"].at(j))
                    wait(act, f["y_done"], j - 2)
                    for c in range(FC):
                        last = nc.scalar.activation(hT[:, m % 2, c, :], ps_s[:, m % 2, c * P:(c + 1) * P], ACT.Gelu,
                                                    bias=b1t[:, bass.ds(e * FC + c, 1)])
                    last.then_inc(f["gelu_done"].sem, 1)
                if not isinstance(j, int) or j + 1 < NTILE:
                    rows_copy(j + 1, m + 1)

            act.wait_ge(experts_loaded.sem, 32 * E)
            w1_copy(act, nc.scalar.copy, 0, "w1_copied_act", 0, 0)
            rows_copy(0, 0)
            for_tiles(act, one, 0)

        def unit_views(kind, par, third):
            if kind == "a":
                return (ps_s[:].rearrange("p b (h k) -> p (b h) k", k=KEYS),
                        prob[:, third, :].rearrange("p (h k) -> p h k", k=KEYS), H, mx[:, par, :],
                        mx[:, par, :, None].to_broadcast([P, H, KEYS]))
            return (ps_s[:, :, 0:4 * K2].rearrange("p b (h k) -> p b h k", k=K2),
                    prob[:, third, 0:HH * K2].rearrange("p (b h k) -> p b h k", b=2, k=K2), HH,
                    mx[:, par, 0:HH].rearrange("p (b h) -> p b h", b=2),
                    mx[:, par, 0:HH].rearrange("p (b h) -> p b h", b=2)[:, :, :, None].to_broadcast([P, 2, 4, K2]))

        def dve_max(dve, n, i):
            kind, k, b, par = unit_at(n, i)
            if not exists(b):
                return
            s, p, _, m, mb = unit_views(kind, par, n % 3)
            dve.wait_ge(sc_done[kind].sem, sc_done[kind].at(b, k))
            nc.vector.tensor_reduce(m, s, axis=AX, op=ALU.max).then_inc(max_done[kind].sem, 1)

        def dve_less_max(dve, n, i):
            kind, k, b, par = unit_at(n, i)
            if not exists(b):
                return
            s, p, _, m, mb = unit_views(kind, par, n % 3)
            dve.wait_ge(max_done[kind].sem, max_done[kind].at(b, k))
            wait_for(dve, pT_done, unit_before(n, i, 3))
            nc.vector.tensor_tensor(p, s, mb, ALU.subtract).then_inc(sub_done[kind].sem, 1)

        def dve_sum(dve, n, i):
            kind, k, b, par = unit_at(n, i)
            if not exists(b):
                return
            heads, width = (H, KEYS) if kind == "a" else (HH, K2)
            dve.wait_ge(exp_done[kind].sem, exp_done[kind].at(b, k))
            nc.vector.tensor_reduce(den[:, par, 0:heads],
                                    prob[:, n % 3, 0:heads * width].rearrange("p (h k) -> p h k", k=width),
                                    axis=AX, op=ALU.add).then_inc(sum_done[kind].sem, 1)

        def dve_reciprocal(dve, n, i):
            kind, k, b, par = unit_at(n, i)
            if not exists(b):
                return
            heads = H if kind == "a" else HH
            dve.wait_ge(sum_done[kind].sem, sum_done[kind].at(b, k))
            wait_for(dve, scaled, unit_before(n, i, 2))
            nc.vector.reciprocal(rden[:, par, 0:heads], den[:, par, 0:heads]).then_inc(rec_done[kind].sem, 1)

        def dve_take(dve, n, job, k, b):
            src = bank_of(n)
            dve.wait_ge(computed[job].sem, computed[job].at(b, k))
            if job == "vx":
                wait(dve, pv_done["x"], b - 1)
                runs = [[0, 1], [2]] if k == 0 else [[3, 4]]
                for run in runs:
                    lo, hi = v_dims(run[0])
                    m, at, skip = len(run), v_column(n, run[0], 0), 32 * G0[run[0]] - lo
                    values = ps_m[:, n % MB, at:at + m * KC * (hi - lo)].rearrange("p (c h j) -> p c h j", c=m, h=KC)
                    last = nc.vector.tensor_tensor(vX[:, run[0]:run[0] + m], values[:, :, :, skip:skip + 64],
                                                   vmask[:, run[0]:run[0] + m, None, :].to_broadcast([P, m, KC, 64]),
                                                   ALU.mult)
                last.then_inc(taken[job].sem, 1)
                return
            if job == "rk":
                nc.vector.tensor_copy(rank[:], src[:, 0:TPB * E].rearrange("p (t e) -> p t e", t=TPB)).then_inc(
                    taken[job].sem, 1)
                return
            which = 1 if job == "oa" else 2
            s = sums(which, k)
            if job == "oa":
                dve.wait_ge(xres_loaded.sem, xres_loaded.at(b))
                add = xres[:, k, :]
            else:
                dve.wait_ge(x1r_made.sem, x1r_made.at(b))
                add = x1r[:, k, :]
            nc.vector.tensor_tensor(s[:], src, add, ALU.add).then_inc(taken[job].sem, 1)

        def dve_stats(dve, which, k, b):
            if not exists(b):
                return
            wait(dve, taken["oa" if which == 1 else "ox"], b, k)
            nc.vector.bn_stats(st[:, 2 * (which - 1) + k, :], sums(which, k)[:]).then_inc(stats_done[which].sem, 1)

        def dve_mean(dve, which, k, b):
            if not exists(b):
                return
            q = 2 * (which - 1) + k
            dve.wait_ge(stats_done[which].sem, stats_done[which].at(b, k))
            wait(dve, eps_added[which], b - 1, k)
            settled(dve)
            nc.vector.bn_aggr(mv[:, q, :], st[:, q, :]).then_inc(mean_done[which].sem, 1)

        def sums(which, k):
            return ((sum1, sum1b), (sum2, sum2b))[which - 1][k]

        def dve_layernorm(dve, which, k, b):
            if not exists(b):
                return
            q = 2 * (which - 1) + k
            dve.wait_ge(rstd_done[which].sem, rstd_done[which].at(b, k))
            if which == 1:
                wait(dve, computed["x1T"], b - 1, 1)
                wait(dve, x1r_made, b - 1)
                dst = x1
            else:
                wait(dve, computed["x2T"], b - 1, k)
                wait(dve, x2_stored[k], b - 1)
                dst = x2s
            nc.vector.tensor_scalar(dst[:, k, :], sums(which, k)[:], mv[:, q, 0:1], rstd[:, q:q + 1],
                                    ALU.subtract, ALU.mult).then_inc(ln_done[which].sem, 1)

        def dve_route(dve, stage, b):
            if not exists(b):
                return
            n = STAGES.index(stage)
            if n == 0:
                dve.wait_ge(taken["rt"].sem, taken["rt"].at(b))
                wait(dve, routed, b - 1)
            else:
                dve.wait_ge(routed.sem, routed.at(b, n - 1))
            rows = rev[:, None, :].to_broadcast([P, TPB, E])
            hot = onehot[:, 0:TPB * E].rearrange("p (t e) -> p t e", t=TPB)
            if stage == "max":
                last = nc.vector.tensor_reduce(lmax[:], logits[:], axis=AX, op=ALU.max)
            elif stage == "less_max":
                wait(dve, gate_exp_done, b - 1)
                last = nc.vector.tensor_tensor(ldif[:], logits[:], lmax[:, :, None].to_broadcast([P, TPB, E]),
                                               ALU.subtract)
            elif stage == "is_max":
                last = nc.vector.tensor_tensor(ismax[:], logits[:], lmax[:, :, None].to_broadcast([P, TPB, E]),
                                               ALU.is_equal)
            elif stage == "weigh":
                last = nc.vector.tensor_tensor(ismax[:], ismax[:], rows, ALU.mult)
            elif stage == "first":
                last = nc.vector.tensor_reduce(best[:], ismax[:], axis=AX, op=ALU.max)
            elif stage == "count":
                last = nc.vector.tensor_tensor(before[:, 0:E], before[:, E:2 * E], onehot[:, E:2 * E], ALU.add)
            elif stage == "onehot":
                last = nc.vector.tensor_tensor(hot, rows, best[:, :, None].to_broadcast([P, TPB, E]), ALU.is_equal)
            elif stage == "count_tile":
                last = nc.vector.tensor_tensor(before[:, E:2 * E], before[:, 0:E], onehot[:, 0:E], ALU.add)
            elif stage == "gate_sum":
                dve.wait_ge(gate_exp_done.sem, gate_exp_done.at(b))
                last = nc.vector.tensor_reduce(lsum[:], lexp[:], axis=AX, op=ALU.add)
            elif stage == "gate":
                for t in range(TPB):
                    wait(dve, entered[t], b - 1)
                last = nc.vector.reciprocal(member[:, :, 1], lsum[:])
            elif stage == "pick":
                dve.wait_ge(taken["rk"].sem, taken["rk"].at(b))
                last = nc.vector.tensor_tensor(rank[:], rank[:], hot, ALU.mult)
            elif stage == "place":
                wait(dve, place_taken, b - 1)
                last = nc.vector.tensor_reduce(place[:], rank[:], axis=AX, op=ALU.add)
            last.then_inc(routed.sem, 1)

        def dve_weights(dve, s):
            if s == 1:
                dve.wait_ge(wT_ready.sem, 1)
                dve.wait_ge(w_loaded.sem, 16 * N_LOADS)
                nc.vector.tensor_tensor(bo_s[:], ps_m[:, 2, 0:D], bo_s[:], ALU.add).then_inc(bo_ready.sem, 1)
                dve.wait_ge(consts_ready.sem, 1)

        def dve_iteration(dve, i):
            stages = iter(STAGES)
            for s in range(6):
                for what, job in step_of(DVE_ORDER[s], s, i, lambda j: j in BY_DVE):
                    if what == "route":
                        dve_route(dve, next(stages), i - 4)
                    elif what == "sum":
                        dve_sum(dve, s - 1, i)
                    elif what == "reciprocal":
                        dve_reciprocal(dve, s - 1, i)
                    elif what == "max":
                        dve_max(dve, s, i)
                    elif what == "less_max":
                        dve_less_max(dve, s, i)
                    elif what[:-2] in ("stats", "mean", "layernorm"):
                        which, k = norm_of(what)
                        do = {"stats": dve_stats, "mean": dve_mean, "layernorm": dve_layernorm}[what[:-2]]
                        do(dve, which, k, norm_batch(which, s, i))
                    else:
                        dve_take(dve, *job)
                if isinstance(i, int) and i == 1:
                    dve_weights(dve, s)

        @block.vector
        def _(dve):
            nc.vector.memset(vA[:].rearrange("p s d -> p (s d)"), 0.0)
            nc.vector.memset(router_s[:, :, E:], 0.0)
            nc.vector.memset(onehot[:], 0.0)
            nc.vector.memset(zeros[:], 0.0)
            nc.vector.memset(batch_step[:], float(S))
            nc.vector.memset(eps[:], EPS)
            nc.vector.memset(neg_half[:], -0.5).then_inc(dve2.sem, 1)

            loop_batches(dve, dve_iteration)

            chain = [1]

            def link(ins):
                chain[0] += 1
                ins.then_inc(dve2.sem, 1)
                dve.wait_ge(dve2.sem, chain[0])

            dve.wait_ge(routed.sem, routed.at(B - 1))
            dve.wait_ge(total_done.sem, 1)
            link(nc.vector.tensor_tensor(n_e[:], ps_s[:, 0, E:2 * E], round_up[:], ALU.add))
            link(nc.vector.tensor_copy(t_i[:], n_e[:]))
            link(nc.vector.tensor_scalar(t_i[:], t_i[:], 7, None, ALU.logical_shift_right))
            link(nc.vector.tensor_copy(t_e[:], t_i[:]))
            link(nc.vector.tensor_tensor_scan(tb_e[:], zeros[:], t_e[:], 0.0, ALU.add, ALU.add))
            link(nc.vector.tensor_scalar(ended[:], tb_e[:], tile_no[:], None, ALU.is_le))
            link(nc.vector.scalar_tensor_tensor(ended_t[:], tb_e[:], tile_no[:], t_e[:], ALU.is_le, ALU.mult))
            link(nc.vector.tensor_reduce(e_f[:], ended[:], axis=AX, op=ALU.add))
            link(nc.vector.tensor_reduce(start_f[:], ended_t[:], axis=AX, op=ALU.add))
            link(nc.vector.tensor_tensor(start_f[:], tile_no[:], start_f[:], ALU.subtract))
            link(nc.vector.scalar_tensor_tensor(start_f[:], e_f[:], float(LIST // P), start_f[:], ALU.mult, ALU.add))
            nc.vector.tensor_scalar(plan_f[:, 1:2], e_f[:], float(E - 1), None, ALU.min).then_inc(plan_made.sem, 1)
            nc.vector.tensor_scalar(plan_f[:, 0:1], start_f[:], float(P), None, ALU.mult).then_inc(plan_made.sem, 1)
            dve.wait_ge(plan_spread.sem, 1)
            plan = ps_s[:, 1, 0:2 * RW].rearrange("p (c j) -> p c j", c=2)
            nc.vector.tensor_copy(plan_i[:], plan[:, :, 0:NTILE]).then_inc(plan_ready.sem, 1)
            dve.wait_ge(plan_ready.sem, 1)
            tail_of_part1(dve)

            def one(j, g, m):
                if not isinstance(j, int) or 3 <= j <= NTILE + 2:
                    q, r = (m - 3) % 2, (m - 3) % XR
                    wait(dve, f["rs3_done"], j - 3)
                    wait_ring(dve, stored, g, m, 3 + XR)
                    nc.vector.tensor_scalar(yo[:, r, :], ys[:, q, :], mv3[:, q, 0:1], rs3[:, q:q + 1],
                                            ALU.subtract, ALU.mult).then_inc(f["ln3_done"].sem, 1)
                if not isinstance(j, int) or 2 <= j <= NTILE + 1:
                    q, r = (m - 2) % 2, (m - 2) % XR
                    wait(dve, f["y_done"], j - 2)
                    wait_ring(dve, b2_loaded, g, m, 2)
                    nc.vector.tensor_tensor(yb[:, q, :], ps_m[:, q, 0:D], b2r[:, r, :], ALU.add).then_inc(
                        f["bias_added"].sem, 1)
                    wait(dve, f["bias_added"], j - 2)
                    gates = (slots[:, j - 2, 1:2] if isinstance(j, int)
                             else slots[:, bass.ds(j - 2, 1), 1:2].rearrange("p a c -> p (a c)"))
                    nc.vector.scalar_tensor_tensor(ys[:, q, :], yb[:, q, :], gates, xg[:, r, :], ALU.mult,
                                                   ALU.add).then_inc(f["res_done"].sem, 1)
                    wait(dve, f["res_done"], j - 2)
                    nc.vector.bn_stats(st3[:, q, :], ys[:, q, :]).then_inc(f["st3_done"].sem, 1)
                    wait(dve, f["st3_done"], j - 2)
                    settled(dve)
                    nc.vector.bn_aggr(mv3[:, q, :], st3[:, q, :]).then_inc(f["mv3_done"].sem, 1)
                if not isinstance(j, int) or j + 1 < NTILE:
                    w1_copy(dve, nc.vector.tensor_copy, 1, "w1_copied_dve", j + 1, m + 1)

            dve.wait_ge(experts_loaded.sem, 32 * E)
            w1_copy(dve, nc.vector.tensor_copy, 1, "w1_copied_dve", 0, 0)
            for_tiles(dve, one, 3)

        def pool_rstd(pool, which, k, b):
            if not exists(b):
                return
            q = 2 * (which - 1) + k
            pool.wait_ge(mean_done[which].sem, mean_done[which].at(b, k))
            wait(pool, ln_done[which], b - 1, k)
            nc.gpsimd.tensor_tensor(ve[:, q:q + 1], mv[:, q, 1:2], eps[:], ALU.add).then_inc(eps_added[which].sem, 1)
            pool.wait_ge(eps_added[which].sem, eps_added[which].at(b, k))
            nc.gpsimd.tensor_tensor(rstd[:, q:q + 1], ve[:, q:q + 1], neg_half[:], ALU.pow).then_inc(
                rstd_done[which].sem, 1)

        def pool_scale(pool, n, i):
            kind, k, b, par = unit_at(n, i)
            if not exists(b):
                return
            heads, width = (H, KEYS) if kind == "a" else (HH, K2)
            pool.wait_ge(rec_done[kind].sem, rec_done[kind].at(b, k))
            p = prob[:, n % 3, 0:heads * width].rearrange("p (h k) -> p h k", k=width)
            nc.gpsimd.tensor_tensor(p, p, rden[:, par, 0:heads, None].to_broadcast([P, heads, width]),
                                    ALU.mult).then_inc(scaled[kind].sem, 1)

        def pool_kxblk(pool, b):
            if not exists(b):
                return
            pool.wait_ge(taken["kx"].sem, taken["kx"].at(b))
            wait(pool, sc_done["x"], b - 1)
            for h in range(KC):
                last = nc.gpsimd.tensor_tensor(kxblk[:, h], kxT[:, h, None, :].to_broadcast([P, HH, K2]),
                                               kmask[:, :, None].to_broadcast([P, HH, K2]), ALU.mult)
            last.then_inc(kxblk_made.sem, 1)

        def pool_x1r(pool, b):
            if not exists(b):
                return
            pool.wait_ge(ln_done[1].sem, ln_done[1].at(b))
            wait(pool, taken["ox"], b - 1)
            nc.gpsimd.tensor_tensor(x1r[:], x1[:], bo_s[:, None, :].to_broadcast([P, TPB, D]),
                                    ALU.add).then_inc(x1r_made.sem, 1)

        def pool_kblk(pool, b):
            if not exists(b):
                return
            pool.wait_ge(taken["k"].sem, taken["k"].at(b))
            wait(pool, sc_done["a"], b - 1)
            for h in range(KC):
                last = nc.gpsimd.tensor_tensor(
                    kblk[:, h], kT[:, h, :, None, :].to_broadcast([P, NSEG, HH, KEYS]),
                    kmask[:, None, :, None].to_broadcast([P, NSEG, HH, KEYS]), ALU.mult)
            last.then_inc(kblk_made.sem, 1)

        def pool_weights(pool, s):
            if s == 5:
                pool.wait_ge(bo_ready.sem, 1)
                pool.wait_ge(lists_filled.sem, lists_filled.at(0))

        def pool_iteration(pool, i):
            for s in range(6):
                for what in POOL_ORDER[s]:
                    if what == "scale":
                        pool_scale(pool, s - 1, i)
                    elif what == "kxblk":
                        pool_kxblk(pool, i - 2)
                    elif what == "x1r":
                        pool_x1r(pool, i - 2)
                    elif what == "kblk":
                        pool_kblk(pool, i)
                    elif what == "enter":
                        pool_enter(pool, i - 4)
                    else:
                        which, k = norm_of(what)
                        pool_rstd(pool, which, k, norm_batch(which, s, i))
                if isinstance(i, int) and i == 1:
                    pool_weights(pool, s)

        def pool_enter(pool, b):
            if not exists(b):
                return
            pool.wait_ge(routed.sem, routed.at(b))
            for t in range(TPB):
                wait(pool, entered[t], b - 1)
            settled(pool)
            nc.gpsimd.tensor_copy(place_i[:], place[:]).then_inc(place_taken.sem, 1)
            nc.gpsimd.tensor_tensor(member[:, :, 0], member[:, :, 0], batch_step[:], ALU.add).then_inc(
                token_stepped.sem, 1)
            for t in range(TPB):
                pool.wait_ge(place_taken.sem, place_taken.at(b))
                pool.wait_ge(token_stepped.sem, token_stepped.at(b))
                settled(pool)
                nc.gpsimd.indirect_dma_start(lists, bass.IndirectOffsetOnAxis(ap=place_i[:, t:t + 1], axis=0),
                                             member[:, t, :], None, bounds_check=LIST_ROWS - 1,
                                             oob_is_err=False).then_inc(entered[t].sem, 16)

        @block.gpsimd
        def _(pool):
            made = [0]

            def link(ins):
                made[0] += 1
                ins.then_inc(consts_made.sem, 1)
                pool.wait_ge(consts_made.sem, made[0])

            g = nc.gpsimd
            link(g.memset(ident[:], 0.0))
            link(g.affine_select(out=ident[:], in_=ident[:], compare_op=ALU.not_equal, fill=1.0, base=0,
                                 pattern=[[-1, P]], channel_multiplier=1))
            pool.sem_inc(ident_made.sem, 1)
            pairs = fill.rearrange("p (r c) -> p r c", c=2)
            link(g.memset(pairs[:, :, 0], float(B * S)))
            g.memset(pairs[:, :, 1], 0.0).then_inc(fill_made.sem, 1)
            link(g.memset(ones[:], 1.0))
            link(g.memset(kmask[:], 1.0))
            link(g.memset(vmask[:].rearrange("p c j -> p (c j)"), 1.0))
            link(g.affine_select(out=kmask[:], in_=kmask[:], compare_op=ALU.is_ge, fill=0.0, base=0,
                                 pattern=[[-DH, HH]], channel_multiplier=1))
            link(g.affine_select(out=kmask[:], in_=kmask[:], compare_op=ALU.is_ge, fill=0.0, base=DH - 1,
                                 pattern=[[DH, HH]], channel_multiplier=-1))
            for c in range(CH):
                v = vmask[:, c, :].rearrange("p (h d) -> p h d", d=DH)
                off = c * P - 2 * G0[c] * K2
                link(g.affine_select(out=v, in_=v, compare_op=ALU.is_ge, fill=0.0, base=off,
                                     pattern=[[-K2, 4], [0, DH]], channel_multiplier=1))
                link(g.affine_select(out=v, in_=v, compare_op=ALU.is_ge, fill=0.0, base=K2 - 1 - off,
                                     pattern=[[K2, 4], [0, DH]], channel_multiplier=-1))
            link(g.memset(tri[:], 1.0))
            link(g.affine_select(out=tri[:], in_=tri[:], compare_op=ALU.is_gt, fill=0.0, base=0, pattern=[[1, P]],
                                 channel_multiplier=-1))
            link(g.iota(rev[:], pattern=[[-1, E]], base=E, channel_multiplier=0, allow_small_or_imprecise_dtypes=True))
            link(g.iota(member[:, :, 0], pattern=[[P, TPB]], base=-S, channel_multiplier=1,
                        allow_small_or_imprecise_dtypes=True))
            link(g.iota(tile_no[:], pattern=[[0, 1]], base=0, channel_multiplier=1,
                        allow_small_or_imprecise_dtypes=True))
            link(g.memset(before[:], 0.0))
            link(g.iota(before[0:1, E:2 * E], pattern=[[LIST, E]], base=0, channel_multiplier=0,
                        allow_small_or_imprecise_dtypes=True))
            link(g.iota(round_up[:], pattern=[[-LIST, E]], base=P - 1, channel_multiplier=0,
                        allow_small_or_imprecise_dtypes=True))
            pool.wait_ge(dve2.sem, 1)
            g.memset(ve[:], 0.0).then_inc(consts_ready.sem, 1)

            loop_batches(pool, pool_iteration)

            tail_of_part1(pool)
            nc.gpsimd.memset(xg[:].rearrange("p m d -> p (m d)"), 0.0).then_inc(rows_cleared.sem, 1)
            pool.wait_ge(rows_cleared.sem, 1)
            pool.wait_ge(plan_ready.sem, 1)
            for t in range(TPB):
                pool.wait_ge(x2_stored[t].sem, 16 * B)

            def token(j):
                return slots[:, j, 0:1] if isinstance(j, int) else slots[:, bass.ds(j, 1), 0:1].rearrange("p a c -> p (a c)")

            def gather(j, g, m):
                wait(pool, f["res_done"], j - XR)
                wait(pool, f["xgT_done"], j - XR)
                wait_ring(pool, gathered, g, m, XR)
                wait_ring(pool, slots_loaded, g, m)
                settled(pool)
                nc.gpsimd.tensor_copy(idx_g[:, m:m + 1], token(j)).then_inc(f["idx_g_made"].sem, 1)
                pool.wait_ge(f["idx_g_made"].sem, f["idx_g_made"].at(j))
                settled(pool)
                nc.gpsimd.indirect_dma_start(xg[:, m, :], None, x2_dram,
                                             bass.IndirectOffsetOnAxis(ap=idx_g[:, m:m + 1], axis=0),
                                             bounds_check=B * S - 1, oob_is_err=False).then_inc(gathered[m].sem, 16)

            def one(j, g, m):
                if not isinstance(j, int) or j + ROWS_AHEAD < NTILE:
                    gather(j + ROWS_AHEAD, g + (m + ROWS_AHEAD) // XR, (m + ROWS_AHEAD) % XR)
                if not isinstance(j, int) or j >= 4:
                    r = (m - 4) % XR
                    wait_ring(pool, stored, g, m, 4 + XR)
                    settled(pool)
                    nc.gpsimd.tensor_copy(idx_s[:, r:r + 1], token(j - 4)).then_inc(f["idx_s_made"].sem, 1)
                    wait(pool, f["ln3_done"], j - 4)
                    wait(pool, f["idx_s_made"], j - 4)
                    settled(pool)
                    nc.gpsimd.indirect_dma_start(out_rows, bass.IndirectOffsetOnAxis(ap=idx_s[:, r:r + 1], axis=0),
                                                 yo[:, r, :], None, bounds_check=B * S - 1,
                                                 oob_is_err=False).then_inc(stored[r].sem, 16)
                if not isinstance(j, int) or 2 <= j <= NTILE + 1:
                    q = (m - 2) % 2
                    wait(pool, f["mv3_done"], j - 2)
                    wait(pool, f["ln3_done"], j - 4)
                    nc.gpsimd.tensor_tensor(ve3[:, q:q + 1], mv3[:, q, 1:2], eps[:], ALU.add).then_inc(f["ve3_done"].sem, 1)
                    wait(pool, f["ve3_done"], j - 2)
                    nc.gpsimd.tensor_tensor(rs3[:, q:q + 1], ve3[:, q:q + 1], neg_half[:], ALU.pow).then_inc(
                        f["rs3_done"].sem, 1)

            for j in range(ROWS_AHEAD):
                gather(j, 0, j)
            for_tiles(pool, one, 4)
            for j in range(NTILE - XR, NTILE):
                wait_ring(pool, stored, j // XR, j % XR)



_INS = ["x", "ctx_1024", "L0_attn_W_qkv", "L0_attn_W_out", "L0_xattn_Wq", "L0_xattn_bq", "L0_xattn_Wk",
        "L0_xattn_bk", "L0_xattn_Wv", "L0_xattn_bv", "L0_xattn_Wo", "L0_xattn_bo", "L0_ffn_router_w", "L0_ffn_w1",
        "L0_ffn_b1", "L0_ffn_w2", "L0_ffn_b2"]


def kernel(**inputs):
    import concourse.bacc as bacc
    from concourse.bass_utils import run_bass_kernel_spmd

    nc = bacc.Bacc("TRN2", target_bir_lowering=False, num_devices=1)
    arrays, args = {}, []
    for name in _INS:
        a = np.ascontiguousarray(inputs[name])
        arrays[f"in_{name}"] = a
        args.append(nc.dram_tensor(f"in_{name}", a.shape, mybir.dt.from_np(a.dtype), kind="ExternalInput").ap())
    shape = inputs["x"].shape
    args.append(nc.dram_tensor("out", shape, mybir.dt.float32, kind="ExternalOutput").ap())
    decoder_layer(nc, *args)
    r = run_bass_kernel_spmd(nc, [arrays], core_ids=[0])
    return r.results[0]["out"]
```
